# Optimizing a Trainium2 kernel written in Bass

```python
import numpy as np
import jax
import jax.numpy as jnp

def _softmax(x, axis=-1):
    return jax.nn.softmax(x, axis=axis)

def _gelu(x):
    return jax.nn.gelu(x, approximate=True)

def _silu(x):
    return jax.nn.silu(x)

def _sigmoid(x):
    return jax.nn.sigmoid(x)

def _layernorm(x, axis=-1, eps=1e-05):
    m = jnp.mean(x, axis=axis, keepdims=True)
    v = jnp.var(x, axis=axis, keepdims=True)
    return (x - m) / jnp.sqrt(v + eps)

def _scatter_add(tgt, idx, src, axis=0):
    return tgt.at[idx].add(src)

def _segment_sum(src, seg, n):
    return jax.ops.segment_sum(src, seg, n)
kernel_name = 'mk_flamingo_gated_d2_seqx_r4_8e3410'

def setup_inputs(seed: int=0):
    np.random.seed(seed)
    _w = jnp.asarray

    def _rec_inputs():
        import jax
        import jax.numpy as jnp
        _rk = jax.random.key(seed)
        x = -0.0002928 + 1 * jax.random.normal(jax.random.fold_in(_rk, 1), (16, 100, 256), jnp.float32)
        _lenS = 100 - jax.random.randint(jax.random.fold_in(_rk, 7), (16,), 0, max(1, 100 // 4) + 1, jnp.int32)
        _lenS2 = 361 - jax.random.randint(jax.random.fold_in(_rk, 8), (16,), 0, max(1, 361 // 4) + 1, jnp.int32)
        _ctx_1024P = jax.random.normal(jax.random.fold_in(_rk, 11), (16, 16, 256), jnp.float32)
        _ctx_1024c = jax.random.dirichlet(jax.random.fold_in(_rk, 511), 0.3 * jnp.ones((16,), jnp.float32), (16, 361))
        _ctx_1024t = jnp.einsum('bsk,bkd->bsd', _ctx_1024c, _ctx_1024P)
        _ctx_1024t = _ctx_1024t * jax.lax.rsqrt(jnp.mean(jnp.square(_ctx_1024t)) + 1e-12) * 0.953939
        ctx_1024 = -1.39393e-06 + 0.999914 * (_ctx_1024t + 0.3 * jax.random.normal(jax.random.fold_in(_rk, 611), (16, 361, 256), jnp.float32))
        _g = jax.random.normal(jax.random.fold_in(_rk, 9001), (2, 2), jnp.float32)
        _g = jnp.sign(_g) * jnp.maximum(jnp.abs(_g), 1.0) + (_g == 0) * 1.0
        g_xattn = _g[0]
        g_ffn = _g[1]
        return (x, ctx_1024, g_xattn, g_ffn)
    x, ctx_1024, g_xattn, g_ffn = _rec_inputs()

    def _L0_xattn_setup():
        import jax, jax.numpy as jnp
        import numpy as np
        D_MODEL = 256
        N_HEADS = 16
        HEAD_DIM = D_MODEL // N_HEADS
        D_FF = 1024
        EPS = 1e-05

        def _layer_norm(x, gamma, beta):
            mu = jnp.mean(x, axis=-1, keepdims=True)
            var = jnp.var(x, axis=-1, keepdims=True)
            return (x - mu) * jax.lax.rsqrt(var + EPS) * gamma + beta
        key = jax.random.key(seed)
        ks = jax.random.split(key, 16)
        B, T, S = (2, 512, 512)
        s = 1.0 / np.sqrt(D_MODEL)
        inp = {'tgt': jax.random.normal(ks[0], (B, T, D_MODEL), jnp.float32), 'memory': jax.random.normal(ks[1], (B, S, D_MODEL), jnp.float32), 'wq': jax.random.normal(ks[2], (D_MODEL, D_MODEL), jnp.float32) * s, 'bq': jnp.zeros((D_MODEL,), jnp.float32), 'wk': jax.random.normal(ks[3], (D_MODEL, D_MODEL), jnp.float32) * s, 'bk': jnp.zeros((D_MODEL,), jnp.float32), 'wv': jax.random.normal(ks[4], (D_MODEL, D_MODEL), jnp.float32) * s, 'bv': jnp.zeros((D_MODEL,), jnp.float32), 'wo': jax.random.normal(ks[5], (D_MODEL, D_MODEL), jnp.float32) * s, 'bo': jnp.zeros((D_MODEL,), jnp.float32), 'w1': jax.random.normal(ks[6], (D_MODEL, D_FF), jnp.float32) * s, 'b1': jnp.zeros((D_FF,), jnp.float32), 'w2': jax.random.normal(ks[7], (D_FF, D_MODEL), jnp.float32) * (1.0 / np.sqrt(D_FF)), 'b2': jnp.zeros((D_MODEL,), jnp.float32), 'g1': jnp.ones((D_MODEL,), jnp.float32), 'be1': jnp.zeros((D_MODEL,), jnp.float32), 'g2': jnp.ones((D_MODEL,), jnp.float32), 'be2': jnp.zeros((D_MODEL,), jnp.float32)}
        return inp
    _L0_xattn_all = _L0_xattn_setup()
    _L0_xattn_in = {k: v for k, v in _L0_xattn_all.items() if k in ('wq', 'bq', 'wk', 'bk', 'wv', 'bv', 'wo', 'bo', 'w1', 'b1', 'w2', 'b2', 'g1', 'be1', 'g2', 'be2')}
    del _L0_xattn_all

    def _L0_ffn_setup():
        import jax, jax.numpy as jnp
        import numpy as np
        B, S, H = (2, 256, 256)
        DFF = 512
        E = 8
        TOPK = 2

        def _expert_ffn(x, w1, b1, w2, b2, wg, bg, w3, b3):
            x1 = jnp.einsum('bsh,hf->bsf', x, w1) + b1
            x2 = jnp.einsum('bsh,hf->bsf', x, w2) + b2
            z = x1 * x2
            s = jax.nn.silu(jnp.einsum('bsf,fg->bsg', z, wg) + bg)
            return jnp.einsum('bsg,gh->bsh', s, w3) + b3
        key = jax.random.key(seed)
        ks = jax.random.split(key, 12)
        sc = 0.02
        return {'x': jax.random.normal(ks[0], (B, S, H), jnp.float32), 'gate_w': jax.random.normal(ks[1], (H, E), jnp.float32) * sc, 'gate_b': jnp.zeros((E,), jnp.float32), 'w1': jax.random.normal(ks[2], (E, H, DFF), jnp.float32) * sc, 'b1': jnp.zeros((E, DFF), jnp.float32), 'w2': jax.random.normal(ks[3], (E, H, DFF), jnp.float32) * sc, 'b2': jnp.zeros((E, DFF), jnp.float32), 'wg': jax.random.normal(ks[4], (E, DFF, DFF), jnp.float32) * sc, 'bg': jnp.zeros((E, DFF), jnp.float32), 'w3': jax.random.normal(ks[5], (E, DFF, H), jnp.float32) * sc, 'b3': jnp.zeros((E, H), jnp.float32)}
    _L0_ffn_all = _L0_ffn_setup()
    _L0_ffn_in = {k: v for k, v in _L0_ffn_all.items() if k in ('gate_w', 'gate_b', 'w1', 'b1', 'w2', 'b2', 'wg', 'bg', 'w3', 'b3')}
    del _L0_ffn_all

    def _L1_xattn_setup():
        import jax, jax.numpy as jnp
        import numpy as np
        D_MODEL = 256
        N_HEADS = 16
        HEAD_DIM = D_MODEL // N_HEADS
        B, L = (2, 512)
        key = jax.random.key(seed)
        ks = jax.random.split(key, 11)
        s = 1.0 / np.sqrt(D_MODEL)
        inp = {'query': jax.random.normal(ks[0], (B, L, D_MODEL), dtype=jnp.float32), 'key': jax.random.normal(ks[1], (B, L, D_MODEL), dtype=jnp.float32), 'value': jax.random.normal(ks[2], (B, L, D_MODEL), dtype=jnp.float32), 'Wq_w': jax.random.normal(ks[3], (D_MODEL, D_MODEL), dtype=jnp.float32) * s, 'Wq_b': jnp.zeros((D_MODEL,), dtype=jnp.float32), 'Wk_w': jax.random.normal(ks[4], (D_MODEL, D_MODEL), dtype=jnp.float32) * s, 'Wk_b': jnp.zeros((D_MODEL,), dtype=jnp.float32), 'Wv_w': jax.random.normal(ks[5], (D_MODEL, D_MODEL), dtype=jnp.float32) * s, 'Wv_b': jnp.zeros((D_MODEL,), dtype=jnp.float32), 'Wo_w': jax.random.normal(ks[6], (D_MODEL, D_MODEL), dtype=jnp.float32) * s, 'Wo_b': jnp.zeros((D_MODEL,), dtype=jnp.float32)}
        return inp
    _L1_xattn_all = _L1_xattn_setup()
    _L1_xattn_in = {k: v for k, v in _L1_xattn_all.items() if k in ('Wq_w', 'Wq_b', 'Wk_w', 'Wk_b', 'Wv_w', 'Wv_b', 'Wo_w', 'Wo_b')}
    del _L1_xattn_all

    def _L1_ffn_setup():
        import jax, jax.numpy as jnp
        import numpy as np
        H = 256
        I = 256
        E = 16
        K = 4
        LIMIT = 7.0
        ALPHA = 1.702
        EPS = 1e-05
        key = jax.random.key(seed)
        ks = jax.random.split(key, 8)
        x = jax.random.normal(ks[0], (2, 128, H), dtype=jnp.float32)
        norm_scale = jnp.ones((H,), dtype=jnp.float32)
        wg = jax.random.normal(ks[1], (H, E), dtype=jnp.float32) * 0.02
        bg = jax.random.normal(ks[2], (E,), dtype=jnp.float32) * 0.02
        w1 = jax.random.normal(ks[3], (E, H, 2 * I), dtype=jnp.float32) * 0.02
        b1 = jax.random.normal(ks[4], (E, 2 * I), dtype=jnp.float32) * 0.02
        w2 = jax.random.normal(ks[5], (E, I, H), dtype=jnp.float32) * 0.02
        b2 = jax.random.normal(ks[6], (E, H), dtype=jnp.float32) * 0.02
        return {'x': x, 'norm_scale': norm_scale, 'wg': wg, 'bg': bg, 'w1': w1, 'b1': b1, 'w2': w2, 'b2': b2}
    _L1_ffn_all = _L1_ffn_setup()
    _L1_ffn_in = {k: v for k, v in _L1_ffn_all.items() if k in ('norm_scale', 'wg', 'bg', 'w1', 'b1', 'w2', 'b2')}
    del _L1_ffn_all
    return {'x': x, 'ctx_1024': ctx_1024, 'g_xattn': g_xattn, 'g_ffn': g_ffn, 'L0_xattn_wq': _L0_xattn_in['wq'], 'L0_xattn_bq': _L0_xattn_in['bq'], 'L0_xattn_wk': _L0_xattn_in['wk'], 'L0_xattn_bk': _L0_xattn_in['bk'], 'L0_xattn_wv': _L0_xattn_in['wv'], 'L0_xattn_bv': _L0_xattn_in['bv'], 'L0_xattn_wo': _L0_xattn_in['wo'], 'L0_xattn_bo': _L0_xattn_in['bo'], 'L0_xattn_w1': _L0_xattn_in['w1'], 'L0_xattn_b1': _L0_xattn_in['b1'], 'L0_xattn_w2': _L0_xattn_in['w2'], 'L0_xattn_b2': _L0_xattn_in['b2'], 'L0_xattn_g1': _L0_xattn_in['g1'], 'L0_xattn_be1': _L0_xattn_in['be1'], 'L0_xattn_g2': _L0_xattn_in['g2'], 'L0_xattn_be2': _L0_xattn_in['be2'], 'L0_ffn_gate_w': _L0_ffn_in['gate_w'], 'L0_ffn_gate_b': _L0_ffn_in['gate_b'], 'L0_ffn_w1': _L0_ffn_in['w1'], 'L0_ffn_b1': _L0_ffn_in['b1'], 'L0_ffn_w2': _L0_ffn_in['w2'], 'L0_ffn_b2': _L0_ffn_in['b2'], 'L0_ffn_wg': _L0_ffn_in['wg'], 'L0_ffn_bg': _L0_ffn_in['bg'], 'L0_ffn_w3': _L0_ffn_in['w3'], 'L0_ffn_b3': _L0_ffn_in['b3'], 'L1_xattn_Wq_w': _L1_xattn_in['Wq_w'], 'L1_xattn_Wq_b': _L1_xattn_in['Wq_b'], 'L1_xattn_Wk_w': _L1_xattn_in['Wk_w'], 'L1_xattn_Wk_b': _L1_xattn_in['Wk_b'], 'L1_xattn_Wv_w': _L1_xattn_in['Wv_w'], 'L1_xattn_Wv_b': _L1_xattn_in['Wv_b'], 'L1_xattn_Wo_w': _L1_xattn_in['Wo_w'], 'L1_xattn_Wo_b': _L1_xattn_in['Wo_b'], 'L1_ffn_norm_scale': _L1_ffn_in['norm_scale'], 'L1_ffn_wg': _L1_ffn_in['wg'], 'L1_ffn_bg': _L1_ffn_in['bg'], 'L1_ffn_w1': _L1_ffn_in['w1'], 'L1_ffn_b1': _L1_ffn_in['b1'], 'L1_ffn_w2': _L1_ffn_in['w2'], 'L1_ffn_b2': _L1_ffn_in['b2']}

def reference(x, ctx_1024, g_xattn, g_ffn, L0_xattn_wq, L0_xattn_bq, L0_xattn_wk, L0_xattn_bk, L0_xattn_wv, L0_xattn_bv, L0_xattn_wo, L0_xattn_bo, L0_xattn_w1, L0_xattn_b1, L0_xattn_w2, L0_xattn_b2, L0_xattn_g1, L0_xattn_be1, L0_xattn_g2, L0_xattn_be2, L0_ffn_gate_w, L0_ffn_gate_b, L0_ffn_w1, L0_ffn_b1, L0_ffn_w2, L0_ffn_b2, L0_ffn_wg, L0_ffn_bg, L0_ffn_w3, L0_ffn_b3, L1_xattn_Wq_w, L1_xattn_Wq_b, L1_xattn_Wk_w, L1_xattn_Wk_b, L1_xattn_Wv_w, L1_xattn_Wv_b, L1_xattn_Wo_w, L1_xattn_Wo_b, L1_ffn_norm_scale, L1_ffn_wg, L1_ffn_bg, L1_ffn_w1, L1_ffn_b1, L1_ffn_w2, L1_ffn_b2):
    import jax
    import jax.numpy as jnp

    def _L0_xattn_ref(tgt, memory, wq, bq, wk, bk, wv, bv, wo, bo, w1, b1, w2, b2, g1, be1, g2, be2):
        import jax, jax.numpy as jnp
        import numpy as np
        D_MODEL = 256
        N_HEADS = 16
        HEAD_DIM = D_MODEL // N_HEADS
        D_FF = 1024
        EPS = 1e-05

        def _layer_norm(x, gamma, beta):
            mu = jnp.mean(x, axis=-1, keepdims=True)
            var = jnp.var(x, axis=-1, keepdims=True)
            return (x - mu) * jax.lax.rsqrt(var + EPS) * gamma + beta
        B, T, _ = tgt.shape
        S = memory.shape[1]
        scale = HEAD_DIM ** (-0.5)
        Q = (tgt @ wq + bq).reshape(B, T, N_HEADS, HEAD_DIM).transpose(0, 2, 1, 3)
        K = (memory @ wk + bk).reshape(B, S, N_HEADS, HEAD_DIM).transpose(0, 2, 1, 3)
        V = (memory @ wv + bv).reshape(B, S, N_HEADS, HEAD_DIM).transpose(0, 2, 1, 3)
        scores = jnp.einsum('bhtd,bhsd->bhts', Q, K) * scale
        attn = jax.nn.softmax(scores, axis=-1)
        ctx = jnp.einsum('bhts,bhsd->bhtd', attn, V)
        ctx = ctx.transpose(0, 2, 1, 3).reshape(B, T, D_MODEL)
        attn_out = ctx @ wo + bo
        x = _layer_norm(tgt + attn_out, g1, be1)
        ff = jax.nn.relu(x @ w1 + b1) @ w2 + b2
        out = _layer_norm(x + ff, g2, be2)
        return out

    def _L0_ffn_ref(x, gate_w, gate_b, w1, b1, w2, b2, wg, bg, w3, b3):
        import jax, jax.numpy as jnp
        import numpy as np
        B, S, H = (2, 256, 256)
        DFF = 512
        E = 8
        TOPK = 2

        def _expert_ffn(x, w1, b1, w2, b2, wg, bg, w3, b3):
            x1 = jnp.einsum('bsh,hf->bsf', x, w1) + b1
            x2 = jnp.einsum('bsh,hf->bsf', x, w2) + b2
            z = x1 * x2
            s = jax.nn.silu(jnp.einsum('bsf,fg->bsg', z, wg) + bg)
            return jnp.einsum('bsg,gh->bsh', s, w3) + b3
        logits = jnp.einsum('bsh,he->bse', x, gate_w) + gate_b
        topv, topi = jax.lax.top_k(logits, TOPK)
        probs = jax.nn.softmax(topv, axis=-1)
        out = jnp.zeros_like(x)
        for e in range(E):
            we = jnp.sum(probs * (topi == e), axis=-1)
            y = _expert_ffn(x, w1[e], b1[e], w2[e], b2[e], wg[e], bg[e], w3[e], b3[e])
            out = out + we[..., None] * y
        return out

    def _L1_xattn_ref(query, key, value, Wq_w, Wq_b, Wk_w, Wk_b, Wv_w, Wv_b, Wo_w, Wo_b):
        import jax, jax.numpy as jnp
        import numpy as np
        D_MODEL = 256
        N_HEADS = 16
        HEAD_DIM = D_MODEL // N_HEADS
        B, L = (2, 512)
        b = query.shape[0]
        Q = query @ Wq_w.T + Wq_b
        K = key @ Wk_w.T + Wk_b
        V = value @ Wv_w.T + Wv_b

        def split_heads(x):
            return x.reshape(b, -1, N_HEADS, HEAD_DIM).transpose(0, 2, 1, 3)
        Qh, Kh, Vh = (split_heads(Q), split_heads(K), split_heads(V))
        scale = 1.0 / jnp.sqrt(jnp.float32(HEAD_DIM))
        energy = jnp.einsum('bhqd,bhkd->bhqk', Qh, Kh) * scale
        attn = jax.nn.softmax(energy, axis=1)
        out = jnp.einsum('bhqk,bhkd->bhqd', attn, Vh)
        out = out.transpose(0, 2, 1, 3).reshape(b, -1, D_MODEL)
        return out @ Wo_w.T + Wo_b

    def _L1_ffn_ref(x, norm_scale, wg, bg, w1, b1, w2, b2):
        import jax, jax.numpy as jnp
        import numpy as np
        H = 256
        I = 256
        E = 16
        K = 4
        LIMIT = 7.0
        ALPHA = 1.702
        EPS = 1e-05
        shape = x.shape
        xf = x.reshape(-1, shape[-1])
        xn = xf * jax.lax.rsqrt(jnp.mean(xf * xf, axis=-1, keepdims=True) + EPS) * norm_scale
        logits = xn @ wg + bg
        vals, idx = jax.lax.top_k(logits, K)
        gates = jax.nn.softmax(vals, axis=-1)
        gate_full = jnp.einsum('tke,tk->te', jax.nn.one_hot(idx, E, dtype=gates.dtype), gates)
        h = jnp.einsum('th,ehd->etd', xn, w1) + b1[:, None, :]
        a = jnp.minimum(h[..., ::2], LIMIT)
        b = jnp.clip(h[..., 1::2], -LIMIT, LIMIT)
        s = a * jax.nn.sigmoid(ALPHA * a) * (b + 1.0)
        y = jnp.einsum('eti,eih->eth', s, w2) + b2[:, None, :]
        t = jnp.einsum('eth,te->th', y, gate_full)
        return x + t.reshape(shape)
    x = x + jnp.tanh(g_xattn[0]) * _L0_xattn_ref(_layernorm(x, axis=-1), ctx_1024, L0_xattn_wq, L0_xattn_bq, L0_xattn_wk, L0_xattn_bk, L0_xattn_wv, L0_xattn_bv, L0_xattn_wo, L0_xattn_bo, L0_xattn_w1, L0_xattn_b1, L0_xattn_w2, L0_xattn_b2, L0_xattn_g1, L0_xattn_be1, L0_xattn_g2, L0_xattn_be2)
    x = x + jnp.tanh(g_ffn[0]) * _L0_ffn_ref(_layernorm(x, axis=-1), L0_ffn_gate_w, L0_ffn_gate_b, L0_ffn_w1, L0_ffn_b1, L0_ffn_w2, L0_ffn_b2, L0_ffn_wg, L0_ffn_bg, L0_ffn_w3, L0_ffn_b3)
    x = x + jnp.tanh(g_xattn[1]) * _L1_xattn_ref(_layernorm(x, axis=-1), ctx_1024, ctx_1024, L1_xattn_Wq_w, L1_xattn_Wq_b, L1_xattn_Wk_w, L1_xattn_Wk_b, L1_xattn_Wv_w, L1_xattn_Wv_b, L1_xattn_Wo_w, L1_xattn_Wo_b)
    x = x + jnp.tanh(g_ffn[1]) * _L1_ffn_ref(_layernorm(x, axis=-1), L1_ffn_norm_scale, L1_ffn_wg, L1_ffn_bg, L1_ffn_w1, L1_ffn_b1, L1_ffn_w2, L1_ffn_b2)
    return x

_drawn_inputs = setup_inputs


def setup_inputs(seed=0):
    import zlib

    import numpy as np

    out = dict(_drawn_inputs(seed))
    spreads = {'g_ffn': (-1.0, 0.6),
     'L0_xattn_bq': (0.0, 0.8),
     'L0_xattn_bk': (0.0, 2.0),
     'L0_xattn_bv': (0.0, 0.322),
     'L0_xattn_bo': (0.0, 0.329),
     'L0_xattn_b1': (0.0, 0.509),
     'L0_xattn_b2': (0.0, 0.385),
     'L0_xattn_g1': (1.0, 0.2),
     'L0_xattn_be1': (0.0, 0.337),
     'L0_xattn_g2': (1.0, 0.2),
     'L0_xattn_be2': (0.0, 0.274),
     'L0_ffn_gate_b': (0.0, 0.671),
     'L0_ffn_b1': (0.0, 0.8),
     'L0_ffn_b2': (0.0, 0.8),
     'L0_ffn_bg': (0.0, 0.8),
     'L0_ffn_b3': (0.0, 2.0),
     'L1_xattn_Wq_b': (0.0, 0.34),
     'L1_xattn_Wk_b': (0.0, 0.1),
     'L1_xattn_Wv_b': (0.0, 0.1),
     'L1_xattn_Wo_b': (0.0, 2.0),
     'L1_ffn_norm_scale': (1.0, 0.6)}
    factors = {'L0_ffn_gate_w': 3.356,
     'L0_ffn_w1': 8.0,
     'L0_ffn_w2': 8.0,
     'L0_ffn_wg': 8.0,
     'L0_ffn_w3': 8.0,
     'L1_ffn_wg': 8.0,
     'L1_ffn_bg': 8.0,
     'L1_ffn_w1': 8.0,
     'L1_ffn_b1': 8.0,
     'L1_ffn_w2': 8.0,
     'L1_ffn_b2': 175.885}
    for name, (base, spread) in spreads.items():
        noise = np.random.default_rng([zlib.crc32(name.encode()), seed]).standard_normal(out[name].shape)
        drawn = base * np.exp(spread * noise) if base else spread * noise
        out[name] = jnp.asarray(drawn.astype(out[name].dtype))
    for name, factor in factors.items():
        out[name] = (out[name] * factor).astype(out[name].dtype)
    return out
```

```python
from contextlib import ExitStack

import concourse.bass as bass
from concourse import mybir

ALU = mybir.AluOpType
ACT = mybir.ActivationFunctionType
F32 = mybir.dt.float32
BF16 = mybir.dt.bfloat16
I32 = mybir.dt.int32
U32 = mybir.dt.uint32
AX = mybir.AxisListType

P = 128
NT, TQ, D = 16, 100, 256
NK = 361
KCH = [(0, 121), (121, 121), (242, 119)]
KMAX = 121
H, HD = 16, 16
KD = D // P
DFF = 1024
FD = DFF // P
QUAD = 4
NQ = NT // QUAD
N4 = QUAD * TQ
NTOK = NT * TQ
PADK = 3 * KMAX
EPS = 1e-5

E0, TOP0, F0 = 8, 2, 512
E1, TOP1, F1 = 16, 4, 256
NB0 = (NTOK * TOP0 + E0 * (P - 1)) // P
NB1 = (NTOK * TOP1 + E1 * (P - 1)) // P
W0 = 2 * (KD * F0) + 4 * F0 + 4 * D
W1 = KD * 2 * F1 + 2 * D
CNT = NTOK // P + 1

C_ID, C_TRI, C_ONE, C_MASK, C_PE, C_HALF = 0, 128, 256, 384, 392, 393
C_THR, C_IOTA, C_REV0, C_REV1 = 394, 394 + CNT, 394 + CNT + 72, 394 + CNT + 80
C_N = C_REV1 + 16

A_U, A_KT, A_CT, A_UT = 36864, 35478, 34034, 30720
A_KT, A_CT = 36864 - 1444, 36864 - 2888
A_QT, A_QB, A_VP, A_W4, A_BC = 27520, 24320, 21248, 19200, 17408
A_P, A_PT = 17408 - 1452, 17408 - 1452 - 1200
A_W1 = A_PT - 4096
A_E = 17408 - 4800
A_XN = E1 * W1
A_NS = A_XN + NT * D
PRE0 = A_W1 // W0
PRE1 = A_E // W1


class Chain:

    def __init__(self, eng, sem):
        self.eng, self.sem, self.base, self.n = eng, sem, 0, 0

    def begin(self, base):
        self.base, self.n = base, 0

    def __call__(self, ins):
        self.n += 1
        ins.then_inc(self.sem, 1)
        self.eng.wait_ge(self.sem, self.base + self.n)


def build(nc, a, out):
    with ExitStack() as ctx:
        def sb(name, shape, dt=F32):
            return ctx.enter_context(nc.sbuf_tensor(name, shape, dt))

        sems = {}

        def sem(name):
            if name not in sems:
                sems[name] = ctx.enter_context(nc.semaphore(name))
            return sems[name]

        PS = ctx.enter_context(nc.psum_tensor("PS", [P, 8, 512], F32))
        AR = sb("arena", [P, E0 * W0])
        X = sb("X", [P, NT, D])
        CST = sb("consts", [P, C_N])
        COLS = sb("bias_cols", [P, 16])
        TG = sb("tanh_gates", [P, 4])
        BR0 = sb("bias_rows0", [P, 3 * F0 + D], BF16)
        BR1 = sb("bias_rows1", [P, 2 * F1 + D], BF16)
        WORK = sb("work", [P, 4096])
        ZERO = sb("zero", [P, D])
        ST6 = sb("bn_stats", [P, NT, 6])
        MV = sb("mean_var", [P, NT, 2])
        RS = sb("rstd", [P, NT])
        NMX = sb("neg_max", [P, H])
        SUM = sb("exp_sum", [P, 2, 2])
        RCP = sb("exp_rcp", [P, 2, 2])
        TMP = sb("tmp_row", [P, 2, D])
        AT = sb("attn_t", [P, 2, KD * TQ])
        MXH = sb("head_max", [P, TQ])
        SMH = sb("head_sum", [P, 3, TQ])
        GW = sb("gate_w", [P, KD, 16 + 8])
        GB = sb("gate_b", [P, 16 + 8])
        GATE = sb("gates", [P, 4, NT])
        SLOT = sb("slots", [P, 4, NT], U32)
        EBI = sb("block_expert", [P, NB1], I32)
        OHB = sb("block_onehot", [P, NB1], BF16)
        OHX = sb("onehot_rows", [P, 2, P], BF16)

        XS = [nc.dram_tensor("pairs_x0", (NB0 * P, D), F32, kind="Internal").ap(),
              nc.dram_tensor("pairs_x1", (NB1 * P, D), F32, kind="Internal").ap()]
        YS = [nc.dram_tensor("pairs_y0", (NB0 * P, D), F32, kind="Internal").ap(),
              nc.dram_tensor("pairs_y1", (NB1 * P, D), F32, kind="Internal").ap()]

        IDN = CST[:, C_ID:C_ID + P]

        def ar(off, *shape):
            n = 1
            for s in shape:
                n *= s
            v = AR[:, off:off + n]
            if len(shape) == 2:
                v = v.rearrange("p (a b) -> p a b", b=shape[1])
            elif len(shape) == 3:
                v = v.rearrange("p (a b c) -> p a b c", b=shape[1], c=shape[2])
            elif len(shape) == 4:
                v = v.rearrange("p (a b c d) -> p a b c d", b=shape[1], c=shape[2], d=shape[3])
            return v

        U = ar(A_U, NT, D)
        UT = ar(A_UT, KD, NTOK)
        QT = ar(A_QT, KD, NTOK)
        CT = [ar(A_CT + 722 * i, KD, NK) for i in range(2)]
        KT = [ar(A_KT + 722 * i, KD, NK) for i in range(2)]
        VP = [ar(A_VP + 1536 * i, 3, 2, D) for i in range(2)]
        QB = [ar(A_QB + 1600 * i, KD, 8, TQ) for i in range(2)]
        PB = [ar(A_P + 726 * i, 2, PADK) for i in range(2)]
        PT = [ar(A_PT + 600 * i, 2, 3 * TQ) for i in range(2)]
        HT = ar(A_QT - 0, FD, N4)
        WQ, WK, WV, WO = [ar(A_W4 + 512 * i, KD, D) for i in range(4)]
        W1S, W2S = ar(A_W1, KD, DFF), ar(A_W1 + 2048, FD, D)
        BC = [ar(A_BC + D * i, D) for i in range(7)]
        EH = [ar(A_E + 1600 * i, QUAD, QUAD * TQ) for i in range(3)]
        XN = ar(A_XN, NT, D)
        NSC = ar(A_NS, D)
        ATV = [AT[:, i, :].rearrange("p (k t) -> p k t", k=KD) for i in range(2)]

        def wk(off, n):
            return WORK[:, off:off + n]

        block = ctx.enter_context(nc.Block())

        @block.sync
        def _(sp):
            def load(dst, src, name):
                sp.dma_start(dst, src).then_inc(sem(name), 16)

            def wload(dst, src, name, k):
                load(dst, src.rearrange("(k p) n -> p k n", k=k), name)

            def expert0(e, name):
                o = e * W0
                wload(ar(o, KD, F0), a["L0_ffn_w1"][e], name, KD)
                wload(ar(o + 1024, KD, F0), a["L0_ffn_w2"][e], name, KD)
                wload(ar(o + 2048, 4, F0), a["L0_ffn_wg"][e], name, 4)
                wload(ar(o + 4096, 4, D), a["L0_ffn_w3"][e], name, 4)

            def expert1(e, name):
                o = e * W1
                wload(ar(o, KD, 2 * F1), a["L1_ffn_w1"][e], name, KD)
                wload(ar(o + 1024, 2, D), a["L1_ffn_w2"][e], name, 2)

            def ctx_tile(b, par, s):
                load(CT[par], a["ctx_t"][b].rearrange("(k p) s -> p k s", k=KD), s)

            load(X[0:TQ], a["x"].rearrange("b p d -> p b d"), "in_x")
            load(CST[:], a["consts"], "in_const")
            load(COLS[:], a["cols"], "in_cols")
            load(TG[:], a["gates"].partition_broadcast(P), "in_gates")
            for i, n in enumerate(["wq", "wk", "wv", "wo"]):
                wload([WQ, WK, WV, WO][i], a["L0_xattn_" + n], "in_w4", KD)
            ctx_tile(0, 0, "in_ct0")
            ctx_tile(1, 1, "in_ct1")
            for i, n in enumerate(["bv", "bo", "g1", "be1", "b2", "g2", "be2"]):
                load(BC[i], a["L0_xattn_" + n].partition_broadcast(P), "in_bc")
            wload(W1S, a["L0_xattn_w1"], "in_ffw", KD)
            wload(W2S, a["L0_xattn_w2"], "in_ffw", FD)
            wload(GW[:, :, 0:E0], a["L0_ffn_gate_w"], "in_gw", KD)
            wload(GW[:, :, E0:E0 + E1], a["L1_ffn_wg"], "in_gw", KD)
            load(GB[:, 0:E0], a["L0_ffn_gate_b"].partition_broadcast(P), "in_gw")
            load(GB[:, E0:E0 + E1], a["L1_ffn_bg"].partition_broadcast(P), "in_gw")
            sp.wait_ge(sem("bias_zeroed"), 1)
            for q in range(3):
                for i, n in enumerate(["b1", "b2", "bg"]):
                    load(WORK[32 * q:32 * q + E0, i * F0:(i + 1) * F0], a["L0_ffn_" + n], "in_br")
                load(WORK[32 * q:32 * q + E0, 3 * F0:3 * F0 + D], a["L0_ffn_b3"], "in_br")
                load(WORK[32 * q:32 * q + E1, 2048:2048 + 2 * F1], a["L1_ffn_b1"], "in_br")
                load(WORK[32 * q:32 * q + E1, 2048 + 2 * F1:2048 + 2 * F1 + D], a["L1_ffn_b2"], "in_br")
            for e in range(PRE0):
                expert0(e, "in_e0")
            sp.wait_ge(sem("zero_set"), 1)
            for l, nb in ((0, NB0), (1, NB1)):
                load(XS[l].rearrange("(i p) d -> p i d", p=P),
                     ZERO[:].rearrange("p (a d) -> p a d", a=1).to_broadcast([P, nb, D]), f"xs_zeroed{l}")

            def attn_ctx(l):
                with sp.Fori(0, (NT - 2) // 2) as r:
                    for h in range(2):
                        sp.wait_ge(sem(f"v_done{l}"), 6 * r + 3 * (h + 1))
                        ctx_tile(2 * r + h + 2, h, f"in_ct{h}" + ("" if l == 0 else "b"))

            attn_ctx(0)

            sp.wait_ge(sem("ff_added"), NT)
            expert0(PRE0, "in_e0")
            sp.wait_ge(sem("ln_out"), 3 * NQ)
            for e in range(PRE0 + 1, E0 - 2):
                expert0(e, "in_e0")
            sp.wait_ge(sem("logit_done0"), 1)
            expert0(E0 - 2, "in_e0")
            sp.wait_ge(sem("scattered0"), 16 * TOP0 * NT)
            expert0(E0 - 1, "in_e0")

            def block_io(l, nb):
                xin, yb = wk(0, 512), wk(3584, 512)

                def rows(t, i):
                    return t[bass.ds(i * P, P), :]

                for i in range(2):
                    load(xin[:, i * D:(i + 1) * D], rows(XS[l], i), f"in_blk{l}_{i}")
                pairs = (nb - 2) // 2

                def step(i, par, fetch):
                    if fetch:
                        sp.wait_ge(sem(f"xt_done{l}"), i + 1)
                        load(xin[:, par * D:(par + 1) * D], rows(XS[l], i + 2), f"in_blk{l}_{par}")
                    sp.wait_ge(sem(f"y_ready{l}"), i + 1)
                    load(rows(YS[l], i), yb[:, par * D:(par + 1) * D], f"y_out{l}_{par}")

                with sp.Fori(0, pairs) as r:
                    for par in range(2):
                        step(2 * r + par, par, True)
                for i in range(2 * pairs, nb):
                    step(i, i % 2, i + 2 < nb)

            sp.wait_ge(sem("scattered0"), 16 * TOP0 * NT)
            block_io(0, NB0)

            for i, n in enumerate(["Wq_w", "Wk_w", "Wv_w", "Wo_w"]):
                wload([WQ, WK, WV, WO][i], a["L1_xattn_" + n], "in_w4b", KD)
            load(BC[0], a["L1_xattn_Wv_b"].partition_broadcast(P), "in_w4b")
            load(BC[1], a["L1_xattn_Wo_b"].partition_broadcast(P), "in_w4b")
            ctx_tile(0, 0, "in_ct0b")
            ctx_tile(1, 1, "in_ct1b")
            for e in range(PRE1):
                expert1(e, "in_e1")
            attn_ctx(1)
            sp.wait_ge(sem("wo_added1"), NT)
            load(NSC, a["L1_ffn_norm_scale"].partition_broadcast(P), "in_nsc")
            for e in range(PRE1, E1):
                expert1(e, "in_e1")
            sp.wait_ge(sem("scattered1"), 16 * TOP1 * NT)
            block_io(1, NB1)

            sp.wait_ge(sem("x_final"), 1)
            load(out.rearrange("b p d -> p b d"), X[0:TQ], "out_done")
            sp.wait_ge(sem("out_done"), 16)

        @block.gpsimd
        def _(pool):
            nc.gpsimd.memset(WORK[0:96, :], 0.0).then_inc(sem("bias_zeroed"), 1)
            nc.gpsimd.memset(ZERO[:], 0.0).then_inc(sem("zero_set"), 1)
            for i in range(2):
                nc.gpsimd.memset(VP[i], 0.0).then_inc(sem("vp_zeroed"), 1)
                nc.gpsimd.memset(PB[i][0:TQ], 0.0).then_inc(sem("pb_zeroed"), 1)
            pool.wait_ge(sem("in_const"), 16)

            def rstd(n, count):
                pool.wait_ge(sem("ln_var"), n)
                nc.gpsimd.tensor_tensor(RS[0:TQ], RS[0:TQ], CST[0:TQ, C_HALF:C_HALF + 1].to_broadcast([TQ, NT]),
                                        ALU.pow).then_inc(sem("ln_rstd"), 1)

            def blockdiag(l):
                pool.wait_ge(sem(f"q_evac{l}"), 2 * NQ)

                def one(b, par, wait):
                    if wait:
                        pool.wait_ge(sem(f"s_done{l}"), (8 if l == 0 else 3) * (b - 1))
                    for c in range(KD):
                        q = QT[:, c, bass.ds(b * TQ, TQ)].rearrange("p (a t) -> p a t", a=1)
                        m = CST[:, C_MASK:C_MASK + 8].unsqueeze(2)
                        nc.gpsimd.tensor_tensor(QB[par][:, c], q.to_broadcast([P, 8, TQ]),
                                                m.to_broadcast([P, 8, TQ]), ALU.mult).then_inc(sem(f"qb_done{l}"), 1)

                one(0, 0, False)
                one(1, 1, False)
                with pool.Fori(0, (NT - 2) // 2) as r:
                    for h in range(2):
                        one(2 * r + h + 2, h, True)

            def scatter(l, top, src):
                pool.wait_ge(sem(f"slots_ready{l}"), 1)
                pool.wait_ge(sem(f"xs_zeroed{l}"), 16)
                for t in range(NT):
                    for k in range(top):
                        nc.gpsimd.indirect_dma_start(
                            out=XS[l], out_offset=bass.IndirectOffsetOnAxis(ap=SLOT[0:TQ, k, t:t + 1], axis=0),
                            in_=src[0:TQ, t, :], in_offset=None).then_inc(sem(f"scattered{l}"), 16)

            def gather(l, top, nb):
                for par in range(2):
                    n = len([i for i in range(nb) if i % 2 == par])
                    pool.wait_ge(sem(f"y_out{l}_{par}"), 16 * n)
                for t in range(NT):
                    for k in range(top):
                        n = t * top + k
                        if n >= 8:
                            pool.wait_ge(sem(f"y_used{l}"), n - 7)
                        nc.gpsimd.indirect_dma_start(
                            out=wk(1024 + (n % 8) * D, D)[0:TQ], out_offset=None, in_=YS[l],
                            in_offset=bass.IndirectOffsetOnAxis(ap=SLOT[0:TQ, k, t:t + 1], axis=0),
                        ).then_inc(sem(f"y_back{l}_{n % 8}"), 16)

            rstd(1, 0)
            blockdiag(0)
            rstd(2, 1)
            rstd(3, 2)
            rstd(4, 3)
            scatter(0, TOP0, U)
            gather(0, TOP0, NB0)
            rstd(5, 4)

            pool.wait_ge(sem("e0_all_done"), 1)
            for i in range(2):
                nc.gpsimd.memset(VP[i], 0.0).then_inc(sem("vp_zeroed"), 1)
            pool.wait_ge(sem("q_evac1"), 2 * NQ)

            def bd(b, par, wait):
                if wait:
                    pool.wait_ge(sem("s_done1"), 3 * (b - 1))
                for c in range(KD):
                    q = QT[:, c, bass.ds(b * TQ, TQ)].rearrange("p (a t) -> p a t", a=1)
                    m = CST[:, C_MASK:C_MASK + 8].unsqueeze(2)
                    nc.gpsimd.tensor_tensor(QB[par][:, c], q.to_broadcast([P, 8, TQ]),
                                            m.to_broadcast([P, 8, TQ]), ALU.mult).then_inc(sem("qb_done1"), 1)

            def head_weights(b, par, wait, more):
                for ch, (k0, kn) in enumerate(KCH):
                    pool.wait_ge(sem("rcp_done1"), 3 * b + ch + 1)
                    e = EH[ch][0:kn].rearrange("p a (h t) -> p (a h) t", h=QUAD)
                    r = SMH[0:kn, ch, :].rearrange("p (a t) -> p a t", a=1)
                    nc.gpsimd.tensor_tensor(e, e, r.to_broadcast([kn, H, TQ]), ALU.mult).then_inc(sem("p_done1"), 1)
                    if ch == 1 and more:
                        bd(b + 2, par, wait)

            bd(0, 0, False)
            bd(1, 1, False)
            with pool.Fori(0, (NT - 2) // 2) as r:
                for h in range(2):
                    head_weights(2 * r + h, h, True, True)
            head_weights(NT - 2, 0, False, False)
            head_weights(NT - 1, 1, False, False)
            rstd(6, 5)
            rstd(7, 6)
            scatter(1, TOP1, XN)
            gather(1, TOP1, NB1)

        @block.scalar
        def _(act):
            act.wait_ge(sem("in_gates"), 16)
            nc.scalar.activation(TG[:], TG[:], ACT.Tanh).then_inc(sem("tg_ready"), 1)
            act.wait_ge(sem("in_cols"), 16)

            def transposes(n):
                for g in range(NQ):
                    for c in range(KD):
                        i = KD * g + c
                        act.wait_ge(sem("tr_done"), 2 * NQ * n + i + 1)
                        nc.scalar.activation(UT[:, c, g * N4:(g + 1) * N4], PS[:, i % 4, 0:N4],
                                             ACT.Identity).then_inc(sem("tr_evac"), 1)

            def k_evac(l, b, par, m):
                act.wait_ge(sem(f"k_done{l}"), 2 * b + m + 1)
                nc.scalar.activation(KT[par][:, m, :], PS[:, 7 if l == 0 else 6 + m, 0:NK], ACT.Identity,
                                     bias=COLS[:, (2 if l == 0 else 14) + m:(3 if l == 0 else 15) + m]
                                     ).then_inc(sem(f"k_evac{l}"), 1)

            def o_evac(l, b, par):
                per = 8 if l == 0 else 3
                act.wait_ge(sem(f"pv_done{l}"), per * (b + 1))
                src = PS[:, 6, 0:KD * TQ] if l == 0 else PS[:, 4:6, 0:TQ]
                dst = AT[:, par, :] if l == 0 else ATV[par]
                nc.scalar.activation(dst, src, ACT.Identity).then_inc(sem(f"o_evac{l}"), 1)

            transposes(0)

            def pt_evac(b, g):
                n = 8 * b + g
                act.wait_ge(sem("t_done"), n + 1)
                return n

            def attn0(b, par, first, last):
                for g in range(8):
                    if g > 0 or not first:
                        pb, pg = (b, g - 1) if g else (b - 1, 7)
                        n = 8 * pb + pg
                        act.wait_ge(sem("t_done"), n + 1)
                        if not (first and pg < 2):
                            act.wait_ge(sem("pv_done0"), n - 1)
                        nc.scalar.activation(PT[pg % 2][0:KMAX], PS[0:KMAX, 4:6, 0:3 * TQ],
                                             ACT.Identity).then_inc(sem("pt_evac"), 1)
                    if g == 2 and not first:
                        o_evac(0, b - 1, 1 - par)
                    if g in (4, 5) and not last:
                        k_evac(0, b + 1, 1 - par, g - 4)
                    n = 8 * b + g
                    act.wait_ge(sem("mx_done"), n + 1)
                    if not (first and g < 2):
                        act.wait_ge(sem("t_done"), n - 1)
                    for j in range(2):
                        ins = nc.scalar.activation(PB[g % 2][0:TQ, j, 0:NK], PS[0:TQ, 2 * (g % 2) + j, 0:NK], ACT.Exp,
                                                   bias=NMX[0:TQ, 2 * g + j:2 * g + j + 1],
                                                   accum_out=SUM[0:TQ, g % 2, j:j + 1])
                    ins.then_inc(sem("exp_done"), 1)

            act.wait_ge(sem("pb_zeroed"), 2)
            k_evac(0, 0, 0, 0)
            k_evac(0, 0, 0, 1)
            attn0(0, 0, True, False)
            with act.Fori(0, (NT - 2) // 2) as r:
                for h in range(2):
                    attn0(2 * r + h + 1, 1 - h, False, False)
            attn0(NT - 1, 1, False, True)
            act.wait_ge(sem("t_done"), 8 * NT)
            act.wait_ge(sem("pv_done0"), 8 * NT - 2)
            nc.scalar.activation(PT[1][0:KMAX], PS[0:KMAX, 4:6, 0:3 * TQ], ACT.Identity).then_inc(sem("pt_evac"), 1)
            o_evac(0, NT - 1, 1)

            transposes(1)
            with act.Fori(0, NQ) as q:
                for f in range(FD):
                    act.wait_ge(sem("h_done"), FD * q + f + 1)
                    nc.scalar.activation(HT[:, f, :], PS[:, f % 4, 0:N4], ACT.Relu,
                                         bias=COLS[:, 4 + f:5 + f]).then_inc(sem("h_evac"), 1)
            transposes(2)

            def gate_exp(l, top):
                act.wait_ge(sem(f"top_ready{l}"), 1)
                nc.scalar.activation(GATE[0:TQ, 0:top], GATE[0:TQ, 0:top], ACT.Exp).then_inc(sem(f"gate_exp{l}"), 1)

            gate_exp(0, TOP0)

            xbt, za, zt, s, st, yb = (wk(o, 512) for o in (512, 1024, 2048, 2560, 3072, 3584))
            zt = wk(2048, 512)

            def xt_evac(l, i, par):
                act.wait_ge(sem(f"xt_done{l}"), i + 1)
                nc.scalar.activation(wk(512 + par * D, D), PS[:, 4, 0:D], ACT.Identity).then_inc(sem(f"xt_evac{l}"), 1)

            def y_evac(l, i, par, wait):
                act.wait_ge(sem(f"y_done{l}"), i + 1)
                if wait is not None:
                    act.wait_ge(sem(f"y_out{l}_{par}"), wait)
                nc.scalar.activation(wk(3584 + par * D, D), PS[:, 3, 0:D], ACT.Identity).then_inc(sem(f"y_ready{l}"), 1)

            def blocks0(i, par, first, last, yw):
                act.wait_ge(sem("a_done"), i + 1)
                nc.scalar.activation(za, PS[:, 0, :], ACT.Identity).then_inc(sem("a_copied"), 1)
                if not first:
                    act.wait_ge(sem("st_done"), i)
                    nc.scalar.activation(wk(3072, 512), PS[:, 6, :], ACT.Identity).then_inc(sem("st_evac"), 1)
                if not last:
                    xt_evac(0, i + 1, 1 - par)
                act.wait_ge(sem("zt_done"), i + 1)
                nc.scalar.activation(zt, PS[:, 5, :], ACT.Identity).then_inc(sem("zt_evac"), 1)
                if not first:
                    y_evac(0, i - 1, 1 - par, yw)
                act.wait_ge(sem("g_done"), i + 1)
                nc.scalar.activation(s, PS[:, 2, :], ACT.Silu).then_inc(sem("s_ready"), 1)

            xt_evac(0, 0, 0)
            blocks0(0, 0, True, False, None)
            blocks0(1, 1, False, False, None)
            blocks0(2, 0, False, False, None)
            R0 = (NB0 - 4) // 2
            with act.Fori(0, R0) as r:
                for h in range(2):
                    blocks0(2 * r + 3 + h, 1 - h, False, False, 16 * (r + 1))
            for i in range(2 * R0 + 3, NB0):
                blocks0(i, i % 2, False, i == NB0 - 1, 16 * ((i - 1) // 2))
            act.wait_ge(sem("st_done"), NB0)
            nc.scalar.activation(wk(3072, 512), PS[:, 6, :], ACT.Identity).then_inc(sem("st_evac"), 1)
            y_evac(0, NB0 - 1, (NB0 - 1) % 2, 16 * ((NB0 - 1) // 2))

            transposes(3)

            def attn1(b, par, first, last):
                for ch, (k0, kn) in enumerate(KCH):
                    act.wait_ge(sem("sub_done1"), 3 * b + ch + 1)
                    nc.scalar.activation(EH[ch][0:kn], EH[ch][0:kn], ACT.Exp).then_inc(sem("exp_done1"), 1)
                    if ch < 2 and not last and ch == 0:
                        k_evac(1, b + 1, 1 - par, 0)
                        k_evac(1, b + 1, 1 - par, 1)
                    if ch == 1 and not first:
                        o_evac(1, b - 1, 1 - par)

            k_evac(1, 0, 0, 0)
            k_evac(1, 0, 0, 1)
            attn1(0, 0, True, False)
            with act.Fori(0, (NT - 2) // 2) as r:
                for h in range(2):
                    attn1(2 * r + h + 1, 1 - h, False, False)
            attn1(NT - 1, 1, False, True)
            o_evac(1, NT - 1, 1)

            act.wait_ge(sem("ln_out"), 6 * NQ)
            with act.Fori(0, NT) as t:
                nc.scalar.activation(XN[0:TQ, t, :], U[0:TQ, t, :], ACT.Square,
                                     accum_out=MV[0:TQ, t, 0:1]).then_inc(sem("sq_done"), 1)
            transposes(4)
            gate_exp(1, TOP1)

            def blocks1(i, par, first, last, yw):
                act.wait_ge(sem("a_min"), i + 1)
                nc.scalar.activation(wk(1280, D), wk(1024, D), ACT.Sigmoid, scale=1.702).then_inc(sem("sig_ready"), 1)
                if not first:
                    act.wait_ge(sem("st_done1"), i)
                    nc.scalar.activation(wk(3072, D), PS[:, 6, 0:D], ACT.Identity).then_inc(sem("st_evac1"), 1)
                if not last:
                    xt_evac(1, i + 1, 1 - par)
                if not first:
                    y_evac(1, i - 1, 1 - par, yw)

            xt_evac(1, 0, 0)
            blocks1(0, 0, True, False, None)
            blocks1(1, 1, False, False, None)
            blocks1(2, 0, False, False, None)
            R1 = (NB1 - 4) // 2
            with act.Fori(0, R1) as r:
                for h in range(2):
                    blocks1(2 * r + 3 + h, 1 - h, False, False, 16 * (r + 1))
            for i in range(2 * R1 + 3, NB1):
                blocks1(i, i % 2, False, i == NB1 - 1, 16 * ((i - 1) // 2))
            act.wait_ge(sem("st_done1"), NB1)
            nc.scalar.activation(wk(3072, D), PS[:, 6, 0:D], ACT.Identity).then_inc(sem("st_evac1"), 1)
            y_evac(1, NB1 - 1, (NB1 - 1) % 2, 16 * ((NB1 - 1) // 2))

        @block.vector
        def _(dve):
            link = Chain(dve, sem("v_chain"))

            dve.wait_ge(sem("in_const"), 16)
            dve.wait_ge(sem("in_x"), 16)

            def norm(n, src, gamma=None, beta=None):
                with dve.Fori(0, NT) as t:
                    nc.vector.bn_stats(ST6[0:TQ, t, :], src[0:TQ, t, :]).then_inc(sem("bn_done"), 1)
                dve.wait_ge(sem("bn_done"), NT * (n + 1))
                me, mo, m2e, m2o = (ST6[0:TQ, :, c] for c in (1, 4, 2, 5))
                mean, dif, rs = MV[0:TQ, :, 0], MV[0:TQ, :, 1], RS[0:TQ]
                link(nc.vector.tensor_tensor(mean, me, mo, ALU.add))
                link(nc.vector.tensor_scalar(mean, mean, 0.5, None, ALU.mult))
                link(nc.vector.tensor_tensor(dif, me, mo, ALU.subtract))
                link(nc.vector.scalar_tensor_tensor(out=dif, in0=dif, scalar=0.25, in1=dif, op0=ALU.mult, op1=ALU.mult))
                link(nc.vector.tensor_tensor(rs, m2e, m2o, ALU.add))
                link(nc.vector.scalar_tensor_tensor(out=rs, in0=rs, scalar=1.0 / D, in1=dif, op0=ALU.mult, op1=ALU.add))
                nc.vector.tensor_scalar(rs, rs, EPS, None, ALU.add).then_inc(sem("ln_var"), 1)
                dve.wait_ge(sem("ln_rstd"), n + 1)
                per = QUAD if gamma is None else QUAD + 1
                ch = Chain(dve, sem(f"ln_chain{n}"))
                with dve.Fori(0, NQ) as q:
                    ch.begin(q * 2)
                    for j in range(QUAD):
                        t = q * QUAD + j
                        ins = nc.vector.tensor_scalar(U[0:TQ, t, :], src[0:TQ, t, :], MV[0:TQ, t, 0:1],
                                                      RS[0:TQ, bass.ds(t, 1)], ALU.subtract, ALU.mult)
                    if gamma is not None:
                        ch(ins)
                        v = U[0:TQ, bass.ds(q * QUAD, QUAD), :]
                        ch(nc.vector.tensor_tensor(v, v, gamma[0:TQ].unsqueeze(1).to_broadcast([TQ, QUAD, D]), ALU.mult))
                        ins = nc.vector.tensor_tensor(v, v, beta[0:TQ].unsqueeze(1).to_broadcast([TQ, QUAD, D]), ALU.add)
                    ins.then_inc(sem("ln_out"), 1)
                dve.wait_ge(sem("ln_out"), NQ * (n + 1))

            def q_evac(l):
                for i in range(2 * NQ):
                    g, m = i // 2, i % 2
                    dve.wait_ge(sem(f"q_done{l}"), i + 1)
                    c = (0 if l == 0 else 12) + m
                    nc.vector.tensor_scalar(QT[:, m, g * N4:(g + 1) * N4], PS[:, 4 + i % 4, 0:N4],
                                            COLS[:, c:c + 1], None, ALU.add).then_inc(sem(f"q_evac{l}"), 1)

            def v_evac(l, b, par, c):
                kn = KCH[c][1]
                dve.wait_ge(sem(f"v_done{l}"), 3 * b + c + 1)
                bank = 7 if l == 0 else 6 + c % 2
                ps = PS[0:kn, bank, 0:D].rearrange("p (a j d) -> p a j d", j=2, d=HD)
                bv = BC[0][0:kn].rearrange("p (a j d) -> p a j d", j=2, d=HD)
                for j in range(2):
                    v = VP[par][0:kn, c, j, :].rearrange("p (a j d) -> p a j d", j=2, d=HD)
                    ins = nc.vector.tensor_tensor(v[:, :, j, :], ps[:, :, j, :], bv[:, :, j, :], ALU.add)
                ins.then_inc(sem(f"v_evac{l}"), 1)

            dve.wait_ge(sem("in_br"), 16 * 18)
            for br, o, n in ((BR0, 0, 3 * F0 + D), (BR1, 2048, 2 * F1 + D)):
                w = wk(o, n)
                link(nc.vector.tensor_copy(br[0:96], w[0:96]))
                link(nc.vector.tensor_tensor(w[0:96], w[0:96], br[0:96], ALU.subtract))
                link(nc.vector.tensor_copy(br[32:64], w[32:64]))
                link(nc.vector.tensor_copy(br[64:96], w[64:96]))
                link(nc.vector.tensor_tensor(w[64:96], w[64:96], br[64:96], ALU.subtract))
                link(nc.vector.tensor_copy(br[64:96], w[64:96]))

            norm(0, X)
            dve.wait_ge(sem("in_cols"), 16)
            q_evac(0)

            ch0 = Chain(dve, sem("attn_chain0"))

            def p_norm(b, g, ch):
                dve.wait_ge(sem("exp_done"), 8 * b + g + 1)
                ch(nc.vector.reciprocal(RCP[0:TQ, g % 2, :], SUM[0:TQ, g % 2, :]))
                for j in range(2):
                    v = PB[g % 2][0:TQ, j, 0:NK]
                    ins = nc.vector.tensor_scalar(v, v, RCP[0:TQ, g % 2, j:j + 1], None, ALU.mult)
                ins.then_inc(sem("p_done"), 1)

            def wo_add0(b, par):
                dve.wait_ge(sem("wo_done0"), b + 1)
                nc.vector.tensor_tensor(TMP[0:TQ, par, :], PS[0:TQ, 7, 0:D], BC[1][0:TQ], ALU.add).then_inc(
                    sem("wo_evac0"), 1)
                dve.wait_ge(sem("wo_evac0"), b + 1)
                u = U[0:TQ, b, :]
                nc.vector.tensor_tensor(u, u, TMP[0:TQ, par, :], ALU.add).then_inc(sem("wo_added0"), 1)

            def attn0(b, par, first, last, ch):
                for g in range(8):
                    if g > 0 or not first:
                        p_norm(*((b, g - 1) if g else (b - 1, 7)), ch)
                    if g == 0 and not first:
                        v_evac(0, b, par, 2)
                    if g == 3 and not first:
                        wo_add0(b - 1, 1 - par)
                    if g in (6, 7) and not last:
                        v_evac(0, b + 1, 1 - par, g - 6)
                    n = 8 * b + g
                    dve.wait_ge(sem("s_done0"), n + 1)
                    nc.vector.tensor_reduce(NMX[0:TQ, 2 * g:2 * g + 2], PS[0:TQ, 2 * (g % 2):2 * (g % 2) + 2, 0:NK],
                                            axis=AX.X, op=ALU.max, negate=True).then_inc(sem("mx_done"), 1)

            dve.wait_ge(sem("in_bc"), 16 * 7)
            dve.wait_ge(sem("vp_zeroed"), 2)
            for c in range(3):
                v_evac(0, 0, 0, c)
            attn0(0, 0, True, False, ch0)
            with dve.Fori(0, (NT - 2) // 2) as r:
                ch0.begin(r * 16 + 7)
                for h in range(2):
                    attn0(2 * r + h + 1, 1 - h, False, False, ch0)
                assert ch0.n == 16
            ch0.begin(7 + 16 * ((NT - 2) // 2))
            attn0(NT - 1, 1, False, True, ch0)
            p_norm(NT - 1, 7, ch0)
            wo_add0(NT - 1, 1)
            dve.wait_ge(sem("wo_added0"), NT)

            norm(1, U, BC[2], BC[3])

            with dve.Fori(0, NQ) as q:
                for j in range(QUAD):
                    t = q * QUAD + j
                    dve.wait_ge(sem("f_done"), t + 1)
                    nc.vector.tensor_tensor(TMP[0:TQ, j % 2, :], PS[0:TQ, 4 + j, 0:D], BC[4][0:TQ],
                                            ALU.add).then_inc(sem("f_evac"), 1)
                    dve.wait_ge(sem("f_evac"), t + 1)
                    u = U[0:TQ, t, :]
                    nc.vector.tensor_tensor(u, u, TMP[0:TQ, j % 2, :], ALU.add).then_inc(sem("ff_added"), 1)
            dve.wait_ge(sem("ff_added"), NT)
            norm(2, U, BC[5], BC[6])
            dve.wait_ge(sem("tg_ready"), 1)
            link(nc.vector.scalar_tensor_tensor(out=X[0:TQ], in0=U[0:TQ], scalar=TG[0:TQ, 0:1], in1=X[0:TQ],
                                                op0=ALU.mult, op1=ALU.add))
            norm(3, X)

            def route(l, top, E, nb, stride, logit_ps):
                NE = NT * E
                c0 = 0 if l == 0 else E0
                L, SC, M, A, B, C, POS = (wk(o * 256, NE) for o in range(7))
                OH = [wk((7 + k) * 256, NE) for k in range(top)]
                v3 = lambda t, n=TQ: t[0:n].rearrange("p (t e) -> p t e", e=E)
                dve.wait_ge(sem("in_gw"), 16 * 4)
                dve.wait_ge(sem(f"logit_done{l}"), 1)
                link(nc.vector.tensor_tensor(v3(L), v3(logit_ps), GB[0:TQ, c0:c0 + E].unsqueeze(1).to_broadcast([TQ, NT, E]), ALU.add))
                rev = CST[0:TQ, (C_REV0 if l == 0 else C_REV1):(C_REV0 if l == 0 else C_REV1) + E].unsqueeze(1).to_broadcast([TQ, NT, E])
                for k in range(top):
                    link(nc.vector.tensor_reduce(GATE[0:TQ, k, :], v3(L), axis=AX.X, op=ALU.max))
                    link(nc.vector.tensor_tensor(v3(SC), v3(L), GATE[0:TQ, k, :].unsqueeze(2).to_broadcast([TQ, NT, E]), ALU.is_equal))
                    link(nc.vector.tensor_tensor(v3(SC), v3(SC), rev, ALU.mult))
                    link(nc.vector.tensor_reduce(RS[0:TQ], v3(SC), axis=AX.X, op=ALU.max))
                    link(nc.vector.tensor_tensor(v3(OH[k]), v3(SC), RS[0:TQ].unsqueeze(2).to_broadcast([TQ, NT, E]), ALU.is_equal))
                    if k + 1 < top:
                        link(nc.vector.scalar_tensor_tensor(out=L[0:TQ], in0=OH[k][0:TQ], scalar=-3.0e38, in1=L[0:TQ],
                                                            op0=ALU.mult, op1=ALU.add))
                    if k:
                        src = OH[0] if k == 1 else M
                        ins = nc.vector.tensor_tensor(M[0:TQ], src[0:TQ], OH[k][0:TQ], ALU.add)
                        if k == top - 1:
                            ins.then_inc(sem(f"mask_ready{l}"), 1)
                            dve.wait_ge(sem(f"mask_ready{l}"), 1)
                        else:
                            link(ins)
                link(nc.vector.tensor_copy(RS[0:TQ], GATE[0:TQ, 0, :]))
                nc.vector.tensor_tensor(GATE[0:TQ, 0:top], GATE[0:TQ, 0:top], RS[0:TQ].unsqueeze(1).to_broadcast([TQ, top, NT]),
                                        ALU.subtract).then_inc(sem(f"top_ready{l}"), 1)
                dve.wait_ge(sem(f"gate_exp{l}"), 1)
                link(nc.vector.tensor_reduce(RS[0:TQ], GATE[0:TQ, 0:top].rearrange("p k t -> p t k"), axis=AX.X, op=ALU.add))
                link(nc.vector.reciprocal(RS[0:TQ], RS[0:TQ]))
                link(nc.vector.tensor_scalar(RS[0:TQ], RS[0:TQ], TG[0:TQ, 2 + l:3 + l], None, ALU.mult))
                link(nc.vector.tensor_tensor(GATE[0:TQ, 0:top], GATE[0:TQ, 0:top], RS[0:TQ].unsqueeze(1).to_broadcast([TQ, top, NT]), ALU.mult))
                dve.wait_ge(sem(f"rank_done{l}"), 1)
                link(nc.vector.tensor_copy(C, PS[:, 1, 0:NE]))
                src, dst = C, A
                s = 1
                while s < NT:
                    link(nc.vector.tensor_tensor(dst[:, s * E:NE], src[:, s * E:NE], src[:, 0:NE - s * E], ALU.add))
                    link(nc.vector.tensor_copy(dst[:, 0:s * E], src[:, 0:s * E]))
                    src, dst = dst, (B if dst is A else A)
                    s *= 2
                cnt = src[:, NE - E:NE]
                link(nc.vector.tensor_tensor(POS, src, C, ALU.subtract))
                link(nc.vector.tensor_tensor(POS[0:TQ], POS[0:TQ], PS[0:TQ, 0, 0:NE], ALU.add))
                big = wk(11 * 256, 1040)
                cmp = big[:, 0:E * CNT].rearrange("p (e c) -> p e c", c=CNT)
                link(nc.vector.tensor_tensor(cmp, cnt.unsqueeze(2).to_broadcast([P, E, CNT]),
                                             CST[:, C_THR:C_THR + CNT].unsqueeze(1).to_broadcast([P, E, CNT]), ALU.is_gt))
                NBK, S1, S2 = (SC[:, o * E:(o + 1) * E] for o in range(3))
                link(nc.vector.tensor_reduce(NBK, cmp, axis=AX.X, op=ALU.add))
                src, dst, s = NBK, S1, 1
                while s < E:
                    link(nc.vector.tensor_tensor(dst[:, s:E], src[:, s:E], src[:, 0:E - s], ALU.add))
                    link(nc.vector.tensor_copy(dst[:, 0:s], src[:, 0:s]))
                    src, dst = dst, (S2 if dst is S1 else S1)
                    s *= 2
                link(nc.vector.tensor_tensor(dst, src, NBK, ALU.subtract))
                link(nc.vector.tensor_scalar(dst, dst, float(P), None, ALU.mult))
                link(nc.vector.tensor_tensor(v3(POS), v3(POS), dst[0:TQ].unsqueeze(1).to_broadcast([TQ, NT, E]), ALU.add))
                for k in range(top):
                    link(nc.vector.tensor_tensor(OH[k][0:TQ], OH[k][0:TQ], POS[0:TQ], ALU.mult))
                    link(nc.vector.tensor_reduce(RS[0:TQ], v3(OH[k]), axis=AX.X, op=ALU.add))
                    link(nc.vector.tensor_copy(SLOT[0:TQ, k, :], RS[0:TQ]))
                be = big[:, 0:nb * E].rearrange("p (i e) -> p i e", e=E)
                link(nc.vector.tensor_tensor(be, src.unsqueeze(1).to_broadcast([P, nb, E]),
                                             CST[:, C_IOTA:C_IOTA + nb].unsqueeze(2).to_broadcast([P, nb, E]), ALU.is_le))
                ebf = M[:, 0:nb]
                link(nc.vector.tensor_reduce(ebf, be, axis=AX.X, op=ALU.add))
                link(nc.vector.tensor_scalar(ebf, ebf, float(E - 1), None, ALU.min))
                link(nc.vector.tensor_scalar(OHB[:, 0:nb], ebf, CST[:, C_PE:C_PE + 1], None, ALU.is_equal))
                link(nc.vector.tensor_scalar(EBI[:, 0:nb], ebf, float(stride), None, ALU.mult))
                nc.vector.tensor_copy(L[0:TQ, 0:1], RS[0:TQ, 0:1]).then_inc(sem(f"slots_ready{l}"), 1)

            route(0, TOP0, E0, NB0, W0, PS[:, 2, 0:NT * E0])

            def onehot(l, i, par, wait):
                if wait:
                    dve.wait_ge(sem(f"y_done{l}"), i - 1)
                nc.vector.tensor_copy(OHX[0:96, par, :], OHB[0:96, bass.ds(i, 1)].to_broadcast([96, P])).then_inc(
                    sem(f"oh_ready{l}"), 1)

            def blocks0(i, par, more):
                dve.wait_ge(sem("ab_done0"), i + 1)
                dve.wait_ge(sem("a_copied"), i + 1)
                nc.vector.tensor_tensor(wk(1536, 512), wk(1024, 512), PS[:, 1, :], ALU.mult).then_inc(sem("z_ready"), 1)
                if more:
                    onehot(0, i + 1, 1 - par, True)

            onehot(0, 0, 0, False)
            onehot(0, 1, 1, False)
            blocks0(0, 0, False)
            R = (NB0 - 2) // 2
            with dve.Fori(0, R) as r:
                for h in range(2):
                    blocks0(2 * r + h + 1, 1 - h, True)
            for i in range(2 * R + 1, NB0):
                blocks0(i, i % 2, i + 1 < NB0)

            def combine(l, top):
                for t in range(NT):
                    for k in range(top):
                        n = t * top + k
                        dve.wait_ge(sem(f"y_back{l}_{n % 8}"), 16 * (n // 8 + 1))
                        nc.vector.scalar_tensor_tensor(out=X[0:TQ, t, :], in0=wk(1024 + (n % 8) * D, D)[0:TQ],
                                                       scalar=GATE[0:TQ, k, t:t + 1], in1=X[0:TQ, t, :],
                                                       op0=ALU.mult, op1=ALU.add).then_inc(sem(f"y_used{l}"), 1)
                        dve.wait_ge(sem(f"y_used{l}"), n + 1)

            combine(0, TOP0)
            nc.vector.memset(TMP[:, 0, 0:1], 0.0).then_inc(sem("e0_all_done"), 1)

            norm(4, X)
            q_evac(1)
            ch1 = Chain(dve, sem("attn_chain1"))

            def head_sum(b, c):
                kn = KCH[c][1]
                dve.wait_ge(sem("exp_done1"), 3 * b + c + 1)
                e = EH[c][0:kn].rearrange("p a (h t) -> p t (a h)", h=QUAD)
                nc.vector.tensor_reduce(SMH[0:kn, c, :], e, axis=AX.X, op=ALU.add).then_inc(sem("hsum_done1"), 1)
                dve.wait_ge(sem("hsum_done1"), 3 * b + c + 1)
                nc.vector.reciprocal(SMH[0:kn, c, :], SMH[0:kn, c, :]).then_inc(sem("rcp_done1"), 1)

            def wo_add1(b, par):
                dve.wait_ge(sem("wo_done1"), b + 1)
                nc.vector.tensor_tensor(TMP[0:TQ, par, :], PS[0:TQ, 7, 0:D], BC[1][0:TQ], ALU.add).then_inc(
                    sem("wo_evac1"), 1)
                dve.wait_ge(sem("wo_evac1"), b + 1)
                x = X[0:TQ, b, :]
                nc.vector.scalar_tensor_tensor(out=x, in0=TMP[0:TQ, par, :], scalar=TG[0:TQ, 1:2], in1=x,
                                               op0=ALU.mult, op1=ALU.add).then_inc(sem("wo_added1"), 1)

            def attn1(b, par, first, last):
                for c, (k0, kn) in enumerate(KCH):
                    if c or not first:
                        head_sum(*((b, c - 1) if c else (b - 1, 2)))
                    if c == 0 and not first:
                        v_evac(1, b, par, 2)
                    n = 3 * b + c
                    dve.wait_ge(sem("s_done1"), n + 1)
                    s4 = PS[0:kn, 0:4, 0:N4].rearrange("p a (h t) -> p a h t", h=QUAD)
                    nc.vector.tensor_reduce(MXH[0:kn], s4.rearrange("p a h t -> p t a h"), axis=AX.XY,
                                            op=ALU.max).then_inc(sem("hmax_done1"), 1)
                    dve.wait_ge(sem("hmax_done1"), n + 1)
                    if not first:
                        dve.wait_ge(sem("pv_done1"), 3 * (b - 1) + c + 1)
                    for bk in range(4):
                        ins = nc.vector.tensor_tensor(EH[c][0:kn, bk, :].rearrange("p (h t) -> p h t", h=QUAD), s4[:, bk],
                                                      MXH[0:kn].unsqueeze(1).to_broadcast([kn, QUAD, TQ]), ALU.subtract)
                    ins.then_inc(sem("sub_done1"), 1)
                    if c == 1 and not last:
                        v_evac(1, b + 1, 1 - par, 0)
                        v_evac(1, b + 1, 1 - par, 1)
                    if c == 2 and not first:
                        wo_add1(b - 1, 1 - par)

            dve.wait_ge(sem("in_w4b"), 16 * 6)
            dve.wait_ge(sem("vp_zeroed"), 4)
            for c in range(3):
                v_evac(1, 0, 0, c)
            attn1(0, 0, True, False)
            with dve.Fori(0, (NT - 2) // 2) as r:
                for h in range(2):
                    attn1(2 * r + h + 1, 1 - h, False, False)
            attn1(NT - 1, 1, False, True)
            head_sum(NT - 1, 2)
            wo_add1(NT - 1, 1)
            dve.wait_ge(sem("wo_added1"), NT)

            norm(5, X)
            dve.wait_ge(sem("sq_done"), NT)
            nc.vector.tensor_scalar(RS[0:TQ], MV[0:TQ, :, 0], 1.0 / D, EPS, ALU.mult, ALU.add).then_inc(sem("ln_var"), 1)
            dve.wait_ge(sem("ln_rstd"), 7)
            dve.wait_ge(sem("in_nsc"), 16)
            with dve.Fori(0, NT) as t:
                nc.vector.scalar_tensor_tensor(out=XN[0:TQ, t, :], in0=U[0:TQ, t, :], scalar=RS[0:TQ, bass.ds(t, 1)],
                                               in1=NSC[0:TQ], op0=ALU.mult, op1=ALU.mult).then_inc(sem("xn_out"), 1)
            link(nc.vector.scalar_tensor_tensor(out=X[0:TQ], in0=U[0:TQ], scalar=TG[0:TQ, 3:4], in1=X[0:TQ],
                                                op0=ALU.mult, op1=ALU.add))
            dve.wait_ge(sem("xn_out"), NT)
            route(1, TOP1, E1, NB1, W1, PS[:, 2, 0:NT * E1])
            onehot(1, 0, 0, False)
            onehot(1, 1, 1, False)
            ch = Chain(dve, sem("blk_chain1"))

            def blocks1(i, par, more, ch):
                dve.wait_ge(sem("ab_done1"), i + 1)
                nc.vector.tensor_scalar(wk(1024, D), PS[:, 0, 0:D], 7.0, None, ALU.min).then_inc(sem("a_min"), 1)
                dve.wait_ge(sem("a_min"), i + 1)
                nc.vector.tensor_scalar(wk(1536, D), PS[:, 0, D:2 * D], 7.0, -7.0, ALU.min, ALU.max).then_inc(
                    sem("b_clip"), 1)
                dve.wait_ge(sem("b_clip"), i + 1)
                ch(nc.vector.scalar_tensor_tensor(out=wk(1792, D), in0=wk(1536, D), scalar=1.0, in1=wk(1024, D),
                                                  op0=ALU.add, op1=ALU.mult))
                dve.wait_ge(sem("sig_ready"), i + 1)
                nc.vector.tensor_tensor(wk(2560 + par * D, D), wk(1792, D), wk(1280, D), ALU.mult).then_inc(sem("s_ready1"), 1)
                if more:
                    onehot(1, i + 1, 1 - par, True)

            blocks1(0, 0, False, ch)
            R = (NB1 - 2) // 2
            with dve.Fori(0, R) as r:
                ch.begin(2 * r + 1)
                for h in range(2):
                    blocks1(2 * r + h + 1, 1 - h, True, ch)
            ch.begin(2 * R + 1)
            for i in range(2 * R + 1, NB1):
                blocks1(i, i % 2, i + 1 < NB1, ch)
            combine(1, TOP1)
            nc.vector.memset(TMP[:, 0, 0:1], 0.0).then_inc(sem("x_final"), 1)

        @block.tensor
        def _(pe):
            mm = nc.tensor.matmul
            pe.wait_ge(sem("in_const"), 16)

            def transposes(n, src, ready, per_quad):
                for g in range(NQ):
                    pe.wait_ge(sem(ready), per_quad(g))
                    for c in range(KD):
                        i = KD * g + c
                        if i >= 4:
                            pe.wait_ge(sem("tr_evac"), 2 * NQ * n + i - 3)
                        for j in range(QUAD):
                            ins = nc.tensor.transpose(PS[:, i % 4, j * TQ:(j + 1) * TQ],
                                                      src[0:TQ, g * QUAD + j, c * P:(c + 1) * P], IDN[0:TQ, 0:TQ])
                        ins.then_inc(sem("tr_done"), 1)

            def q_proj(l, n):
                for i in range(2 * NQ):
                    g, m = i // 2, i % 2
                    if m == 0:
                        pe.wait_ge(sem("tr_evac"), 2 * NQ * n + 2 * (g + 1))
                    if i >= 4:
                        pe.wait_ge(sem(f"q_evac{l}"), i - 3)
                    for k in range(KD):
                        ins = mm(PS[:, 4 + i % 4, 0:N4], WQ[:, k, m * P:(m + 1) * P], UT[:, k, g * N4:(g + 1) * N4],
                                 start=(k == 0), stop=(k == KD - 1))
                    ins.then_inc(sem(f"q_done{l}"), 1)

            def k_proj(l, par, m):
                for k in range(KD):
                    ins = mm(PS[:, 7 if l == 0 else 6 + m, 0:NK], WK[:, k, m * P:(m + 1) * P], CT[par][:, k, :],
                             start=(k == 0), stop=(k == KD - 1))
                ins.then_inc(sem(f"k_done{l}"), 1)

            def v_proj(l, par, c):
                k0, kn = KCH[c]
                for k in range(KD):
                    ins = mm(PS[0:kn, 7 if l == 0 else 6 + c % 2, 0:D], CT[par][:, k, k0:k0 + kn], WV[:, k, :],
                             start=(k == 0), stop=(k == KD - 1))
                ins.then_inc(sem(f"v_done{l}"), 1)

            def wo_proj(l, b, par):
                pe.wait_ge(sem(f"o_evac{l}"), b + 1)
                for k in range(KD):
                    ins = mm(PS[0:TQ, 7, 0:D], ATV[par][:, k, :], WO[:, k, :], start=(k == 0), stop=(k == KD - 1))
                ins.then_inc(sem(f"wo_done{l}"), 1)

            transposes(0, U, "ln_out", lambda g: g + 1)
            pe.wait_ge(sem("in_w4"), 16 * 4)
            q_proj(0, 0)

            def scores0(b, par, g, first):
                n = 8 * b + g
                if g == 0:
                    pe.wait_ge(sem("qb_done0"), 2 * (b + 1))
                    pe.wait_ge(sem("k_evac0"), 2 * (b + 1))
                if not (first and g < 2):
                    pe.wait_ge(sem("exp_done"), n - 1)
                for j in range(2):
                    h = 2 * g + j
                    ins = mm(PS[0:TQ, 2 * (g % 2) + j, 0:NK], QB[par][:, h // 8, h % 8, :], KT[par][:, h // 8, :],
                             start=True, stop=True)
                ins.then_inc(sem("s_done0"), 1)

            def p_transpose(b, g, first):
                n = 8 * b + g
                pe.wait_ge(sem("p_done"), n + 1)
                pe.wait_ge(sem("pt_evac"), n)
                for j in range(2):
                    for c in range(3):
                        ins = nc.tensor.transpose(PS[0:KMAX, 4 + j, c * TQ:(c + 1) * TQ],
                                                  PB[g % 2][0:TQ, j, c * KMAX:(c + 1) * KMAX], IDN[0:TQ, 0:TQ])
                ins.then_inc(sem("t_done"), 1)

            def values0(b, par, g):
                n = 8 * b + g
                pe.wait_ge(sem("pt_evac"), n + 1)
                if g == 0:
                    pe.wait_ge(sem("v_evac0"), 3 * (b + 1))
                    pe.wait_ge(sem("o_evac0"), b)
                q, c8 = g % 4, g // 4
                for j in range(2):
                    for c, (k0, kn) in enumerate(KCH):
                        ins = mm(PS[32 * q:32 * q + 32, 6, c8 * TQ:(c8 + 1) * TQ], VP[par][0:kn, c, j, 32 * g:32 * g + 32],
                                 PT[g % 2][0:kn, j, c * TQ:(c + 1) * TQ], start=(j == 0 and c == 0), stop=(j == 1 and c == 2))
                ins.then_inc(sem("pv_done0"), 1)

            def proj_piece0(b, par, i, first):
                if i == 0:
                    if first:
                        pe.wait_ge(sem("v_evac0"), 3)
                    else:
                        pe.wait_ge(sem("wo_evac0"), b - 1)
                    pe.wait_ge(sem(f"in_ct{par}"), 16 * (b // 2 + 1) if isinstance(b, int) else first_ct(b, par))
                    k_proj(0, par, 0)
                elif i == 1:
                    pe.wait_ge(sem("k_evac0"), 2 * b + 1)
                    k_proj(0, par, 1)
                else:
                    pe.wait_ge(sem("k_evac0"), 2 * b + 2)
                    pe.wait_ge(sem("v_evac0"), 3 * b + i - 2)
                    v_proj(0, par, i - 2)

            ct_expr = {}

            def first_ct(b, par):
                return ct_expr["v"]

            def attn0(b, par, first, last):
                for g in range(8):
                    scores0(b, par, g, first)
                    if g > 0 or not first:
                        p_transpose(*((b, g - 1) if g else (b - 1, 7)), first)
                    if g == 2 and not first:
                        pe.wait_ge(sem("v_evac0"), 3 * (b + 1))
                        wo_proj(0, b - 1, 1 - par)
                    if g >= 3 and not last:
                        proj_piece0(b + 1, 1 - par, g - 3, first)
                    if g >= 2:
                        values0(b, par, g - 2)
                    elif not first:
                        values0(b - 1, 1 - par, 6 + g)

            pe.wait_ge(sem("in_ct0"), 16)
            pe.wait_ge(sem("q_evac0"), 2 * NQ)
            k_proj(0, 0, 0)
            pe.wait_ge(sem("k_evac0"), 1)
            k_proj(0, 0, 1)
            for c in range(3):
                pe.wait_ge(sem("k_evac0"), 2)
                if c:
                    pe.wait_ge(sem("v_evac0"), c)
                v_proj(0, 0, c)
            attn0(0, 0, True, False)
            with pe.Fori(0, (NT - 2) // 2) as r:
                for h in range(2):
                    ct_expr["v"] = 16 * (r + 2)
                    attn0(2 * r + h + 1, 1 - h, False, False)
            attn0(NT - 1, 1, False, True)
            p_transpose(NT - 1, 7, False)
            values0(NT - 1, 1, 6)
            values0(NT - 1, 1, 7)
            pe.wait_ge(sem("wo_evac0"), NT - 1)
            wo_proj(0, NT - 1, 1)

            transposes(1, U, "ln_out", lambda g: NQ + g + 1)
            pe.wait_ge(sem("in_ffw"), 32)
            pe.wait_ge(sem("tr_evac"), 2 * NQ * 2)
            with pe.Fori(0, NQ) as q:
                for f in range(FD):
                    if f > 3:
                        pe.wait_ge(sem("h_evac"), FD * q + f - 3)
                    for k in range(KD):
                        ins = mm(PS[:, f % 4, 0:N4], W1S[:, k, f * P:(f + 1) * P], UT[:, k, bass.ds(q * N4, N4)],
                                 start=(k == 0), stop=(k == KD - 1))
                    ins.then_inc(sem("h_done"), 1)
                pe.wait_ge(sem("h_evac"), FD * q + FD)
                for j in range(QUAD):
                    if j == 3:
                        pe.wait_ge(sem("f_evac"), QUAD * q + 1)
                    for f in range(FD):
                        ins = mm(PS[0:TQ, 4 + j, 0:D], HT[:, f, j * TQ:(j + 1) * TQ], W2S[:, f, :],
                                 start=(f == 0), stop=(f == FD - 1))
                    ins.then_inc(sem("f_done"), 1)
                pe.wait_ge(sem("f_evac"), QUAD * q + 3)

            def logits(l, n, E):
                c0 = 0 if l == 0 else E0
                pe.wait_ge(sem("in_gw"), 16 * 4)
                pe.wait_ge(sem("tr_evac"), 2 * NQ * (n + 1))
                for t in range(NT):
                    for k in range(KD):
                        ins = mm(PS[0:TQ, 2, t * E:(t + 1) * E], UT[:, k, t * TQ:(t + 1) * TQ], GW[:, k, c0:c0 + E],
                                 start=(k == 0), stop=(k == KD - 1))
                ins.then_inc(sem(f"logit_done{l}"), 1)
                pe.wait_ge(sem(f"mask_ready{l}"), 1)
                M = wk(2 * 256, NT * E)
                mm(PS[0:TQ, 0, 0:NT * E], CST[0:TQ, C_TRI:C_TRI + TQ], M[0:TQ], start=True, stop=True)
                mm(PS[:, 1, 0:NT * E], CST[0:TQ, C_ONE:C_ONE + P], M[0:TQ], start=True, stop=True).then_inc(
                    sem(f"rank_done{l}"), 1)

            transposes(2, U, "ln_out", lambda g: 3 * NQ + g + 1)
            logits(0, 2, E0)

            def x_transpose(l, i, par, w):
                pe.wait_ge(sem(f"in_blk{l}_{par}"), w)
                for c in range(KD):
                    ins = nc.tensor.transpose(PS[:, 4, c * P:(c + 1) * P], wk(par * D + c * P, P), IDN)
                ins.then_inc(sem(f"xt_done{l}"), 1)

            def row(o, n):
                return AR[:, bass.ds(o, n)]

            def expert_of(i, E, stride):
                return pe.value_load(EBI[0:1, bass.ds(i, 1)], min_val=0, max_val=(E - 1) * stride)

            def y_proj(l, off, nk, o3, br, brc, par):
                mm(PS[:, 3, 0:D], OHX[0:96, par, :], br[0:96, brc:brc + D], start=True, stop=False)
                for k in range(nk):
                    ins = mm(PS[:, 3, 0:D], wk(3072 + k * P, P), row(off + o3 + k * D, D), start=False, stop=(k == nk - 1))
                ins.then_inc(sem(f"y_done{l}"), 1)

            def ab0(i, par, first):
                off = expert_of(i, E0, W0)
                pe.wait_ge(sem("xt_evac0"), i + 1)
                pe.wait_ge(sem("oh_ready0"), i + 1)
                if not first:
                    pe.wait_ge(sem("z_ready"), i)
                for m in range(2):
                    mm(PS[:, m, :], OHX[0:96, par, :], BR0[0:96, m * F0:(m + 1) * F0], start=True, stop=False)
                    for k in range(KD):
                        ins = mm(PS[:, m, :], wk(512 + par * D + k * P, P), row(off + m * 1024 + k * F0, F0),
                                 start=False, stop=(k == KD - 1))
                    ins.then_inc(sem("a_done" if m == 0 else "ab_done0"), 1)

            def t4(src, bank, name, waits):
                for s_, v in waits:
                    pe.wait_ge(sem(s_), v)
                for k in range(4):
                    ins = nc.tensor.transpose(PS[:, bank, k * P:(k + 1) * P], wk(src + k * P, P), IDN)
                ins.then_inc(sem(name), 1)

            def blocks0(i, par, first, last, w):
                ab0(i, par, first)
                if not first:
                    t4(2560, 6, "st_done", [("s_ready", i)])
                if not last:
                    x_transpose(0, i + 1, 1 - par, w)
                t4(1536, 5, "zt_done", [("z_ready", i + 1)])
                if not first:
                    off = expert_of(i - 1, E0, W0)
                    pe.wait_ge(sem("st_evac"), i)
                    y_proj(0, off, 4, 4096, BR0, 3 * F0, 1 - par)
                off = expert_of(i, E0, W0)
                pe.wait_ge(sem("zt_evac"), i + 1)
                if not first:
                    pe.wait_ge(sem("s_ready"), i)
                mm(PS[:, 2, :], OHX[0:96, par, :], BR0[0:96, 2 * F0:3 * F0], start=True, stop=False)
                for k in range(4):
                    ins = mm(PS[:, 2, :], wk(2048 + k * P, P), row(off + 2048 + k * F0, F0), start=False, stop=(k == 3))
                ins.then_inc(sem("g_done"), 1)

            pe.wait_ge(sem("slots_ready0"), 1)
            pe.wait_ge(sem("in_e0"), 16 * 4 * E0)
            x_transpose(0, 0, 0, 16)
            blocks0(0, 0, True, False, 16)
            R = (NB0 - 2) // 2
            with pe.Fori(0, R) as r:
                for h in range(2):
                    blocks0(2 * r + h + 1, 1 - h, False, False, 16 * (r + 2))
            for i in range(2 * R + 1, NB0):
                blocks0(i, i % 2, False, i == NB0 - 1, 16 * ((i + 1) // 2 + 1))
            t4(2560, 6, "st_done", [("s_ready", NB0)])
            off = expert_of(NB0 - 1, E0, W0)
            pe.wait_ge(sem("st_evac"), NB0)
            pe.wait_ge(sem("y_ready0"), NB0 - 1)
            y_proj(0, off, 4, 4096, BR0, 3 * F0, (NB0 - 1) % 2)

            transposes(3, U, "ln_out", lambda g: 4 * NQ + g + 1)
            pe.wait_ge(sem("in_w4b"), 16 * 6)
            q_proj(1, 3)

            def scores1(b, par, c, first):
                k0, kn = KCH[c]
                n = 3 * b + c
                if c == 0:
                    pe.wait_ge(sem("qb_done1"), 2 * (b + 1))
                    pe.wait_ge(sem("k_evac1"), 2 * (b + 1))
                pe.wait_ge(sem("sub_done1"), n)
                for bk in range(4):
                    q = QB[par][:, bk // 2, (bk % 2) * 4:(bk % 2) * 4 + 4, :].rearrange("p h t -> p (h t)")
                    ins = mm(PS[0:kn, bk, 0:N4], KT[par][:, bk // 2, k0:k0 + kn], q, start=True, stop=True)
                ins.then_inc(sem("s_done1"), 1)

            def values1(b, par, c):
                k0, kn = KCH[c]
                pe.wait_ge(sem("p_done1"), 3 * b + c + 1)
                if c == 0:
                    pe.wait_ge(sem("v_evac1"), 3 * (b + 1))
                    pe.wait_ge(sem("o_evac1"), b)
                for g in range(8):
                    q, c8 = g % 4, g // 4
                    for j in range(2):
                        h = 2 * g + j
                        ins = mm(PS[32 * q:32 * q + 32, 4 + c8, 0:TQ], VP[par][0:kn, c, j, 32 * g:32 * g + 32],
                                 EH[c][0:kn, h // 4, (h % 4) * TQ:(h % 4 + 1) * TQ],
                                 start=(c == 0 and j == 0), stop=(c == 2 and j == 1), skip_group_check=True)
                ins.then_inc(sem("pv_done1"), 1)

            def attn1(b, par, first, last, ctw):
                for c in range(3):
                    scores1(b, par, c, first)
                    if c == 2 and not first:
                        pe.wait_ge(sem("v_evac1"), 3 * (b + 1) + (0 if last else 2))
                        wo_proj(1, b - 1, 1 - par)
                    if c == 2 and not last:
                        pe.wait_ge(sem("v_evac1"), 3 * (b + 1) + 1)
                        v_proj(1, 1 - par, 2)
                    if c < 2 and not first:
                        values1(b - 1, 1 - par, 1 + c)
                    if c == 2:
                        values1(b, par, 0)
                    if c == 0 and not last:
                        pe.wait_ge(sem(f"in_ct{1 - par}b"), ctw)
                        pe.wait_ge(sem("v_evac1"), 3 * (b + 1))
                        k_proj(1, 1 - par, 0)
                        k_proj(1, 1 - par, 1)
                    if c == 1 and not last:
                        pe.wait_ge(sem("k_evac1"), 2 * (b + 2))
                        v_proj(1, 1 - par, 0)
                        v_proj(1, 1 - par, 1)

            pe.wait_ge(sem("in_ct0b"), 16)
            pe.wait_ge(sem("q_evac1"), 2 * NQ)
            k_proj(1, 0, 0)
            k_proj(1, 0, 1)
            pe.wait_ge(sem("k_evac1"), 2)
            v_proj(1, 0, 0)
            v_proj(1, 0, 1)
            pe.wait_ge(sem("v_evac1"), 1)
            v_proj(1, 0, 2)
            attn1(0, 0, True, False, 16)
            with pe.Fori(0, (NT - 2) // 2) as r:
                for h in range(2):
                    attn1(2 * r + h + 1, 1 - h, False, False, 16 * (r + 2))
            attn1(NT - 1, 1, False, True, None)
            values1(NT - 1, 1, 1)
            values1(NT - 1, 1, 2)
            pe.wait_ge(sem("wo_evac1"), NT - 1)
            wo_proj(1, NT - 1, 1)

            transposes(4, XN, "xn_out", lambda g: QUAD * (g + 1))
            logits(1, 4, E1)

            def ab1(i, par, first):
                off = expert_of(i, E1, W1)
                pe.wait_ge(sem("xt_evac1"), i + 1)
                pe.wait_ge(sem("oh_ready1"), i + 1)
                if not first:
                    pe.wait_ge(sem("b_clip"), i)
                mm(PS[:, 0, :], OHX[0:96, par, :], BR1[0:96, 0:2 * F1], start=True, stop=False)
                for k in range(KD):
                    ins = mm(PS[:, 0, :], wk(512 + par * D + k * P, P), row(off + k * 512, 512), start=False,
                             stop=(k == KD - 1))
                ins.then_inc(sem("ab_done1"), 1)

            def tail1(i, par, xt):
                pe.wait_ge(sem("s_ready1"), i + 1)
                for k in range(2):
                    ins = nc.tensor.transpose(PS[:, 6, k * P:(k + 1) * P], wk(2560 + par * D + k * P, P), IDN)
                ins.then_inc(sem("st_done1"), 1)
                if xt:
                    x_transpose(1, *xt)
                off = expert_of(i, E1, W1)
                pe.wait_ge(sem("st_evac1"), i + 1)
                y_proj(1, off, 2, 1024, BR1, 2 * F1, par)

            pe.wait_ge(sem("slots_ready1"), 1)
            pe.wait_ge(sem("in_e1"), 16 * 2 * E1)
            x_transpose(1, 0, 0, 16)
            ab1(0, 0, True)
            x_transpose(1, 1, 1, 16)
            R = (NB1 - 2) // 2
            with pe.Fori(0, R) as r:
                for h in range(2):
                    i = 2 * r + h + 1
                    ab1(i, 1 - h, False)
                    tail1(i - 1, h, (i + 1, h, 16 * (r + 2)))
            for i in range(2 * R + 1, NB1):
                ab1(i, i % 2, False)
                tail1(i - 1, (i - 1) % 2, (i + 1, (i + 1) % 2, 16 * ((i + 1) // 2 + 1)) if i + 1 < NB1 else None)
            tail1(NB1 - 1, (NB1 - 1) % 2, None)


def constants():
    import numpy as np
    c = np.zeros((P, C_N), np.float32)
    p = np.arange(P)
    c[:, C_ID:C_ID + P] = np.eye(P)
    c[:, C_TRI:C_TRI + P] = p[:, None] < p[None, :]
    c[:, C_ONE:C_ONE + P] = 1.0
    c[:, C_MASK:C_MASK + 8] = np.where(p[:, None] // HD == np.arange(8)[None, :], HD ** -0.5, 0.0)
    c[:, C_PE] = p % 32
    c[:, C_HALF] = -0.5
    c[:, C_THR:C_THR + CNT] = P * np.arange(CNT)
    c[:, C_IOTA:C_IOTA + 72] = np.arange(72)
    c[:, C_REV0:C_REV0 + E0] = E0 - np.arange(E0)
    c[:, C_REV1:C_REV1 + E1] = E1 - np.arange(E1)
    return c


def kernel(**inputs):
    import numpy as np
    import concourse.bacc as bacc
    from concourse.bass_utils import run_bass_kernel_spmd as run

    g = {k: np.asarray(v) for k, v in inputs.items()}
    arrays = {"x": g["x"], "ctx_t": g["ctx_1024"].transpose(0, 2, 1), "consts": constants()}
    arrays["gates"] = np.concatenate([g["g_xattn"], g["g_ffn"]])

    def cols(v):
        return v.reshape(-1, P).T

    arrays["cols"] = np.concatenate([cols(g["L0_xattn_bq"]), cols(g["L0_xattn_bk"]), cols(g["L0_xattn_b1"]),
                                     cols(g["L1_xattn_Wq_b"]), cols(g["L1_xattn_Wk_b"])], axis=1)
    for n in ["wq", "wk", "wv", "wo", "w1", "w2", "bv", "bo", "g1", "be1", "b2", "g2", "be2"]:
        arrays["L0_xattn_" + n] = g["L0_xattn_" + n]
    for n in ["Wq_w", "Wk_w", "Wv_w", "Wo_w"]:
        arrays["L1_xattn_" + n] = g["L1_xattn_" + n].T
    for n in ["Wv_b", "Wo_b"]:
        arrays["L1_xattn_" + n] = g["L1_xattn_" + n]
    for n in ["gate_w", "gate_b", "w1", "w2", "wg", "w3", "b1", "b2", "bg", "b3"]:
        arrays["L0_ffn_" + n] = g["L0_ffn_" + n]
    for n in ["norm_scale", "wg", "bg", "w2", "b2"]:
        arrays["L1_ffn_" + n] = g["L1_ffn_" + n]
    arrays["L1_ffn_w1"] = g["L1_ffn_w1"].reshape(E1, D, F1, 2).transpose(0, 1, 3, 2).reshape(E1, D, 2 * F1)
    arrays["L1_ffn_b1"] = g["L1_ffn_b1"].reshape(E1, F1, 2).transpose(0, 2, 1).reshape(E1, 2 * F1)

    nc = bacc.Bacc("TRN2", target_bir_lowering=False, num_devices=1)
    feed, aps = {}, {}
    for n, v in arrays.items():
        v = np.ascontiguousarray(v)
        feed["in_" + n] = v
        aps[n] = nc.dram_tensor("in_" + n, v.shape, mybir.dt.from_np(v.dtype), kind="ExternalInput").ap()
    out = nc.dram_tensor("out_0", (NT, TQ, D), F32, kind="ExternalOutput").ap()
    build(nc, aps, out)
    r = run(nc, [feed], core_ids=[0])
    return r.results[0]["out_0"]
```

```python
from contextlib import ExitStack

import concourse.bass as bass
from concourse import mybir

ALU = mybir.AluOpType
ACT = mybir.ActivationFunctionType
F32 = mybir.dt.float32
BF16 = mybir.dt.bfloat16
I32 = mybir.dt.int32
U32 = mybir.dt.uint32
AX = mybir.AxisListType

P = 128
NT, TQ, D = 16, 100, 256
NK = 361
KCH = [(0, 121), (121, 121), (242, 119)]
KMAX = 121
H, HD = 16, 16
KD = D // P
DFF = 1024
FD = DFF // P
QUAD = 4
NQ = NT // QUAD
N4 = QUAD * TQ
NTOK = NT * TQ
PADK = 3 * KMAX
EPS = 1e-5

E0, TOP0, F0 = 8, 2, 512
E1, TOP1, F1 = 16, 4, 256
NB0 = (NTOK * TOP0 + E0 * (P - 1)) // P
NB1 = (NTOK * TOP1 + E1 * (P - 1)) // P
W0 = 2 * (KD * F0) + 4 * F0 + 4 * D
W1 = KD * 2 * F1 + 2 * D
CNT = NTOK // P + 1

C_ID, C_TRI, C_ONE, C_MASK, C_PE, C_HALF, C_PART = 0, 128, 256, 384, 392, 393, 394
C_THR, C_IOTA, C_REV0, C_REV1 = 395, 395 + CNT, 395 + CNT + P, 395 + CNT + P + E0
C_N = C_REV1 + 16

A_U, A_UT = 36864, 30720
A_KT, A_CT = A_U - 4 * NK, A_U - 8 * NK
A_QT, A_QB, A_VP, A_W4, A_BC = 27520, 24320, 21248, 19200, 17408
A_PT = 17408 - 1200
A_W1 = A_PT - 4096
A_E = 17408 - 4800
A_XN = E1 * W1
A_NS = A_XN + NT * D
ROUND = 1.5 * 2.0 ** 23
PRE0 = A_W1 // W0
PRE1 = A_E // W1


class Chain:

    def __init__(self, eng, sem):
        self.eng, self.sem, self.base, self.n = eng, sem, 0, 0

    def begin(self, base):
        self.base, self.n = base, 0

    def __call__(self, ins):
        self.n += 1
        ins.then_inc(self.sem, 1)
        self.eng.wait_ge(self.sem, self.base + self.n)


def build(nc, a, out):
    with ExitStack() as ctx:
        def sb(name, shape, dt=F32):
            return ctx.enter_context(nc.sbuf_tensor(name, shape, dt))

        sems = {}

        def sem(name):
            if name not in sems:
                sems[name] = ctx.enter_context(nc.semaphore(name))
            return sems[name]

        PS = ctx.enter_context(nc.psum_tensor("PS", [P, 8, 512], F32))
        AR = sb("arena", [P, E0 * W0])
        X = sb("X", [P, NT, D])
        CST = sb("consts", [P, C_N])
        COLS = sb("bias_cols", [P, 16])
        TG = sb("tanh_gates", [P, 4])
        BR0 = sb("bias_rows0", [P, 3 * F0 + D], BF16)
        BR1 = sb("bias_rows1", [P, 2 * F1 + D], BF16)
        WORK = sb("work", [P, 4096])
        ST6 = sb("bn_stats", [P, NT, 6])
        MV = sb("mean_var", [P, NT, 2])
        RS = sb("rstd", [P, NT])
        NMX = sb("neg_max", [P, H])
        SUM = sb("exp_sum", [P, 4, 2])
        RCP = sb("exp_rcp", [P, 4, 2])
        TMP = sb("tmp_row", [P, 2, D])
        AT = sb("attn_t", [P, 2, KD * TQ])
        MXH = sb("head_max", [P, TQ])
        SMH = sb("head_sum", [P, 3, TQ])
        GW = sb("gate_w", [P, KD, 16 + 8])
        GB = sb("gate_b", [P, 16 + 8])
        GATE = sb("gates", [P, 4, NT])
        SLOT = sb("slots", [P, 4, NT], U32)
        EBI = sb("block_expert", [P, NB1], I32)
        INV = sb("token_of_row", [P, NB1], U32)
        OHB = sb("block_onehot", [P, NB1], BF16)
        OHX = sb("onehot_rows", [P, 4, P], BF16)

        XS = [nc.dram_tensor(f"tokens{l}", (NTOK, D), F32, kind="Internal").ap() for l in range(2)]
        YS = [nc.dram_tensor("pairs_y0", (NB0 * P, D), F32, kind="Internal").ap(),
              nc.dram_tensor("pairs_y1", (NB1 * P, D), F32, kind="Internal").ap()]

        IDN = CST[:, C_ID:C_ID + P]

        def ar(off, *shape):
            n = 1
            for s in shape:
                n *= s
            v = AR[:, off:off + n]
            if len(shape) == 2:
                v = v.rearrange("p (a b) -> p a b", b=shape[1])
            elif len(shape) == 3:
                v = v.rearrange("p (a b c) -> p a b c", b=shape[1], c=shape[2])
            elif len(shape) == 4:
                v = v.rearrange("p (a b c d) -> p a b c d", b=shape[1], c=shape[2], d=shape[3])
            return v

        U = ar(A_U, NT, D)
        UT = ar(A_UT, KD, NTOK)
        QT = ar(A_QT, KD, NTOK)
        CT = [ar(A_CT + 722 * i, KD, NK) for i in range(2)]
        KT = [ar(A_KT + 722 * i, KD, NK) for i in range(2)]
        VP = [ar(A_VP + 1536 * i, 3, 2, D) for i in range(2)]
        QB = [ar(A_QB + 1600 * i, KD, 8, TQ) for i in range(2)]
        PT = [ar(A_PT + 600 * i, 2, 3 * TQ) for i in range(2)]
        HT = ar(A_QT - 0, FD, N4)
        WQ, WK, WV, WO = [ar(A_W4 + 512 * i, KD, D) for i in range(4)]
        W1S, W2S = ar(A_W1, KD, DFF), ar(A_W1 + 2048, FD, D)
        BC = [ar(A_BC + D * i, D) for i in range(7)]
        EH = [ar(A_E + 1600 * i, QUAD, QUAD * TQ) for i in range(3)]
        XN = ar(A_XN, NT, D)
        NSC = ar(A_NS, D)
        ATV = [AT[:, i, :].rearrange("p (k t) -> p k t", k=KD) for i in range(2)]

        def wk(off, n):
            return WORK[:, off:off + n]

        PB = [wk(2 * PADK * i, 2 * PADK).rearrange("p (j k) -> p j k", j=2) for i in range(4)]

        def pair_codes(l, top, nb):
            n = top * NT
            if l == 0:
                o = (wk(0, n * P // 2), wk(n * P // 2, n * nb), wk(n * P // 2 + n * nb, n * nb // 2))
            else:
                o = (AR[:, A_U:A_U + n * P // 2], AR[:, A_UT:A_UT + n * nb], AR[:, A_XN:A_XN + n * nb // 2])
            pr, pb, eq = (v.bitcast(BF16) for v in o)
            return (pr.rearrange("p (n r) -> p n r", r=P), pb.rearrange("p (n c b) -> p n c b", c=2, b=nb),
                    eq.rearrange("p (n b) -> p n b", b=nb))

        block = ctx.enter_context(nc.Block())

        @block.sync
        def _(sp):
            def load(dst, src, name):
                sp.dma_start(dst, src).then_inc(sem(name), 16)

            def wload(dst, src, name, k):
                load(dst, src.rearrange("(k p) n -> p k n", k=k), name)

            def expert0(e, name):
                o = e * W0
                wload(ar(o, KD, F0), a["L0_ffn_w1"][e], name, KD)
                wload(ar(o + 1024, KD, F0), a["L0_ffn_w2"][e], name, KD)
                wload(ar(o + 2048, 4, F0), a["L0_ffn_wg"][e], name, 4)
                wload(ar(o + 4096, 4, D), a["L0_ffn_w3"][e], name, 4)

            def expert1(e, name):
                o = e * W1
                wload(ar(o, KD, 2 * F1), a["L1_ffn_w1"][e], name, KD)
                wload(ar(o + 1024, 2, D), a["L1_ffn_w2"][e], name, 2)

            def ctx_tile(b, par, s):
                load(CT[par], a["ctx_t"][b].rearrange("(k p) s -> p k s", k=KD), s)

            load(X[0:TQ], a["x"].rearrange("b p d -> p b d"), "in_x")
            load(CST[:], a["consts"], "in_const")
            load(COLS[:], a["cols"], "in_cols")
            load(TG[:], a["gates"].partition_broadcast(P), "in_gates")
            for i, n in enumerate(["wq", "wk", "wv", "wo"]):
                wload([WQ, WK, WV, WO][i], a["L0_xattn_" + n], "in_w4", KD)
            ctx_tile(0, 0, "in_ct0")
            ctx_tile(1, 1, "in_ct1")
            for i, n in enumerate(["bv", "bo", "g1", "be1", "b2", "g2", "be2"]):
                load(BC[i], a["L0_xattn_" + n].partition_broadcast(P), "in_bc")
            wload(W1S, a["L0_xattn_w1"], "in_ffw", KD)
            wload(W2S, a["L0_xattn_w2"], "in_ffw", FD)
            wload(GW[:, :, 0:E0], a["L0_ffn_gate_w"], "in_gw", KD)
            wload(GW[:, :, E0:E0 + E1], a["L1_ffn_wg"], "in_gw", KD)
            load(GB[:, 0:E0], a["L0_ffn_gate_b"].partition_broadcast(P), "in_gw")
            load(GB[:, E0:E0 + E1], a["L1_ffn_bg"].partition_broadcast(P), "in_gw")
            for e in range(PRE0):
                expert0(e, "in_e0")
            def tokens_out(l, src, ready, per_quad):
                rows = XS[l].rearrange("(t p) d -> p t d", p=TQ)
                for q in range(NQ):
                    sp.wait_ge(sem(ready), per_quad(q))
                    load(rows[:, q * QUAD:(q + 1) * QUAD, :], src[0:TQ, q * QUAD:(q + 1) * QUAD, :], f"tokens_out{l}")

            def attn_ctx(l):
                with sp.Fori(0, (NT - 2) // 2) as r:
                    for h in range(2):
                        sp.wait_ge(sem(f"v_done{l}"), 6 * r + 3 * (h + 1))
                        ctx_tile(2 * r + h + 2, h, f"in_ct{h}" + ("" if l == 0 else "b"))

            attn_ctx(0)

            sp.wait_ge(sem("bias_zeroed"), 1)
            for q in range(3):
                for i, n in enumerate(["b1", "b2", "bg"]):
                    load(WORK[32 * q:32 * q + E0, i * F0:(i + 1) * F0], a["L0_ffn_" + n], "in_br")
                load(WORK[32 * q:32 * q + E0, 3 * F0:3 * F0 + D], a["L0_ffn_b3"], "in_br")
                load(WORK[32 * q:32 * q + E1, 2048:2048 + 2 * F1], a["L1_ffn_b1"], "in_br")
                load(WORK[32 * q:32 * q + E1, 2048 + 2 * F1:2048 + 2 * F1 + D], a["L1_ffn_b2"], "in_br")

            tokens_out(0, U, "ln_out", lambda q: 2 * NQ + 2 * (q + 1))
            sp.wait_ge(sem("ff_added"), NT)
            expert0(PRE0, "in_e0")
            sp.wait_ge(sem("ln_out"), 4 * NQ)
            for e in range(PRE0 + 1, E0 - 2):
                expert0(e, "in_e0")
            sp.wait_ge(sem("logit_done0"), 1)
            expert0(E0 - 2, "in_e0")
            sp.wait_ge(sem("tokens_out0"), 16 * NQ)
            expert0(E0 - 1, "in_e0")

            def results_out(l, nb):
                def store(i, par):
                    sp.wait_ge(sem(f"y_ready{l}"), i + 1)
                    load(YS[l][bass.ds(i * P, P), :], wk(3584 + par * D, D), f"y_out{l}_{par}")

                with sp.Fori(0, nb // 2) as r:
                    for par in range(2):
                        store(2 * r + par, par)
                if nb % 2:
                    store(nb - 1, 0)

            results_out(0, NB0)

            for i, n in enumerate(["Wq_w", "Wk_w", "Wv_w", "Wo_w"]):
                wload([WQ, WK, WV, WO][i], a["L1_xattn_" + n], "in_w4b", KD)
            load(BC[0], a["L1_xattn_Wv_b"].partition_broadcast(P), "in_w4b")
            load(BC[1], a["L1_xattn_Wo_b"].partition_broadcast(P), "in_w4b")
            ctx_tile(0, 0, "in_ct0b")
            ctx_tile(1, 1, "in_ct1b")
            for e in range(PRE1):
                expert1(e, "in_e1")
            attn_ctx(1)
            sp.wait_ge(sem("wo_added1"), NT)
            load(NSC, a["L1_ffn_norm_scale"].partition_broadcast(P), "in_nsc")
            for e in range(PRE1, E1):
                expert1(e, "in_e1")
            tokens_out(1, XN, "xn_out", lambda q: QUAD * (q + 1))
            results_out(1, NB1)

            sp.wait_ge(sem("x_final"), 1)
            load(out.rearrange("b p d -> p b d"), X[0:TQ], "out_done")
            sp.wait_ge(sem("out_done"), 16)

        @block.gpsimd
        def _(pool):
            for i in range(2):
                nc.gpsimd.memset(VP[i], 0.0).then_inc(sem("vp_zeroed"), 1)
            nc.gpsimd.memset(WORK[0:TQ, 0:8 * PADK], 0.0).then_inc(sem("pb_zeroed"), 1)
            pool.wait_ge(sem("in_const"), 16)

            def rstd(n, t0=0, nt=NT):
                pool.wait_ge(sem("ln_var"), n)
                r = RS[0:TQ, t0:t0 + nt]
                nc.gpsimd.tensor_tensor(r, r, CST[0:TQ, C_HALF:C_HALF + 1].to_broadcast([TQ, nt]),
                                        ALU.pow).then_inc(sem("ln_rstd"), 1)

            def blockdiag(l, b, par, wait):
                if wait:
                    pool.wait_ge(sem(f"s_done{l}"), (8 if l == 0 else 3) * (b - 1))
                for c in range(KD):
                    q = QT[:, c, bass.ds(b * TQ, TQ)].rearrange("p (a t) -> p a t", a=1)
                    m = CST[:, C_MASK:C_MASK + 8].unsqueeze(2)
                    nc.gpsimd.tensor_tensor(QB[par][:, c], q.to_broadcast([P, 8, TQ]),
                                            m.to_broadcast([P, 8, TQ]), ALU.mult).then_inc(sem(f"qb_done{l}"), 1)

            def blocks_in(l, nb):
                def fetch(i, par):
                    nc.gpsimd.indirect_dma_start(
                        out=wk(par * D, D), out_offset=None, in_=XS[l],
                        in_offset=bass.IndirectOffsetOnAxis(ap=INV[:, i:i + 1], axis=0),
                    ).then_inc(sem(f"in_blk{l}_{par}"), 16)

                pool.wait_ge(sem(f"rows_known{l}"), 1)
                pool.wait_ge(sem(f"tokens_out{l}"), 16 * NQ)
                for i in range(nb):
                    if i >= 2:
                        pool.wait_ge(sem(f"xt_done{l}"), i - 1)
                    fetch(i, i % 2)

            def gather(l, top, nb):
                for par in range(2):
                    n = len([i for i in range(nb) if i % 2 == par])
                    pool.wait_ge(sem(f"y_out{l}_{par}"), 16 * n)
                for t in range(NT):
                    for k in range(top):
                        n = t * top + k
                        if n >= 8:
                            pool.wait_ge(sem(f"y_used{l}"), n - 7)
                        nc.gpsimd.indirect_dma_start(
                            out=wk(1024 + (n % 8) * D, D)[0:TQ], out_offset=None, in_=YS[l],
                            in_offset=bass.IndirectOffsetOnAxis(ap=SLOT[0:TQ, k, t:t + 1], axis=0),
                        ).then_inc(sem(f"y_back{l}_{n % 8}"), 16)

            rstd(1)
            pool.wait_ge(sem("q_evac0"), 2 * NQ)
            blockdiag(0, 0, 0, False)
            blockdiag(0, 1, 1, False)
            with pool.Fori(0, (NT - 2) // 2) as r:
                for h in range(2):
                    blockdiag(0, 2 * r + h + 2, h, True)
            rstd(2)
            pool.wait_ge(sem("wo_added0"), NT)
            nc.gpsimd.memset(WORK[0:96, 0:2048 + 2 * F1 + D], 0.0).then_inc(sem("bias_zeroed"), 1)
            for q in range(NQ):
                rstd(3 + 2 * q, q * QUAD, QUAD)
                rstd(4 + 2 * q, q * QUAD, QUAD)
            blocks_in(0, NB0)
            gather(0, TOP0, NB0)
            rstd(11)

            pool.wait_ge(sem("e0_all_done"), 1)
            for i in range(2):
                nc.gpsimd.memset(VP[i], 0.0).then_inc(sem("vp_zeroed"), 1)
            pool.wait_ge(sem("q_evac1"), 2 * NQ)

            def head_weights(b, par, wait, more):
                for ch, (k0, kn) in enumerate(KCH):
                    pool.wait_ge(sem("rcp_done1"), 3 * b + ch + 1)
                    e = EH[ch][0:kn].rearrange("p a (h t) -> p (a h) t", h=QUAD)
                    r = SMH[0:kn, ch, :].rearrange("p (a t) -> p a t", a=1)
                    nc.gpsimd.tensor_tensor(e, e, r.to_broadcast([kn, H, TQ]), ALU.mult).then_inc(sem("p_done1"), 1)
                    if ch == 1 and more:
                        blockdiag(1, b + 2, par, wait)

            blockdiag(1, 0, 0, False)
            blockdiag(1, 1, 1, False)
            with pool.Fori(0, (NT - 2) // 2) as r:
                for h in range(2):
                    head_weights(2 * r + h, h, True, True)
            head_weights(NT - 2, 0, False, False)
            head_weights(NT - 1, 1, False, False)
            rstd(12)
            rstd(13)
            blocks_in(1, NB1)
            gather(1, TOP1, NB1)

        @block.scalar
        def _(act):
            act.wait_ge(sem("in_gates"), 16)
            nc.scalar.activation(TG[:], TG[:], ACT.Tanh).then_inc(sem("tg_ready"), 1)
            act.wait_ge(sem("in_cols"), 16)

            def t_evac(n, g, c, bank):
                act.wait_ge(sem("tr_done"), 2 * NQ * n + KD * g + c + 1)
                nc.scalar.activation(UT[:, c, g * N4:(g + 1) * N4], PS[:, bank, 0:N4],
                                     ACT.Identity).then_inc(sem("tr_evac"), 1)

            def transposes(n):
                for g in range(NQ):
                    for c in range(KD):
                        t_evac(n, g, c, (KD * g + c) % 4)

            def k_evac(l, b, par, m):
                act.wait_ge(sem(f"k_done{l}"), 2 * b + m + 1)
                nc.scalar.activation(KT[par][:, m, :], PS[:, 7 if l == 0 else 6 + m, 0:NK], ACT.Identity,
                                     bias=COLS[:, (2 if l == 0 else 14) + m:(3 if l == 0 else 15) + m]
                                     ).then_inc(sem(f"k_evac{l}"), 1)

            def o_evac(l, b, par):
                per = 8 if l == 0 else 3
                act.wait_ge(sem(f"pv_done{l}"), per * (b + 1))
                src = PS[:, 6, 0:KD * TQ] if l == 0 else PS[:, 4:6, 0:TQ]
                dst = AT[:, par, :] if l == 0 else ATV[par]
                nc.scalar.activation(dst, src, ACT.Identity).then_inc(sem(f"o_evac{l}"), 1)

            transposes(0)

            def pt_evac(b, g, wait):
                n = 8 * b + g
                act.wait_ge(sem("t_done"), n + 1)
                if wait:
                    act.wait_ge(sem("pv_done0"), n - 1)
                nc.scalar.activation(PT[g % 2][0:KMAX], PS[0:KMAX, 4:6, 0:3 * TQ],
                                     ACT.Identity).then_inc(sem("pt_evac"), 1)

            def attn0(b, par, first, last):
                for g in range(8):
                    if g == 3 and not first:
                        o_evac(0, b - 1, 1 - par)
                    if g >= 2:
                        pt_evac(b, g - 2, not first or g >= 4)
                    elif not first:
                        pt_evac(b - 1, 6 + g, True)
                    if g in (4, 5) and not last:
                        k_evac(0, b + 1, 1 - par, g - 4)
                    n = 8 * b + g
                    act.wait_ge(sem("mx_done"), n + 1)
                    if not (first and g < 4):
                        act.wait_ge(sem("t_done"), n - 3)
                    for j in range(2):
                        ins = nc.scalar.activation(PB[g % 4][0:TQ, j, 0:NK], PS[0:TQ, 2 * (g % 2) + j, 0:NK], ACT.Exp,
                                                   bias=NMX[0:TQ, 2 * g + j:2 * g + j + 1],
                                                   accum_out=SUM[0:TQ, g % 4, j:j + 1])
                    ins.then_inc(sem("exp_done"), 1)

            act.wait_ge(sem("pb_zeroed"), 1)
            k_evac(0, 0, 0, 0)
            k_evac(0, 0, 0, 1)
            attn0(0, 0, True, False)
            with act.Fori(0, (NT - 2) // 2) as r:
                for h in range(2):
                    attn0(2 * r + h + 1, 1 - h, False, False)
            attn0(NT - 1, 1, False, True)
            pt_evac(NT - 1, 6, True)
            pt_evac(NT - 1, 7, True)
            o_evac(0, NT - 1, 1)

            for q in range(NQ):
                for c in range(KD):
                    t_evac(1, q, c, 6 + c)
                for f in range(FD):
                    act.wait_ge(sem("h_done"), FD * q + f + 1)
                    if q and f == 0:
                        act.wait_ge(sem("f_done"), QUAD * q)
                    nc.scalar.activation(HT[:, f, :], PS[:, f % 4, 0:N4], ACT.Relu,
                                         bias=COLS[:, 4 + f:5 + f]).then_inc(sem("h_evac"), 1)
            transposes(2)

            def gate_exp(l, top):
                act.wait_ge(sem(f"top_ready{l}"), 1)
                nc.scalar.activation(GATE[0:TQ, 0:top], GATE[0:TQ, 0:top], ACT.Exp).then_inc(sem(f"gate_exp{l}"), 1)

            gate_exp(0, TOP0)

            def partition_code(l, top, nb):
                act.wait_ge(sem(f"block_code{l}"), 1)
                _, pb, eq = pair_codes(l, top, nb)
                nc.scalar.activation(pb[0:TQ, :, 0, :], eq[0:TQ], ACT.Identity,
                                     scale=CST[0:TQ, C_PART:C_PART + 1]).then_inc(sem(f"part_code{l}"), 1)

            partition_code(0, TOP0, NB0)

            za, zt, s = wk(1024, 512), wk(2048, 512), wk(2560, 512)

            def xt_evac(l, i, par):
                act.wait_ge(sem(f"xt_done{l}"), i + 1)
                nc.scalar.activation(wk(512 + par * D, D), PS[:, 4, 0:D], ACT.Identity).then_inc(sem(f"xt_evac{l}"), 1)

            def y_evac(l, i, par, wait):
                act.wait_ge(sem(f"y_done{l}"), i + 1)
                if wait is not None:
                    act.wait_ge(sem(f"y_out{l}_{par}"), wait)
                nc.scalar.activation(wk(3584 + par * D, D), PS[:, 3, 0:D], ACT.Identity).then_inc(sem(f"y_ready{l}"), 1)

            def blocks0(i, par, first, last, yw):
                act.wait_ge(sem("a_done"), i + 1)
                nc.scalar.activation(za, PS[:, 0, :], ACT.Identity).then_inc(sem("a_copied"), 1)
                if not first:
                    act.wait_ge(sem("st_done"), i)
                    nc.scalar.activation(wk(3072, 512), PS[:, 6, :], ACT.Identity).then_inc(sem("st_evac"), 1)
                if not last:
                    xt_evac(0, i + 1, 1 - par)
                act.wait_ge(sem("zt_done"), i + 1)
                nc.scalar.activation(zt, PS[:, 5, :], ACT.Identity).then_inc(sem("zt_evac"), 1)
                if not first:
                    y_evac(0, i - 1, 1 - par, yw)
                act.wait_ge(sem("g_done"), i + 1)
                nc.scalar.activation(s, PS[:, 2, :], ACT.Silu).then_inc(sem("s_ready"), 1)

            xt_evac(0, 0, 0)
            blocks0(0, 0, True, False, None)
            blocks0(1, 1, False, False, None)
            blocks0(2, 0, False, False, None)
            R0 = (NB0 - 4) // 2
            with act.Fori(0, R0) as r:
                for h in range(2):
                    blocks0(2 * r + 3 + h, 1 - h, False, False, 16 * (r + 1))
            for i in range(2 * R0 + 3, NB0):
                blocks0(i, i % 2, False, i == NB0 - 1, 16 * ((i - 1) // 2))
            act.wait_ge(sem("st_done"), NB0)
            nc.scalar.activation(wk(3072, 512), PS[:, 6, :], ACT.Identity).then_inc(sem("st_evac"), 1)
            y_evac(0, NB0 - 1, (NB0 - 1) % 2, 16 * ((NB0 - 1) // 2))

            transposes(3)

            def attn1(b, par, first, last):
                for ch, (k0, kn) in enumerate(KCH):
                    if ch == 2 and not first:
                        o_evac(1, b - 1, 1 - par)
                    act.wait_ge(sem("sub_done1"), 12 * b + 4 * ch + 4)
                    nc.scalar.activation(EH[ch][0:kn], EH[ch][0:kn], ACT.Exp).then_inc(sem("exp_done1"), 1)
                    if ch == 0 and not last:
                        k_evac(1, b + 1, 1 - par, 0)
                        k_evac(1, b + 1, 1 - par, 1)

            k_evac(1, 0, 0, 0)
            k_evac(1, 0, 0, 1)
            attn1(0, 0, True, False)
            with act.Fori(0, (NT - 2) // 2) as r:
                for h in range(2):
                    attn1(2 * r + h + 1, 1 - h, False, False)
            attn1(NT - 1, 1, False, True)
            o_evac(1, NT - 1, 1)

            transposes(4)
            gate_exp(1, TOP1)
            partition_code(1, TOP1, NB1)

            def blocks1(i, par, xt, st, yw):
                if xt:
                    xt_evac(1, i + 1, 1 - par)
                act.wait_ge(sem("a_min"), i + 1)
                nc.scalar.activation(wk(1280, D), wk(1024, D), ACT.Sigmoid, scale=1.702).then_inc(sem("sig_ready"), 1)
                if yw is not None:
                    y_evac(1, i - 2, par, yw)
                if st:
                    act.wait_ge(sem("st_done1"), i)
                    nc.scalar.activation(wk(3072, D), PS[:, 6, 0:D], ACT.Identity).then_inc(sem("st_evac1"), 1)

            xt_evac(1, 0, 0)
            blocks1(0, 0, True, False, None)
            blocks1(1, 1, True, True, None)
            for i in (2, 3):
                blocks1(i, i % 2, True, True, 0)
            R1 = (NB1 - 5) // 2
            with act.Fori(0, R1) as r:
                for h in range(2):
                    blocks1(2 * r + 4 + h, h, True, True, 16 * (r + 1))
            for i in range(2 * R1 + 4, NB1):
                blocks1(i, i % 2, i + 1 < NB1, True, 16 * ((i - 2) // 2))
            y_evac(1, NB1 - 2, NB1 % 2, 16 * ((NB1 - 2) // 2))
            act.wait_ge(sem("st_done1"), NB1)
            nc.scalar.activation(wk(3072, D), PS[:, 6, 0:D], ACT.Identity).then_inc(sem("st_evac1"), 1)
            y_evac(1, NB1 - 1, (NB1 - 1) % 2, 16 * ((NB1 - 1) // 2))

        @block.vector
        def _(dve):
            link = Chain(dve, sem("v_chain"))

            dve.wait_ge(sem("in_const"), 16)
            dve.wait_ge(sem("in_x"), 16)

            def stats(t, src):
                nc.vector.bn_stats(ST6[0:TQ, t, :], src[0:TQ, t, :]).then_inc(sem("bn_done"), 1)

            def variance(t0, nt):
                st = ST6[0:TQ, t0:t0 + nt]
                me, mo, m2e, m2o = (st[:, :, c] for c in (1, 4, 2, 5))
                mean, dif, rs = MV[0:TQ, t0:t0 + nt, 0], MV[0:TQ, t0:t0 + nt, 1], RS[0:TQ, t0:t0 + nt]
                link(nc.vector.tensor_tensor(mean, me, mo, ALU.add))
                link(nc.vector.tensor_scalar(mean, mean, 0.5, None, ALU.mult))
                link(nc.vector.tensor_tensor(dif, me, mo, ALU.subtract))
                link(nc.vector.scalar_tensor_tensor(out=dif, in0=dif, scalar=0.25, in1=dif, op0=ALU.mult, op1=ALU.mult))
                link(nc.vector.tensor_tensor(rs, m2e, m2o, ALU.add))
                link(nc.vector.scalar_tensor_tensor(out=dif, in0=rs, scalar=1.0 / D, in1=dif, op0=ALU.mult, op1=ALU.add))
                nc.vector.tensor_scalar(rs, dif, EPS, None, ALU.add).then_inc(sem("ln_var"), 1)

            def apply(q, src, gamma=None, beta=None):
                for t in range(q * QUAD, (q + 1) * QUAD):
                    ins = nc.vector.tensor_scalar(U[0:TQ, t, :], src[0:TQ, t, :], MV[0:TQ, t, 0:1],
                                                  RS[0:TQ, t:t + 1], ALU.subtract, ALU.mult)
                if gamma is not None:
                    link(ins)
                    v = U[0:TQ, q * QUAD:(q + 1) * QUAD, :]
                    link(nc.vector.tensor_tensor(v, v, gamma[0:TQ].unsqueeze(1).to_broadcast([TQ, QUAD, D]), ALU.mult))
                    ins = nc.vector.tensor_tensor(v, v, beta[0:TQ].unsqueeze(1).to_broadcast([TQ, QUAD, D]), ALU.add)
                ins.then_inc(sem("ln_out"), 1)

            def norm(bn, rstd, src, gamma=None, beta=None):
                dve.wait_ge(sem("bn_done"), bn)
                variance(0, NT)
                dve.wait_ge(sem("ln_rstd"), rstd)
                for q in range(NQ):
                    apply(q, src, gamma, beta)

            def q_evac(l):
                for i in range(2 * NQ):
                    g, m = i // 2, i % 2
                    dve.wait_ge(sem(f"q_done{l}"), i + 1)
                    c = (0 if l == 0 else 12) + m
                    nc.vector.tensor_scalar(QT[:, m, g * N4:(g + 1) * N4], PS[:, 4 + i % 4, 0:N4],
                                            COLS[:, c:c + 1], None, ALU.add).then_inc(sem(f"q_evac{l}"), 1)

            def v_evac(l, b, par, c):
                kn = KCH[c][1]
                dve.wait_ge(sem(f"v_done{l}"), 3 * b + c + 1)
                bank = 7 if l == 0 else 6 + c % 2
                ps = PS[0:kn, bank, 0:D].rearrange("p (a j d) -> p a j d", j=2, d=HD)
                bv = BC[0][0:kn].rearrange("p (a j d) -> p a j d", j=2, d=HD)
                for j in range(2):
                    v = VP[par][0:kn, c, j, :].rearrange("p (a j d) -> p a j d", j=2, d=HD)
                    ins = nc.vector.tensor_tensor(v[:, :, j, :], ps[:, :, j, :], bv[:, :, j, :], ALU.add)
                ins.then_inc(sem(f"v_evac{l}"), 1)

            with dve.Fori(0, NT) as t:
                stats(t, X)
            norm(NT, 1, X)
            dve.wait_ge(sem("in_cols"), 16)
            q_evac(0)

            ch0 = Chain(dve, sem("attn_chain0"))

            def p_norm(b, g, ch):
                dve.wait_ge(sem("exp_done"), 8 * b + g + 1)
                ch(nc.vector.reciprocal(RCP[0:TQ, g % 4, :], SUM[0:TQ, g % 4, :]))
                for j in range(2):
                    v = PB[g % 4][0:TQ, j, 0:NK]
                    ins = nc.vector.tensor_scalar(v, v, RCP[0:TQ, g % 4, j:j + 1], None, ALU.mult)
                ins.then_inc(sem("p_done"), 1)

            def wo_add0(b, par):
                dve.wait_ge(sem("wo_done0"), b + 1)
                nc.vector.tensor_tensor(TMP[0:TQ, par, :], PS[0:TQ, 7, 0:D], BC[1][0:TQ], ALU.add).then_inc(
                    sem("wo_evac0"), 1)
                dve.wait_ge(sem("wo_evac0"), b + 1)
                u = U[0:TQ, b, :]
                nc.vector.tensor_tensor(u, u, TMP[0:TQ, par, :], ALU.add).then_inc(sem("wo_added0"), 1)
                dve.wait_ge(sem("wo_added0"), b + 1)
                stats(b, U)

            def attn0(b, par, first, last, ch):
                for g in range(8):
                    n = 8 * b + g
                    dve.wait_ge(sem("s_done0"), n + 1)
                    nc.vector.tensor_reduce(NMX[0:TQ, 2 * g:2 * g + 2], PS[0:TQ, 2 * (g % 2):2 * (g % 2) + 2, 0:NK],
                                            axis=AX.X, op=ALU.max, negate=True).then_inc(sem("mx_done"), 1)
                    if g > 0 or not first:
                        p_norm(*((b, g - 1) if g else (b - 1, 7)), ch)
                    if g == 0 and not first:
                        v_evac(0, b, par, 2)
                    if g == 3 and not first:
                        wo_add0(b - 1, 1 - par)
                    if g in (6, 7) and not last:
                        v_evac(0, b + 1, 1 - par, g - 6)

            dve.wait_ge(sem("in_bc"), 16 * 7)
            dve.wait_ge(sem("vp_zeroed"), 2)
            for c in range(3):
                v_evac(0, 0, 0, c)
            attn0(0, 0, True, False, ch0)
            with dve.Fori(0, (NT - 2) // 2) as r:
                ch0.begin(r * 16 + 7)
                for h in range(2):
                    attn0(2 * r + h + 1, 1 - h, False, False, ch0)
                assert ch0.n == 16
            ch0.begin(7 + 16 * ((NT - 2) // 2))
            attn0(NT - 1, 1, False, True, ch0)
            p_norm(NT - 1, 7, ch0)
            wo_add0(NT - 1, 1)

            norm(2 * NT, 2, U, BC[2], BC[3])

            dve.wait_ge(sem("in_br"), 16 * 18)
            for br, o, n in ((BR0, 0, 3 * F0 + D), (BR1, 2048, 2 * F1 + D)):
                w = wk(o, n)
                link(nc.vector.tensor_copy(br[0:96], w[0:96]))
                link(nc.vector.tensor_tensor(w[0:96], w[0:96], br[0:96], ALU.subtract))
                link(nc.vector.tensor_copy(br[32:64], w[32:64]))
                link(nc.vector.tensor_copy(br[64:96], w[64:96]))
                link(nc.vector.tensor_tensor(w[64:96], w[64:96], br[64:96], ALU.subtract))
                link(nc.vector.tensor_copy(br[64:96], w[64:96]))

            dve.wait_ge(sem("tg_ready"), 1)
            for q in range(NQ):
                for t in range(q * QUAD, (q + 1) * QUAD):
                    dve.wait_ge(sem("f_done"), t + 1)
                    nc.vector.tensor_tensor(TMP[0:TQ, t % 2, :], PS[0:TQ, 4 + t % 2, 0:D], BC[4][0:TQ],
                                            ALU.add).then_inc(sem("f_evac"), 1)
                    dve.wait_ge(sem("f_evac"), t + 1)
                    u = U[0:TQ, t, :]
                    nc.vector.tensor_tensor(u, u, TMP[0:TQ, t % 2, :], ALU.add).then_inc(sem("ff_added"), 1)
                    dve.wait_ge(sem("ff_added"), t + 1)
                    stats(t, U)
                dve.wait_ge(sem("bn_done"), 2 * NT + 2 * QUAD * q + QUAD)
                variance(q * QUAD, QUAD)
                dve.wait_ge(sem("ln_rstd"), 3 + 2 * q)
                apply(q, U, BC[5], BC[6])
                dve.wait_ge(sem("ln_out"), 2 * NQ + 2 * q + 1)
                x, u = (v[0:TQ, q * QUAD:(q + 1) * QUAD, :] for v in (X, U))
                link(nc.vector.scalar_tensor_tensor(out=x, in0=u, scalar=TG[0:TQ, 0:1], in1=x, op0=ALU.mult, op1=ALU.add))
                for t in range(q * QUAD, (q + 1) * QUAD):
                    stats(t, X)
                dve.wait_ge(sem("bn_done"), 2 * NT + 2 * QUAD * (q + 1))
                variance(q * QUAD, QUAD)
                dve.wait_ge(sem("ln_rstd"), 4 + 2 * q)
                apply(q, X)
            dve.wait_ge(sem("ln_out"), 4 * NQ)

            def route(l, top, E, nb, stride, logit_ps):
                NE = NT * E
                c0 = 0 if l == 0 else E0
                L, SC, M, A, B, C, POS = (wk(o * 256, NE) for o in range(7))
                OH = [wk((7 + k) * 256, NE) for k in range(top)]
                v3 = lambda t, n=TQ: t[0:n].rearrange("p (t e) -> p t e", e=E)
                dve.wait_ge(sem("in_gw"), 16 * 4)
                dve.wait_ge(sem(f"logit_done{l}"), 1)
                link(nc.vector.tensor_tensor(v3(L), v3(logit_ps), GB[0:TQ, c0:c0 + E].unsqueeze(1).to_broadcast([TQ, NT, E]), ALU.add))
                rev = CST[0:TQ, (C_REV0 if l == 0 else C_REV1):(C_REV0 if l == 0 else C_REV1) + E].unsqueeze(1).to_broadcast([TQ, NT, E])
                for k in range(top):
                    link(nc.vector.tensor_reduce(GATE[0:TQ, k, :], v3(L), axis=AX.X, op=ALU.max))
                    link(nc.vector.tensor_tensor(v3(SC), v3(L), GATE[0:TQ, k, :].unsqueeze(2).to_broadcast([TQ, NT, E]), ALU.is_equal))
                    link(nc.vector.tensor_tensor(v3(SC), v3(SC), rev, ALU.mult))
                    link(nc.vector.tensor_reduce(RS[0:TQ], v3(SC), axis=AX.X, op=ALU.max))
                    link(nc.vector.tensor_tensor(v3(OH[k]), v3(SC), RS[0:TQ].unsqueeze(2).to_broadcast([TQ, NT, E]), ALU.is_equal))
                    if k + 1 < top:
                        link(nc.vector.scalar_tensor_tensor(out=L[0:TQ], in0=OH[k][0:TQ], scalar=-3.0e38, in1=L[0:TQ],
                                                            op0=ALU.mult, op1=ALU.add))
                    if k:
                        src = OH[0] if k == 1 else M
                        ins = nc.vector.tensor_tensor(M[0:TQ], src[0:TQ], OH[k][0:TQ], ALU.add)
                        if k == top - 1:
                            ins.then_inc(sem(f"mask_ready{l}"), 1)
                            dve.wait_ge(sem(f"mask_ready{l}"), 1)
                        else:
                            link(ins)
                link(nc.vector.tensor_copy(RS[0:TQ], GATE[0:TQ, 0, :]))
                nc.vector.tensor_tensor(GATE[0:TQ, 0:top], GATE[0:TQ, 0:top], RS[0:TQ].unsqueeze(1).to_broadcast([TQ, top, NT]),
                                        ALU.subtract).then_inc(sem(f"top_ready{l}"), 1)
                dve.wait_ge(sem(f"gate_exp{l}"), 1)
                link(nc.vector.tensor_reduce(RS[0:TQ], GATE[0:TQ, 0:top].rearrange("p k t -> p t k"), axis=AX.X, op=ALU.add))
                link(nc.vector.reciprocal(RS[0:TQ], RS[0:TQ]))
                link(nc.vector.tensor_scalar(RS[0:TQ], RS[0:TQ], TG[0:TQ, 2 + l:3 + l], None, ALU.mult))
                link(nc.vector.tensor_tensor(GATE[0:TQ, 0:top], GATE[0:TQ, 0:top], RS[0:TQ].unsqueeze(1).to_broadcast([TQ, top, NT]), ALU.mult))
                dve.wait_ge(sem(f"rank_done{l}"), 1)
                link(nc.vector.tensor_copy(C, PS[:, 1, 0:NE]))
                src, dst = C, A
                s = 1
                while s < NT:
                    link(nc.vector.tensor_tensor(dst[:, s * E:NE], src[:, s * E:NE], src[:, 0:NE - s * E], ALU.add))
                    link(nc.vector.tensor_copy(dst[:, 0:s * E], src[:, 0:s * E]))
                    src, dst = dst, (B if dst is A else A)
                    s *= 2
                cnt = src[:, NE - E:NE]
                link(nc.vector.tensor_tensor(POS, src, C, ALU.subtract))
                link(nc.vector.tensor_tensor(POS[0:TQ], POS[0:TQ], PS[0:TQ, 0, 0:NE], ALU.add))
                big = wk(11 * 256, 1040)
                cmp = big[:, 0:E * CNT].rearrange("p (e c) -> p e c", c=CNT)
                link(nc.vector.tensor_tensor(cmp, cnt.unsqueeze(2).to_broadcast([P, E, CNT]),
                                             CST[:, C_THR:C_THR + CNT].unsqueeze(1).to_broadcast([P, E, CNT]), ALU.is_gt))
                NBK, S1, S2 = (SC[:, o * E:(o + 1) * E] for o in range(3))
                link(nc.vector.tensor_reduce(NBK, cmp, axis=AX.X, op=ALU.add))
                src, dst, s = NBK, S1, 1
                while s < E:
                    link(nc.vector.tensor_tensor(dst[:, s:E], src[:, s:E], src[:, 0:E - s], ALU.add))
                    link(nc.vector.tensor_copy(dst[:, 0:s], src[:, 0:s]))
                    src, dst = dst, (S2 if dst is S1 else S1)
                    s *= 2
                link(nc.vector.tensor_tensor(dst, src, NBK, ALU.subtract))
                link(nc.vector.tensor_scalar(dst, dst, float(P), None, ALU.mult))
                link(nc.vector.tensor_tensor(v3(POS), v3(POS), dst[0:TQ].unsqueeze(1).to_broadcast([TQ, NT, E]), ALU.add))
                NP = top * NT
                slot, blk, pos = (wk(3872 + o * 64, NP)[0:TQ] for o in range(3))
                for k in range(top):
                    link(nc.vector.tensor_tensor(OH[k][0:TQ], OH[k][0:TQ], POS[0:TQ], ALU.mult))
                    link(nc.vector.tensor_reduce(slot[:, k * NT:(k + 1) * NT], v3(OH[k]), axis=AX.X, op=ALU.add))
                link(nc.vector.tensor_copy(SLOT[0:TQ, 0:top, :], slot.rearrange("p (k t) -> p k t", t=NT)))
                be = big[:, 0:nb * E].rearrange("p (i e) -> p i e", e=E)
                link(nc.vector.tensor_tensor(be, src.unsqueeze(1).to_broadcast([P, nb, E]),
                                             CST[:, C_IOTA:C_IOTA + nb].unsqueeze(2).to_broadcast([P, nb, E]), ALU.is_le))
                ebf = M[:, 0:nb]
                link(nc.vector.tensor_reduce(ebf, be, axis=AX.X, op=ALU.add))
                link(nc.vector.tensor_scalar(ebf, ebf, float(E - 1), None, ALU.min))
                link(nc.vector.tensor_scalar(OHB[:, 0:nb], ebf, CST[:, C_PE:C_PE + 1], None, ALU.is_equal))
                link(nc.vector.tensor_scalar(EBI[:, 0:nb], ebf, float(stride), None, ALU.mult))
                nc.vector.tensor_copy(L[0:TQ, 0:1], RS[0:TQ, 0:1]).then_inc(sem(f"slots_ready{l}"), 1)

                link(nc.vector.tensor_scalar(blk, slot, 1.0 / P, 0.5 / P - 0.5, ALU.mult, ALU.add))
                link(nc.vector.tensor_scalar(blk, blk, ROUND, None, ALU.add))
                link(nc.vector.tensor_scalar(blk, blk, -ROUND, None, ALU.add))
                link(nc.vector.scalar_tensor_tensor(out=pos, in0=blk, scalar=-float(P), in1=slot, op0=ALU.mult, op1=ALU.add))
                if l:
                    dve.wait_ge(sem("tokens_out1"), 16 * NQ)
                pr, pb, eq = pair_codes(l, top, nb)
                nc.vector.tensor_tensor(eq[0:TQ], blk.unsqueeze(2).to_broadcast([TQ, NP, nb]),
                                        CST[0:TQ, C_IOTA:C_IOTA + nb].unsqueeze(1).to_broadcast([TQ, NP, nb]),
                                        ALU.is_equal).then_inc(sem(f"block_code{l}"), 1)
                dve.wait_ge(sem(f"block_code{l}"), 1)
                for k in range(top):
                    g = slice(k * NT, (k + 1) * NT)
                    nc.vector.tensor_tensor(pb[0:TQ, g, 1, :], eq[0:TQ, g, :],
                                            CST[0:TQ, C_IOTA:C_IOTA + NT].unsqueeze(2).to_broadcast([TQ, NT, nb]), ALU.mult)
                    nc.vector.tensor_tensor(pr[0:TQ, g, :], pos[:, g].unsqueeze(2).to_broadcast([TQ, NT, P]),
                                            CST[0:TQ, C_IOTA:C_IOTA + P].unsqueeze(1).to_broadcast([TQ, NT, P]),
                                            ALU.is_equal).then_inc(sem(f"row_code{l}"), 1)
                dve.wait_ge(sem(f"tokens_found{l}"), 1)
                idf = wk(3872, nb)
                link(nc.vector.tensor_scalar(idf, PS[:, 5, nb:2 * nb], float(TQ), None, ALU.mult))
                link(nc.vector.tensor_tensor(idf, idf, PS[:, 5, 0:nb], ALU.add))
                nc.vector.tensor_copy(INV[:, 0:nb], idf).then_inc(sem(f"rows_known{l}"), 1)

            route(0, TOP0, E0, NB0, W0, PS[:, 6, 0:NT * E0])

            def onehot(l, i, slot, done):
                if done is not None:
                    dve.wait_ge(sem(f"y_done{l}"), done)
                nc.vector.tensor_copy(OHX[0:96, slot, :], OHB[0:96, bass.ds(i, 1)].to_broadcast([96, P])).then_inc(
                    sem(f"oh_ready{l}"), 1)

            def blocks0(i, par, more):
                dve.wait_ge(sem("ab_done0"), i + 1)
                dve.wait_ge(sem("a_copied"), i + 1)
                nc.vector.tensor_tensor(wk(1536, 512), wk(1024, 512), PS[:, 1, :], ALU.mult).then_inc(sem("z_ready"), 1)
                if more:
                    onehot(0, i + 1, 1 - par, i)

            onehot(0, 0, 0, None)
            onehot(0, 1, 1, None)
            blocks0(0, 0, False)
            R = (NB0 - 2) // 2
            with dve.Fori(0, R) as r:
                for h in range(2):
                    blocks0(2 * r + h + 1, 1 - h, True)
            for i in range(2 * R + 1, NB0):
                blocks0(i, i % 2, i + 1 < NB0)

            def combine(l, top):
                for t in range(NT):
                    for k in range(top):
                        n = t * top + k
                        dve.wait_ge(sem(f"y_back{l}_{n % 8}"), 16 * (n // 8 + 1))
                        nc.vector.scalar_tensor_tensor(out=X[0:TQ, t, :], in0=wk(1024 + (n % 8) * D, D)[0:TQ],
                                                       scalar=GATE[0:TQ, k, t:t + 1], in1=X[0:TQ, t, :],
                                                       op0=ALU.mult, op1=ALU.add).then_inc(sem(f"y_used{l}"), 1)
                        dve.wait_ge(sem(f"y_used{l}"), n + 1)
                    if l == 0:
                        stats(t, X)

            combine(0, TOP0)
            nc.vector.memset(TMP[:, 0, 0:1], 0.0).then_inc(sem("e0_all_done"), 1)

            norm(5 * NT, 11, X)
            q_evac(1)
            ch1 = Chain(dve, sem("attn_chain1"))

            def head_sum(b, c):
                kn = KCH[c][1]
                dve.wait_ge(sem("exp_done1"), 3 * b + c + 1)
                e = EH[c][0:kn].rearrange("p a (h t) -> p t (a h)", h=QUAD)
                nc.vector.tensor_reduce(SMH[0:kn, c, :], e, axis=AX.X, op=ALU.add).then_inc(sem("hsum_done1"), 1)
                dve.wait_ge(sem("hsum_done1"), 3 * b + c + 1)
                nc.vector.reciprocal(SMH[0:kn, c, :], SMH[0:kn, c, :]).then_inc(sem("rcp_done1"), 1)

            def wo_add1(b, par):
                dve.wait_ge(sem("wo_done1"), b + 1)
                nc.vector.tensor_tensor(TMP[0:TQ, par, :], PS[0:TQ, 7, 0:D], BC[1][0:TQ], ALU.add).then_inc(
                    sem("wo_evac1"), 1)
                dve.wait_ge(sem("wo_evac1"), b + 1)
                x = X[0:TQ, b, :]
                nc.vector.scalar_tensor_tensor(out=x, in0=TMP[0:TQ, par, :], scalar=TG[0:TQ, 1:2], in1=x,
                                               op0=ALU.mult, op1=ALU.add).then_inc(sem("wo_added1"), 1)
                dve.wait_ge(sem("wo_added1"), b + 1)
                stats(b, X)

            def attn1(b, par, first, last):
                for c, (k0, kn) in enumerate(KCH):
                    n = 3 * b + c
                    dve.wait_ge(sem("s_done1"), n + 1)
                    s4 = PS[0:kn, 0:4, 0:N4].rearrange("p a (h t) -> p a h t", h=QUAD)
                    nc.vector.tensor_reduce(MXH[0:kn], s4.rearrange("p a h t -> p t a h"), axis=AX.XY,
                                            op=ALU.max).then_inc(sem("hmax_done1"), 1)
                    dve.wait_ge(sem("hmax_done1"), n + 1)
                    if not first:
                        dve.wait_ge(sem("pv_done1"), 3 * (b - 1) + c + 1)
                    for bk in range(4):
                        ins = nc.vector.tensor_tensor(EH[c][0:kn, bk, :].rearrange("p (h t) -> p h t", h=QUAD), s4[:, bk],
                                                      MXH[0:kn].unsqueeze(1).to_broadcast([kn, QUAD, TQ]), ALU.subtract)
                        ins.then_inc(sem("sub_done1"), 1)
                    if c or not first:
                        head_sum(*((b, c - 1) if c else (b - 1, 2)))
                    if c == 1 and not last:
                        v_evac(1, b + 1, 1 - par, 0)
                        v_evac(1, b + 1, 1 - par, 1)
                    if c == 2 and not first:
                        wo_add1(b - 1, 1 - par)
                    if c == 2 and not last:
                        v_evac(1, b + 1, 1 - par, 2)

            dve.wait_ge(sem("in_w4b"), 16 * 6)
            dve.wait_ge(sem("vp_zeroed"), 4)
            for c in range(3):
                v_evac(1, 0, 0, c)
            attn1(0, 0, True, False)
            with dve.Fori(0, (NT - 2) // 2) as r:
                for h in range(2):
                    attn1(2 * r + h + 1, 1 - h, False, False)
            attn1(NT - 1, 1, False, True)
            head_sum(NT - 1, 2)
            wo_add1(NT - 1, 1)

            dve.wait_ge(sem("bn_done"), 6 * NT)
            variance(0, NT)
            dve.wait_ge(sem("ln_rstd"), 12)
            RS2, var = SMH[0:TQ, 0, 0:NT], MV[0:TQ, :, 1]
            link(nc.vector.tensor_copy(RS2, RS[0:TQ]))
            link(nc.vector.tensor_tensor(var, var, RS2, ALU.mult))
            link(nc.vector.tensor_tensor(var, var, RS2, ALU.mult))
            for q in range(NQ):
                for t in range(q * QUAD, (q + 1) * QUAD):
                    ins = nc.vector.tensor_scalar(U[0:TQ, t, :], X[0:TQ, t, :], MV[0:TQ, t, 0:1], RS[0:TQ, t:t + 1],
                                                  ALU.subtract, ALU.mult)
                ins.then_inc(sem("ln_out"), 1)
            dve.wait_ge(sem("ln_out"), 6 * NQ)
            nc.vector.tensor_scalar(RS[0:TQ], var, EPS, None, ALU.add).then_inc(sem("ln_var"), 1)
            link(nc.vector.scalar_tensor_tensor(out=X[0:TQ], in0=U[0:TQ], scalar=TG[0:TQ, 3:4], in1=X[0:TQ],
                                                op0=ALU.mult, op1=ALU.add))
            dve.wait_ge(sem("ln_rstd"), 13)
            dve.wait_ge(sem("in_nsc"), 16)
            with dve.Fori(0, NT) as t:
                nc.vector.scalar_tensor_tensor(out=XN[0:TQ, t, :], in0=U[0:TQ, t, :], scalar=RS[0:TQ, bass.ds(t, 1)],
                                               in1=NSC[0:TQ], op0=ALU.mult, op1=ALU.mult).then_inc(sem("xn_out"), 1)
            dve.wait_ge(sem("xn_out"), NT)
            route(1, TOP1, E1, NB1, W1, PS[:, 6, 0:NT * E1])
            for i in range(4):
                onehot(1, i, i, None)
            ch = Chain(dve, sem("blk_chain1"))

            def blocks1(i, par, slot, done, ch):
                dve.wait_ge(sem("ab_done1"), i + 1)
                nc.vector.tensor_scalar(wk(1024, D), PS[:, par, 0:D], 7.0, None, ALU.min).then_inc(sem("a_min"), 1)
                dve.wait_ge(sem("a_min"), i + 1)
                nc.vector.tensor_scalar(wk(1536, D), PS[:, par, D:2 * D], 7.0, -7.0, ALU.min, ALU.max).then_inc(
                    sem("b_clip"), 1)
                dve.wait_ge(sem("b_clip"), i + 1)
                ch(nc.vector.scalar_tensor_tensor(out=wk(1792, D), in0=wk(1536, D), scalar=1.0, in1=wk(1024, D),
                                                  op0=ALU.add, op1=ALU.mult))
                dve.wait_ge(sem("sig_ready"), i + 1)
                nc.vector.tensor_tensor(wk(2560 + par * D, D), wk(1792, D), wk(1280, D), ALU.mult).then_inc(sem("s_ready1"), 1)
                if slot is not None:
                    onehot(1, i + 2, slot, done)

            blocks1(0, 0, None, None, ch)
            blocks1(1, 1, None, None, ch)
            R = (NB1 - 4) // 4
            with dve.Fori(0, R) as r:
                ch.begin(4 * r + 2)
                for h in range(4):
                    i = 4 * r + h + 2
                    blocks1(i, h % 2, h, i - 1, ch)
            ch.begin(4 * R + 2)
            for i in range(4 * R + 2, NB1):
                blocks1(i, i % 2, (i + 2) % 4 if i + 2 < NB1 else None, i - 1, ch)
            combine(1, TOP1)
            nc.vector.memset(TMP[:, 0, 0:1], 0.0).then_inc(sem("x_final"), 1)

        @block.tensor
        def _(pe):
            mm = nc.tensor.matmul
            pe.wait_ge(sem("in_const"), 16)

            def transposes(n, src, ready, per_quad, quads=range(NQ), b0=0, banks=4):
                for g in quads:
                    pe.wait_ge(sem(ready), per_quad(g))
                    for c in range(KD):
                        i = KD * g + c
                        if i >= banks:
                            pe.wait_ge(sem("tr_evac"), 2 * NQ * n + i - banks + 1)
                        for j in range(QUAD):
                            ins = nc.tensor.transpose(PS[:, b0 + i % banks, j * TQ:(j + 1) * TQ],
                                                      src[0:TQ, g * QUAD + j, c * P:(c + 1) * P], IDN[0:TQ, 0:TQ])
                        ins.then_inc(sem("tr_done"), 1)

            def q_proj(l, n):
                for i in range(2 * NQ):
                    g, m = i // 2, i % 2
                    if m == 0:
                        pe.wait_ge(sem("tr_evac"), 2 * NQ * n + 2 * (g + 1))
                    if i >= 4:
                        pe.wait_ge(sem(f"q_evac{l}"), i - 3)
                    for k in range(KD):
                        ins = mm(PS[:, 4 + i % 4, 0:N4], WQ[:, k, m * P:(m + 1) * P], UT[:, k, g * N4:(g + 1) * N4],
                                 start=(k == 0), stop=(k == KD - 1))
                    ins.then_inc(sem(f"q_done{l}"), 1)

            def k_proj(l, par, m):
                for k in range(KD):
                    ins = mm(PS[:, 7 if l == 0 else 6 + m, 0:NK], WK[:, k, m * P:(m + 1) * P], CT[par][:, k, :],
                             start=(k == 0), stop=(k == KD - 1))
                ins.then_inc(sem(f"k_done{l}"), 1)

            def v_proj(l, par, c):
                k0, kn = KCH[c]
                for k in range(KD):
                    ins = mm(PS[0:kn, 7 if l == 0 else 6 + c % 2, 0:D], CT[par][:, k, k0:k0 + kn], WV[:, k, :],
                             start=(k == 0), stop=(k == KD - 1))
                ins.then_inc(sem(f"v_done{l}"), 1)

            def wo_proj(l, b, par):
                pe.wait_ge(sem(f"o_evac{l}"), b + 1)
                for k in range(KD):
                    ins = mm(PS[0:TQ, 7, 0:D], ATV[par][:, k, :], WO[:, k, :], start=(k == 0), stop=(k == KD - 1))
                ins.then_inc(sem(f"wo_done{l}"), 1)

            transposes(0, U, "ln_out", lambda g: g + 1)
            pe.wait_ge(sem("in_w4"), 16 * 4)
            q_proj(0, 0)

            def scores0(b, par, g, first):
                n = 8 * b + g
                if g == 0:
                    pe.wait_ge(sem("qb_done0"), 2 * (b + 1))
                    pe.wait_ge(sem("k_evac0"), 2 * (b + 1))
                if not (first and g < 2):
                    pe.wait_ge(sem("exp_done"), n - 1)
                for j in range(2):
                    h = 2 * g + j
                    ins = mm(PS[0:TQ, 2 * (g % 2) + j, 0:NK], QB[par][:, h // 8, h % 8, :], KT[par][:, h // 8, :],
                             start=True, stop=True)
                ins.then_inc(sem("s_done0"), 1)

            def p_transpose(b, g, first):
                n = 8 * b + g
                pe.wait_ge(sem("p_done"), n + 1)
                pe.wait_ge(sem("pt_evac"), n)
                for j in range(2):
                    for c in range(3):
                        ins = nc.tensor.transpose(PS[0:KMAX, 4 + j, c * TQ:(c + 1) * TQ],
                                                  PB[g % 4][0:TQ, j, c * KMAX:(c + 1) * KMAX], IDN[0:TQ, 0:TQ])
                ins.then_inc(sem("t_done"), 1)

            def values0(b, par, g):
                n = 8 * b + g
                pe.wait_ge(sem("pt_evac"), n + 1)
                if g == 0:
                    pe.wait_ge(sem("v_evac0"), 3 * (b + 1))
                    pe.wait_ge(sem("o_evac0"), b)
                q, c8 = g % 4, g // 4
                for j in range(2):
                    for c, (k0, kn) in enumerate(KCH):
                        ins = mm(PS[32 * q:32 * q + 32, 6, c8 * TQ:(c8 + 1) * TQ], VP[par][0:kn, c, j, 32 * g:32 * g + 32],
                                 PT[g % 2][0:kn, j, c * TQ:(c + 1) * TQ], start=(j == 0 and c == 0), stop=(j == 1 and c == 2))
                ins.then_inc(sem("pv_done0"), 1)

            def proj_piece0(b, par, i, first):
                if i == 0:
                    if first:
                        pe.wait_ge(sem("v_evac0"), 3)
                    else:
                        pe.wait_ge(sem("wo_evac0"), b - 1)
                    k_proj(0, par, 0)
                elif i == 1:
                    pe.wait_ge(sem("k_evac0"), 2 * b + 1)
                    k_proj(0, par, 1)
                else:
                    pe.wait_ge(sem("k_evac0"), 2 * b + 2)
                    pe.wait_ge(sem("v_evac0"), 3 * b + i - 2)
                    v_proj(0, par, i - 2)

            def attn0(b, par, first, last, ctw):
                for g in range(8):
                    scores0(b, par, g, first)
                    if g >= 2:
                        p_transpose(b, g - 2, first)
                    elif not first:
                        p_transpose(b - 1, 6 + g, first)
                    if g == 0 and not first:
                        proj_piece0(b, par, 4, None)
                    if g == 3 and not first:
                        pe.wait_ge(sem("v_evac0"), 3 * (b + 1))
                        wo_proj(0, b - 1, 1 - par)
                    if g >= 4 and not last:
                        if g == 4:
                            pe.wait_ge(sem(f"in_ct{1 - par}"), ctw)
                        proj_piece0(b + 1, 1 - par, g - 4, first)
                    if g >= 3:
                        values0(b, par, g - 3)
                    elif not first:
                        values0(b - 1, 1 - par, 5 + g)

            pe.wait_ge(sem("in_ct0"), 16)
            pe.wait_ge(sem("q_evac0"), 2 * NQ)
            k_proj(0, 0, 0)
            pe.wait_ge(sem("k_evac0"), 1)
            k_proj(0, 0, 1)
            for c in range(3):
                pe.wait_ge(sem("k_evac0"), 2)
                if c:
                    pe.wait_ge(sem("v_evac0"), c)
                v_proj(0, 0, c)
            attn0(0, 0, True, False, 16)
            with pe.Fori(0, (NT - 2) // 2) as r:
                for h in range(2):
                    attn0(2 * r + h + 1, 1 - h, False, False, 16 * (r + 2))
            attn0(NT - 1, 1, False, True, None)
            p_transpose(NT - 1, 6, False)
            values0(NT - 1, 1, 5)
            p_transpose(NT - 1, 7, False)
            values0(NT - 1, 1, 6)
            values0(NT - 1, 1, 7)
            pe.wait_ge(sem("wo_evac0"), NT - 1)
            wo_proj(0, NT - 1, 1)

            pe.wait_ge(sem("in_ffw"), 32)
            for q in range(NQ):
                transposes(1, U, "ln_out", lambda g: NQ + g + 1, [q], 6, 2)
                pe.wait_ge(sem("tr_evac"), 2 * NQ + 2 * (q + 1))
                for f in range(FD):
                    if FD * q + f > 3:
                        pe.wait_ge(sem("h_evac"), FD * q + f - 3)
                    for k in range(KD):
                        ins = mm(PS[:, f % 4, 0:N4], W1S[:, k, f * P:(f + 1) * P], UT[:, k, q * N4:(q + 1) * N4],
                                 start=(k == 0), stop=(k == KD - 1))
                    ins.then_inc(sem("h_done"), 1)
                pe.wait_ge(sem("h_evac"), FD * q + FD)
                for j in range(QUAD):
                    t = QUAD * q + j
                    if t > 1:
                        pe.wait_ge(sem("f_evac"), t - 1)
                    for f in range(FD):
                        ins = mm(PS[0:TQ, 4 + t % 2, 0:D], HT[:, f, j * TQ:(j + 1) * TQ], W2S[:, f, :],
                                 start=(f == 0), stop=(f == FD - 1))
                    ins.then_inc(sem("f_done"), 1)

            def logits(l, n, E):
                c0 = 0 if l == 0 else E0
                pe.wait_ge(sem("in_gw"), 16 * 4)
                for t in range(NT):
                    if t % QUAD == 0:
                        pe.wait_ge(sem("tr_evac"), 2 * NQ * n + 2 * (t // QUAD + 1))
                    for k in range(KD):
                        ins = mm(PS[0:TQ, 6, t * E:(t + 1) * E], UT[:, k, t * TQ:(t + 1) * TQ], GW[:, k, c0:c0 + E],
                                 start=(k == 0), stop=(k == KD - 1))
                ins.then_inc(sem(f"logit_done{l}"), 1)
                pe.wait_ge(sem(f"mask_ready{l}"), 1)
                M = wk(2 * 256, NT * E)
                mm(PS[0:TQ, 0, 0:NT * E], CST[0:TQ, C_TRI:C_TRI + TQ], M[0:TQ], start=True, stop=True)
                mm(PS[:, 1, 0:NT * E], CST[0:TQ, C_ONE:C_ONE + P], M[0:TQ], start=True, stop=True).then_inc(
                    sem(f"rank_done{l}"), 1)

            def find_tokens(l, top, nb):
                pr, pb, _ = pair_codes(l, top, nb)
                pe.wait_ge(sem(f"part_code{l}"), 1)
                for n in range(top * NT):
                    if n % NT == 0:
                        pe.wait_ge(sem(f"row_code{l}"), n // NT + 1)
                    ins = mm(PS[:, 5, 0:2 * nb], pr[0:TQ, n, :], pb[0:TQ, n].rearrange("p c b -> p (c b)"),
                             start=(n == 0), stop=(n == top * NT - 1))
                ins.then_inc(sem(f"tokens_found{l}"), 1)

            transposes(2, U, "ln_out", lambda g: 2 * NQ + 2 * (g + 1))
            logits(0, 2, E0)
            find_tokens(0, TOP0, NB0)

            def x_transpose(l, i, par, w):
                pe.wait_ge(sem(f"in_blk{l}_{par}"), w)
                for c in range(KD):
                    ins = nc.tensor.transpose(PS[:, 4, c * P:(c + 1) * P], wk(par * D + c * P, P), IDN)
                ins.then_inc(sem(f"xt_done{l}"), 1)

            def row(o, n):
                return AR[:, bass.ds(o, n)]

            def expert_of(i, E, stride):
                return pe.value_load(EBI[0:1, bass.ds(i, 1)], min_val=0, max_val=(E - 1) * stride)

            def y_proj(l, off, nk, o3, br, brc, par):
                mm(PS[:, 3, 0:D], OHX[0:96, par, :], br[0:96, brc:brc + D], start=True, stop=False)
                for k in range(nk):
                    ins = mm(PS[:, 3, 0:D], wk(3072 + k * P, P), row(off + o3 + k * D, D), start=False, stop=(k == nk - 1))
                ins.then_inc(sem(f"y_done{l}"), 1)

            def ab0(i, par, first):
                off = expert_of(i, E0, W0)
                pe.wait_ge(sem("xt_evac0"), i + 1)
                pe.wait_ge(sem("oh_ready0"), i + 1)
                if not first:
                    pe.wait_ge(sem("z_ready"), i)
                for m in range(2):
                    mm(PS[:, m, :], OHX[0:96, par, :], BR0[0:96, m * F0:(m + 1) * F0], start=True, stop=False)
                    for k in range(KD):
                        ins = mm(PS[:, m, :], wk(512 + par * D + k * P, P), row(off + m * 1024 + k * F0, F0),
                                 start=False, stop=(k == KD - 1))
                    ins.then_inc(sem("a_done" if m == 0 else "ab_done0"), 1)

            def t4(src, bank, name, waits):
                for s_, v in waits:
                    pe.wait_ge(sem(s_), v)
                for k in range(4):
                    ins = nc.tensor.transpose(PS[:, bank, k * P:(k + 1) * P], wk(src + k * P, P), IDN)
                ins.then_inc(sem(name), 1)

            def blocks0(i, par, first, last, w):
                ab0(i, par, first)
                if not first:
                    t4(2560, 6, "st_done", [("s_ready", i)])
                if not last:
                    x_transpose(0, i + 1, 1 - par, w)
                t4(1536, 5, "zt_done", [("z_ready", i + 1)])
                if not first:
                    off = expert_of(i - 1, E0, W0)
                    pe.wait_ge(sem("st_evac"), i)
                    y_proj(0, off, 4, 4096, BR0, 3 * F0, 1 - par)
                off = expert_of(i, E0, W0)
                pe.wait_ge(sem("zt_evac"), i + 1)
                if not first:
                    pe.wait_ge(sem("s_ready"), i)
                mm(PS[:, 2, :], OHX[0:96, par, :], BR0[0:96, 2 * F0:3 * F0], start=True, stop=False)
                for k in range(4):
                    ins = mm(PS[:, 2, :], wk(2048 + k * P, P), row(off + 2048 + k * F0, F0), start=False, stop=(k == 3))
                ins.then_inc(sem("g_done"), 1)

            pe.wait_ge(sem("slots_ready0"), 1)
            pe.wait_ge(sem("in_e0"), 16 * 4 * E0)
            x_transpose(0, 0, 0, 16)
            blocks0(0, 0, True, False, 16)
            R = (NB0 - 2) // 2
            with pe.Fori(0, R) as r:
                for h in range(2):
                    blocks0(2 * r + h + 1, 1 - h, False, False, 16 * (r + 2))
            for i in range(2 * R + 1, NB0):
                blocks0(i, i % 2, False, i == NB0 - 1, 16 * ((i + 1) // 2 + 1))
            t4(2560, 6, "st_done", [("s_ready", NB0)])
            off = expert_of(NB0 - 1, E0, W0)
            pe.wait_ge(sem("st_evac"), NB0)
            pe.wait_ge(sem("y_ready0"), NB0 - 1)
            y_proj(0, off, 4, 4096, BR0, 3 * F0, (NB0 - 1) % 2)

            transposes(3, U, "ln_out", lambda g: 4 * NQ + g + 1)
            pe.wait_ge(sem("in_w4b"), 16 * 6)
            q_proj(1, 3)

            def scores1(b, par, c, first):
                k0, kn = KCH[c]
                n = 3 * b + c
                if c == 0:
                    pe.wait_ge(sem("qb_done1"), 2 * (b + 1))
                    pe.wait_ge(sem("k_evac1"), 2 * (b + 1))
                for bk in range(4):
                    if c or not first:
                        pe.wait_ge(sem("sub_done1"), 4 * n - 3 + bk)
                    q = QB[par][:, bk // 2, (bk % 2) * 4:(bk % 2) * 4 + 4, :].rearrange("p h t -> p (h t)")
                    ins = mm(PS[0:kn, bk, 0:N4], KT[par][:, bk // 2, k0:k0 + kn], q, start=True, stop=True)
                ins.then_inc(sem("s_done1"), 1)

            def values1(b, par, c):
                k0, kn = KCH[c]
                pe.wait_ge(sem("p_done1"), 3 * b + c + 1)
                if c == 0:
                    pe.wait_ge(sem("v_evac1"), 3 * (b + 1))
                for g in range(8):
                    q, c8 = g % 4, g // 4
                    for j in range(2):
                        h = 2 * g + j
                        ins = mm(PS[32 * q:32 * q + 32, 4 + c8, 0:TQ], VP[par][0:kn, c, j, 32 * g:32 * g + 32],
                                 EH[c][0:kn, h // 4, (h % 4) * TQ:(h % 4 + 1) * TQ],
                                 start=(c == 0 and j == 0), stop=(c == 2 and j == 1), skip_group_check=True)
                ins.then_inc(sem("pv_done1"), 1)

            def attn1(b, par, first, last, ctw):
                for c in range(3):
                    scores1(b, par, c, first)
                    if not first:
                        values1(b - 1, 1 - par, c)
                    if c == 0 and not last:
                        pe.wait_ge(sem(f"in_ct{1 - par}b"), ctw)
                        pe.wait_ge(sem("v_evac1"), 3 * (b + 1))
                        k_proj(1, 1 - par, 0)
                        k_proj(1, 1 - par, 1)
                    if c == 1 and not last:
                        pe.wait_ge(sem("k_evac1"), 2 * (b + 2))
                        v_proj(1, 1 - par, 0)
                        v_proj(1, 1 - par, 1)
                    if c == 2 and not last:
                        pe.wait_ge(sem("v_evac1"), 3 * (b + 1) + 1)
                        v_proj(1, 1 - par, 2)
                    if c == 2 and not first:
                        pe.wait_ge(sem("v_evac1"), 3 * (b + 1) + (0 if last else 2))
                        wo_proj(1, b - 1, 1 - par)

            pe.wait_ge(sem("in_ct0b"), 16)
            pe.wait_ge(sem("q_evac1"), 2 * NQ)
            k_proj(1, 0, 0)
            k_proj(1, 0, 1)
            pe.wait_ge(sem("k_evac1"), 2)
            v_proj(1, 0, 0)
            v_proj(1, 0, 1)
            pe.wait_ge(sem("v_evac1"), 1)
            v_proj(1, 0, 2)
            attn1(0, 0, True, False, 16)
            with pe.Fori(0, (NT - 2) // 2) as r:
                for h in range(2):
                    attn1(2 * r + h + 1, 1 - h, False, False, 16 * (r + 2))
            attn1(NT - 1, 1, False, True, None)
            values1(NT - 1, 1, 0)
            values1(NT - 1, 1, 1)
            values1(NT - 1, 1, 2)
            pe.wait_ge(sem("wo_evac1"), NT - 1)
            wo_proj(1, NT - 1, 1)

            transposes(4, XN, "xn_out", lambda g: QUAD * (g + 1))
            logits(1, 4, E1)
            find_tokens(1, TOP1, NB1)

            def ab1(i, par, slot, first):
                off = expert_of(i, E1, W1)
                pe.wait_ge(sem("xt_evac1"), i + 1)
                pe.wait_ge(sem("oh_ready1"), i + 1)
                if not first:
                    pe.wait_ge(sem("b_clip"), i - 1)
                mm(PS[:, par, :], OHX[0:96, slot, :], BR1[0:96, 0:2 * F1], start=True, stop=False)
                for k in range(KD):
                    ins = mm(PS[:, par, :], wk(512 + par * D + k * P, P), row(off + k * 512, 512), start=False,
                             stop=(k == KD - 1))
                ins.then_inc(sem("ab_done1"), 1)

            def st1(i, par):
                pe.wait_ge(sem("s_ready1"), i + 1)
                for k in range(2):
                    ins = nc.tensor.transpose(PS[:, 6, k * P:(k + 1) * P], wk(2560 + par * D + k * P, P), IDN)
                ins.then_inc(sem("st_done1"), 1)

            def y1(i, slot):
                off = expert_of(i, E1, W1)
                pe.wait_ge(sem("st_evac1"), i + 1)
                y_proj(1, off, 2, 1024, BR1, 2 * F1, slot)

            pe.wait_ge(sem("slots_ready1"), 1)
            pe.wait_ge(sem("in_e1"), 16 * 2 * E1)
            x_transpose(1, 0, 0, 16)
            ab1(0, 0, 0, True)
            x_transpose(1, 1, 1, 16)
            ab1(1, 1, 1, True)
            x_transpose(1, 2, 0, 32)
            st1(0, 0)
            R = (NB1 - 4) // 4
            with pe.Fori(0, R) as r:
                for h in range(4):
                    i = 4 * r + h + 2
                    ab1(i, h % 2, (h + 2) % 4, False)
                    x_transpose(1, i + 1, (h + 1) % 2, 16 * (2 * r + (h + 3) // 2 + 1))
                    y1(i - 2, h)
                    st1(i - 1, (h + 1) % 2)
            for i in range(4 * R + 2, NB1):
                ab1(i, i % 2, i % 4, False)
                if i + 1 < NB1:
                    x_transpose(1, i + 1, (i + 1) % 2, 16 * ((i + 1) // 2 + 1))
                y1(i - 2, (i - 2) % 4)
                st1(i - 1, (i - 1) % 2)
            y1(NB1 - 2, (NB1 - 2) % 4)
            st1(NB1 - 1, (NB1 - 1) % 2)
            y1(NB1 - 1, (NB1 - 1) % 4)


def constants():
    import numpy as np
    c = np.zeros((P, C_N), np.float32)
    p = np.arange(P)
    c[:, C_ID:C_ID + P] = np.eye(P)
    c[:, C_TRI:C_TRI + P] = p[:, None] < p[None, :]
    c[:, C_ONE:C_ONE + P] = 1.0
    c[:, C_MASK:C_MASK + 8] = np.where(p[:, None] // HD == np.arange(8)[None, :], HD ** -0.5, 0.0)
    c[:, C_PE] = p % 32
    c[:, C_HALF] = -0.5
    c[:, C_THR:C_THR + CNT] = P * np.arange(CNT)
    c[:, C_PART] = p
    c[:, C_IOTA:C_IOTA + P] = p
    c[:, C_REV0:C_REV0 + E0] = E0 - np.arange(E0)
    c[:, C_REV1:C_REV1 + E1] = E1 - np.arange(E1)
    return c


def kernel(**inputs):
    import numpy as np
    import concourse.bacc as bacc
    from concourse.bass_utils import run_bass_kernel_spmd as run

    g = {k: np.asarray(v) for k, v in inputs.items()}
    arrays = {"x": g["x"], "ctx_t": g["ctx_1024"].transpose(0, 2, 1), "consts": constants()}
    arrays["gates"] = np.concatenate([g["g_xattn"], g["g_ffn"]])

    def cols(v):
        return v.reshape(-1, P).T

    arrays["cols"] = np.concatenate([cols(g["L0_xattn_bq"]), cols(g["L0_xattn_bk"]), cols(g["L0_xattn_b1"]),
                                     cols(g["L1_xattn_Wq_b"]), cols(g["L1_xattn_Wk_b"])], axis=1)
    for n in ["wq", "wk", "wv", "wo", "w1", "w2", "bv", "bo", "g1", "be1", "b2", "g2", "be2"]:
        arrays["L0_xattn_" + n] = g["L0_xattn_" + n]
    for n in ["Wq_w", "Wk_w", "Wv_w", "Wo_w"]:
        arrays["L1_xattn_" + n] = g["L1_xattn_" + n].T
    for n in ["Wv_b", "Wo_b"]:
        arrays["L1_xattn_" + n] = g["L1_xattn_" + n]
    for n in ["gate_w", "gate_b", "w1", "w2", "wg", "w3", "b1", "b2", "bg", "b3"]:
        arrays["L0_ffn_" + n] = g["L0_ffn_" + n]
    for n in ["norm_scale", "wg", "bg", "w2", "b2"]:
        arrays["L1_ffn_" + n] = g["L1_ffn_" + n]
    arrays["L1_ffn_w1"] = g["L1_ffn_w1"].reshape(E1, D, F1, 2).transpose(0, 1, 3, 2).reshape(E1, D, 2 * F1)
    arrays["L1_ffn_b1"] = g["L1_ffn_b1"].reshape(E1, F1, 2).transpose(0, 2, 1).reshape(E1, 2 * F1)

    nc = bacc.Bacc("TRN2", target_bir_lowering=False, num_devices=1)
    feed, aps = {}, {}
    for n, v in arrays.items():
        v = np.ascontiguousarray(v)
        feed["in_" + n] = v
        aps[n] = nc.dram_tensor("in_" + n, v.shape, mybir.dt.from_np(v.dtype), kind="ExternalInput").ap()
    out = nc.dram_tensor("out_0", (NT, TQ, D), F32, kind="ExternalOutput").ap()
    build(nc, aps, out)
    r = run(nc, [feed], core_ids=[0])
    return r.results[0]["out_0"]
```

```python
from contextlib import ExitStack

import concourse.bass as bass
from concourse import mybir

ALU = mybir.AluOpType
ACT = mybir.ActivationFunctionType
F32 = mybir.dt.float32
BF16 = mybir.dt.bfloat16
I32 = mybir.dt.int32
U32 = mybir.dt.uint32
AX = mybir.AxisListType

P = 128
NT, TQ, D = 16, 100, 256
NK = 361
KCH = [(0, 121), (121, 121), (242, 119)]
KMAX = 121
H, HD = 16, 16
KD = D // P
DFF = 1024
FD = DFF // P
QUAD = 4
NQ = NT // QUAD
N4 = QUAD * TQ
NTOK = NT * TQ
PADK = 3 * KMAX
EPS = 1e-5

E0, TOP0, F0 = 8, 2, 512
E1, TOP1, F1 = 16, 4, 256
NB0 = (NTOK * TOP0 + E0 * (P - 1)) // P
NB1 = (NTOK * TOP1 + E1 * (P - 1)) // P
W0 = 2 * (KD * F0) + 4 * F0 + 4 * D
W1 = KD * 2 * F1 + 2 * D
CNT = NTOK // P + 1

C_ID, C_TRI, C_ONE, C_MASK, C_PE, C_HALF, C_PART = 0, 128, 256, 384, 392, 393, 394
C_THR, C_IOTA, C_REV0, C_REV1 = 395, 395 + CNT, 395 + CNT + P, 395 + CNT + P + E0
C_N = C_REV1 + 16

A_U, A_UT = 36864, 30720
A_KT, A_CT = A_U - 4 * NK, A_U - 8 * NK
A_QT, A_QB, A_VP, A_W4, A_BC = 27520, 24320, 21248, 19200, 17408
A_PT = 17408 - 1200
A_W1 = A_PT - 4096
A_E = 17408 - 4800
A_XN = E1 * W1
A_NS = A_XN + NT * D
ROUND = 1.5 * 2.0 ** 23
PRE0 = A_W1 // W0
PRE1 = A_E // W1


class Chain:

    def __init__(self, eng, sem):
        self.eng, self.sem, self.base, self.n = eng, sem, 0, 0

    def begin(self, base):
        self.base, self.n = base, 0

    def __call__(self, ins):
        self.n += 1
        ins.then_inc(self.sem, 1)
        self.eng.wait_ge(self.sem, self.base + self.n)


def build(nc, a, out):
    with ExitStack() as ctx:
        def sb(name, shape, dt=F32):
            return ctx.enter_context(nc.sbuf_tensor(name, shape, dt))

        sems = {}

        def sem(name):
            if name not in sems:
                sems[name] = ctx.enter_context(nc.semaphore(name))
            return sems[name]

        PS = ctx.enter_context(nc.psum_tensor("PS", [P, 8, 512], F32))
        AR = sb("arena", [P, E0 * W0])
        X = sb("X", [P, NT, D])
        CST = sb("consts", [P, C_N])
        COLS = sb("bias_cols", [P, 16])
        TG = sb("tanh_gates", [P, 4])
        BR0 = sb("bias_rows0", [P, 3 * F0 + D], BF16)
        BR1 = sb("bias_rows1", [P, 2 * F1 + D], BF16)
        WORK = sb("work", [P, 4096])
        ST6 = sb("bn_stats", [P, NT, 6])
        MV = sb("mean_var", [P, NT, 2])
        RS = sb("rstd", [P, NT])
        NMX = sb("neg_max", [P, H])
        SUM = sb("exp_sum", [P, 4, 2])
        RCP = sb("exp_rcp", [P, 4, 2])
        TMP = sb("tmp_row", [P, 2, D])
        AT = sb("attn_t", [P, 2, KD * TQ])
        MXH = sb("head_max", [P, TQ])
        SMH = sb("head_sum", [P, 3, TQ])
        GW = sb("gate_w", [P, KD, 16 + 8])
        GB = sb("gate_b", [P, 16 + 8])
        GATE = sb("gates", [P, 4, NT])
        EBI = sb("block_expert", [P, NB1], I32)
        TOK = sb("token_of_row", [P, NB1], U32)
        PAIR = sb("pair_of_row", [P, NB1], U32)
        OHB = sb("block_onehot", [P, NB1], BF16)
        OHX = sb("onehot_rows", [P, 4, P], BF16)

        XS = [nc.dram_tensor(f"tokens{l}", (NTOK, D), F32, kind="Internal").ap() for l in range(2)]
        YS = [nc.dram_tensor(f"pairs_y{l}", (NTOK * top + nb * P, D), F32, kind="Internal").ap()
              for l, (top, nb) in enumerate([(TOP0, NB0), (TOP1, NB1)])]

        IDN = CST[:, C_ID:C_ID + P]

        def ar(off, *shape):
            n = 1
            for s in shape:
                n *= s
            v = AR[:, off:off + n]
            if len(shape) == 2:
                v = v.rearrange("p (a b) -> p a b", b=shape[1])
            elif len(shape) == 3:
                v = v.rearrange("p (a b c) -> p a b c", b=shape[1], c=shape[2])
            elif len(shape) == 4:
                v = v.rearrange("p (a b c d) -> p a b c d", b=shape[1], c=shape[2], d=shape[3])
            return v

        U = ar(A_U, NT, D)
        UT = ar(A_UT, KD, NTOK)
        QT = ar(A_QT, KD, NTOK)
        CT = [ar(A_CT + 722 * i, KD, NK) for i in range(2)]
        KT = [ar(A_KT + 722 * i, KD, NK) for i in range(2)]
        VP = [ar(A_VP + 1536 * i, 3, 2, D) for i in range(2)]
        QB = [ar(A_QB + 1600 * i, KD, 8, TQ) for i in range(2)]
        PT = [ar(A_PT + 600 * i, 2, 3 * TQ) for i in range(2)]
        HT = ar(A_QT - 0, FD, N4)
        WQ, WK, WV, WO = [ar(A_W4 + 512 * i, KD, D) for i in range(4)]
        W1S, W2S = ar(A_W1, KD, DFF), ar(A_W1 + 2048, FD, D)
        BC = [ar(A_BC + D * i, D) for i in range(7)]
        BVO = AR[:, A_BC + 2 * D:A_BC + 3 * D].bitcast(BF16)
        ONE3 = OHX[:, 3, :]
        NEG = ar(A_BC + 3 * D, P)
        EH = [ar(A_E + 1600 * i, QUAD, QUAD * TQ) for i in range(3)]
        XN = ar(A_XN, NT, D)
        NSC = ar(A_NS, D)
        ATV = [AT[:, i, :].rearrange("p (k t) -> p k t", k=KD) for i in range(2)]

        def wk(off, n):
            return WORK[:, off:off + n]

        PB = [wk(2 * PADK * i, 2 * PADK).rearrange("p (j k) -> p j k", j=2) for i in range(4)]

        def results(l, t, n=1):
            top = TOP0 if l == 0 else TOP1
            v = wk((t % 8) * top * D, n * top * D) if l == 0 else ar(A_XN + t * top * D, n * top * D)
            return v.rearrange("p (k d) -> p k d", d=D)

        def pair_codes(l, top, nb):
            n = top * NT
            if l == 0:
                o = (wk(0, n * P // 2), wk(n * P // 2, n * nb), wk(n * P // 2 + n * nb, n * nb // 2))
            else:
                o = (AR[:, A_U:A_U + n * P // 2], AR[:, A_UT:A_UT + n * nb], AR[:, A_XN:A_XN + n * nb // 2])
            pr, pb, eq = (v.bitcast(BF16) for v in o)
            return (pr.rearrange("p (n r) -> p n r", r=P), pb.rearrange("p (n c b) -> p n c b", c=2, b=nb),
                    eq.rearrange("p (n b) -> p n b", b=nb))

        block = ctx.enter_context(nc.Block())

        @block.sync
        def _(sp):
            def load(dst, src, name):
                sp.dma_start(dst, src).then_inc(sem(name), 16)

            def wload(dst, src, name, k):
                load(dst, src.rearrange("(k p) n -> p k n", k=k), name)

            def expert0(e, parts=range(4)):
                for i in parts:
                    name, k, n, o = [("w1", KD, F0, 0), ("w2", KD, F0, 1024), ("wg", 4, F0, 2048), ("w3", 4, D, 4096)][i]
                    wload(ar(e * W0 + o, k, n), a["L0_ffn_" + name][e], "in_e0", k)

            def expert1(e, name):
                o = e * W1
                wload(ar(o, KD, 2 * F1), a["L1_ffn_w1"][e], name, KD)
                wload(ar(o + 1024, 2, D), a["L1_ffn_w2"][e], name, 2)

            def ctx_tile(b, par, s):
                load(CT[par], a["ctx_t"][b].rearrange("(k p) s -> p k s", k=KD), s)

            for q in range(NQ):
                t = slice(q * QUAD, (q + 1) * QUAD)
                load(X[0:TQ, t, :], a["x"][t].rearrange("b p d -> p b d"), f"in_x{q}")
            load(CST[:], a["consts"], "in_const")
            load(COLS[:], a["cols"], "in_cols")
            load(TG[:], a["gates"].partition_broadcast(P), "in_gates")
            for i, n in enumerate(["wq", "wk", "wv", "wo"]):
                wload([WQ, WK, WV, WO][i], a["L0_xattn_" + n], "in_w4", KD)
            ctx_tile(0, 0, "in_ct0")
            ctx_tile(1, 1, "in_ct1")
            for i, n in enumerate(["bv", "bo", "g1", "be1", "b2", "g2", "be2"]):
                load(BC[i], a["L0_xattn_" + n].partition_broadcast(P), "in_bc")
            wload(W1S, a["L0_xattn_w1"], "in_ffw", KD)
            wload(W2S, a["L0_xattn_w2"], "in_ffw", FD)
            wload(GW[:, :, 0:E0], a["L0_ffn_gate_w"], "in_gw", KD)
            wload(GW[:, :, E0:E0 + E1], a["L1_ffn_wg"], "in_gw", KD)
            load(GB[:, 0:E0], a["L0_ffn_gate_b"].partition_broadcast(P), "in_gw")
            load(GB[:, E0:E0 + E1], a["L1_ffn_bg"].partition_broadcast(P), "in_gw")
            for e in range(PRE0):
                expert0(e)

            def tokens_out(l, src, ready, per_quad, quads=range(NQ)):
                rows = XS[l].rearrange("(t p) d -> p t d", p=TQ)
                for q in quads:
                    sp.wait_ge(sem(ready), per_quad(q))
                    load(rows[:, q * QUAD:(q + 1) * QUAD, :], src[0:TQ, q * QUAD:(q + 1) * QUAD, :], f"tokens_out{l}")

            def attn_ctx(l):
                with sp.Fori(0, (NT - 2) // 2) as r:
                    for h in range(2):
                        sp.wait_ge(sem(f"v_done{l}"), 6 * r + 3 * (h + 1))
                        ctx_tile(2 * r + h + 2, h, f"in_ct{h}" + ("" if l == 0 else "b"))

            attn_ctx(0)

            sp.wait_ge(sem("bias_zeroed"), 1)
            for q in range(3):
                for i, n in enumerate(["b1", "b2", "bg"]):
                    load(WORK[32 * q:32 * q + E0, i * F0:(i + 1) * F0], a["L0_ffn_" + n], "in_br")
                load(WORK[32 * q:32 * q + E0, 3 * F0:3 * F0 + D], a["L0_ffn_b3"], "in_br")
                load(WORK[32 * q:32 * q + E1, 2048:2048 + 2 * F1], a["L1_ffn_b1"], "in_br")
                load(WORK[32 * q:32 * q + E1, 2048 + 2 * F1:2048 + 2 * F1 + D], a["L1_ffn_b2"], "in_br")

            assert PRE0 == 2 and 2 * W0 + 1024 <= A_W1 and 4 * W0 >= A_W4 and 5 * W0 + 1024 <= A_QT
            assert 3 * W0 + 1024 >= A_PT and 3 * W0 + 2048 <= A_BC and 3 * W0 + 4096 >= A_W4
            expert0(4)
            expert0(2, [0])
            expert0(3, [1, 3])
            expert0(5, [0])
            tokens_out(0, U, "ln_out", lambda q: 2 * NQ + 2 * (q + 1), range(NQ - 1))
            sp.wait_ge(sem("ff_added"), NT)
            expert0(2, [1, 2, 3])
            expert0(3, [0])
            expert0(5, [1, 2, 3])
            tokens_out(0, U, "ln_out", lambda q: 2 * NQ + 2 * (q + 1), [NQ - 1])
            sp.wait_ge(sem("ln_out"), 4 * NQ)
            expert0(3, [2])
            sp.wait_ge(sem("logit_done0"), 1)
            expert0(E0 - 2)
            sp.wait_ge(sem("tokens_out0"), 16 * NQ)
            expert0(E0 - 1)

            def results_back(l, top, nb):
                for par in range(2):
                    n = len([i for i in range(nb) if i % 2 == par])
                    sp.wait_ge(sem(f"y_out{l}_{par}"), 16 * n)
                rows = YS[l][0:NTOK * top].rearrange("(u p) d -> p u d", p=TQ)
                step = 1 if l == 0 else 2
                for t in range(0, NT, step):
                    if l == 0 and t >= 8:
                        sp.wait_ge(sem("y_used0"), top * ((t - 8) // 2 * 2 + 2))
                    load(results(l, t, step)[0:TQ], rows[:, t * top:(t + step) * top, :], f"y_back_{t // step % 8}")

            sp.wait_ge(sem("y_ready0"), NB0)
            for i, n in enumerate(["Wq_w", "Wk_w", "Wv_w", "Wo_w"]):
                wload([WQ, WK, WV, WO][i], a["L1_xattn_" + n], "in_w4b", KD)
            load(BC[0], a["L1_xattn_Wv_b"].partition_broadcast(P), "in_w4b")
            load(BC[1], a["L1_xattn_Wo_b"].partition_broadcast(P), "in_w4b")
            ctx_tile(0, 0, "in_ct0b")
            results_back(0, TOP0, NB0)
            ctx_tile(1, 1, "in_ct1b")
            for e in range(PRE1):
                expert1(e, "in_e1")
            attn_ctx(1)
            sp.wait_ge(sem("wo_added1"), NT + 1)
            load(NSC, a["L1_ffn_norm_scale"].partition_broadcast(P), "in_nsc")
            for e in range(PRE1, E1):
                expert1(e, "in_e1")
            tokens_out(1, XN, "xn_out", lambda q: QUAD * (q + 1))
            results_back(1, TOP1, NB1)

            for q in range(NQ):
                sp.wait_ge(sem("y_used1"), TOP1 * QUAD * (q + 1))
                t = slice(q * QUAD, (q + 1) * QUAD)
                load(out[t].rearrange("b p d -> p b d"), X[0:TQ, t, :], "out_done")
            sp.wait_ge(sem("out_done"), 16 * NQ)

        @block.gpsimd
        def _(pool):
            for i in range(2):
                nc.gpsimd.memset(VP[i], 0.0).then_inc(sem("vp_zeroed"), 1)
            nc.gpsimd.memset(WORK[0:TQ, 0:8 * PADK], 0.0).then_inc(sem("pb_zeroed"), 1)
            pool.wait_ge(sem("in_const"), 16)

            def rstd(n, t0=0, nt=NT):
                pool.wait_ge(sem("ln_var"), n)
                r = RS[0:TQ, t0:t0 + nt]
                nc.gpsimd.tensor_tensor(r, r, CST[0:TQ, C_HALF:C_HALF + 1].to_broadcast([TQ, nt]),
                                        ALU.pow).then_inc(sem("ln_rstd"), 1)

            def blockdiag(l, b, par, wait):
                if wait:
                    pool.wait_ge(sem(f"s_done{l}"), (8 if l == 0 else 3) * (b - 1))
                for c in range(KD):
                    q = QT[:, c, bass.ds(b * TQ, TQ)].rearrange("p (a t) -> p a t", a=1)
                    m = CST[:, C_MASK:C_MASK + 8].unsqueeze(2)
                    nc.gpsimd.tensor_tensor(QB[par][:, c], q.to_broadcast([P, 8, TQ]),
                                            m.to_broadcast([P, 8, TQ]), ALU.mult).then_inc(sem(f"qb_done{l}"), 1)

            def blocks_io(l, nb):
                lag = 2 if l == 0 else 3

                def fetch(i):
                    nc.gpsimd.indirect_dma_start(
                        out=wk((i % 2) * D, D), out_offset=None, in_=XS[l],
                        in_offset=bass.IndirectOffsetOnAxis(ap=TOK[:, i:i + 1], axis=0),
                    ).then_inc(sem(f"in_blk{l}_{i % 2}"), 16)

                def store(i):
                    pool.wait_ge(sem(f"y_ready{l}"), i + 1)
                    nc.gpsimd.indirect_dma_start(
                        out=YS[l], out_offset=bass.IndirectOffsetOnAxis(ap=PAIR[:, i:i + 1], axis=0),
                        in_=wk(3584 + (i % 2) * D, D), in_offset=None,
                    ).then_inc(sem(f"y_out{l}_{i % 2}"), 16)

                pool.wait_ge(sem(f"rows_known{l}"), 1)
                pool.wait_ge(sem(f"tokens_out{l}"), 16 * NQ)
                fetch(0)
                fetch(1)
                pool.wait_ge(sem(f"rows_known{l}"), 2)
                for i in range(nb - 2):
                    pool.wait_ge(sem(f"xt_done{l}"), i + 1)
                    fetch(i + 2)
                    if i >= lag:
                        store(i - lag)
                for i in range(nb - 2 - lag, nb):
                    store(i)

            def tile_codes(l, top, nb):
                pool.wait_ge(sem(f"block_code{l}"), 1)
                _, pb, eq = pair_codes(l, top, nb)
                for k in range(top):
                    g = slice(k * NT, (k + 1) * NT)
                    f = CST[0:TQ, C_IOTA + k:C_IOTA + top * NT:top].unsqueeze(2).to_broadcast([TQ, NT, nb])
                    nc.gpsimd.tensor_tensor(pb[0:TQ, g, 1, :], eq[0:TQ, g, :], f, ALU.mult).then_inc(
                        sem(f"tile_code{l}"), 1)

            def first_blockdiags(l):
                pool.wait_ge(sem(f"q_evac{l}"), 2)
                blockdiag(l, 0, 0, False)
                blockdiag(l, 1, 1, False)
                pool.wait_ge(sem(f"q_evac{l}"), 2 * NQ)

            rstd(1)
            first_blockdiags(0)
            with pool.Fori(0, (NT - 2) // 2) as r:
                for h in range(2):
                    blockdiag(0, 2 * r + h + 2, h, True)
            rstd(2)
            pool.wait_ge(sem("wo_added0"), NT)
            nc.gpsimd.memset(WORK[0:96, 0:2048 + 2 * F1 + D], 0.0).then_inc(sem("bias_zeroed"), 1)
            for q in range(NQ):
                rstd(3 + 2 * q, q * QUAD, QUAD)
                rstd(4 + 2 * q, q * QUAD, QUAD)
            tile_codes(0, TOP0, NB0)
            blocks_io(0, NB0)
            for i in range(2):
                nc.gpsimd.memset(VP[i], 0.0).then_inc(sem("vp_zeroed"), 1)
            for q in range(NQ):
                rstd(11 + q, q * QUAD, QUAD)


            def head_weights(b, par, wait, more):
                for ch, (k0, kn) in enumerate(KCH):
                    pool.wait_ge(sem("rcp_done1"), 3 * b + ch + 1)
                    e = EH[ch][0:kn].rearrange("p a (h t) -> p (a h) t", h=QUAD)
                    r = SMH[0:kn, ch, :].rearrange("p (a t) -> p a t", a=1)
                    nc.gpsimd.tensor_tensor(e, e, r.to_broadcast([kn, H, TQ]), ALU.mult).then_inc(sem("p_done1"), 1)
                    if ch == 1 and more:
                        blockdiag(1, b + 2, par, wait)

            first_blockdiags(1)
            with pool.Fori(0, (NT - 2) // 2) as r:
                for h in range(2):
                    head_weights(2 * r + h, h, True, True)
            head_weights(NT - 2, 0, False, False)
            head_weights(NT - 1, 1, False, False)
            rstd(11 + NQ)
            pool.wait_ge(sem("ln_var"), 12 + NQ)
            v = MV[0:TQ, :, 1]
            nc.gpsimd.tensor_tensor(v, v, CST[0:TQ, C_HALF:C_HALF + 1].to_broadcast([TQ, NT]),
                                    ALU.pow).then_inc(sem("ln_rstd"), 1)
            tile_codes(1, TOP1, NB1)
            blocks_io(1, NB1)

        @block.scalar
        def _(act):
            act.wait_ge(sem("in_gates"), 16)
            nc.scalar.activation(TG[:], TG[:], ACT.Tanh).then_inc(sem("tg_ready"), 1)
            act.wait_ge(sem("in_cols"), 16)

            def t_evac(n, g, c, bank):
                act.wait_ge(sem("tr_done"), 2 * NQ * n + KD * g + c + 1)
                nc.scalar.activation(UT[:, c, g * N4:(g + 1) * N4], PS[:, bank, 0:N4],
                                     ACT.Identity).then_inc(sem("tr_evac"), 1)

            def transposes(n):
                for g in range(NQ):
                    for c in range(KD):
                        t_evac(n, g, c, (KD * g + c) % 4)

            def k_evac(l, b, par, m, bank=None):
                act.wait_ge(sem(f"k_done{l}"), 2 * b + m + 1)
                nc.scalar.activation(KT[par][:, m, :], PS[:, bank or (7 if l == 0 else 6 + m), 0:NK], ACT.Identity,
                                     bias=COLS[:, (2 if l == 0 else 14) + m:(3 if l == 0 else 15) + m]
                                     ).then_inc(sem(f"k_evac{l}"), 1)

            def o_evac(l, b, par):
                per = 8 if l == 0 else 3
                act.wait_ge(sem(f"pv_done{l}"), per * (b + 1))
                src = PS[:, 6, 0:KD * TQ] if l == 0 else PS[:, 4:6, 0:TQ]
                dst = AT[:, par, :] if l == 0 else ATV[par]
                nc.scalar.activation(dst, src, ACT.Identity).then_inc(sem(f"o_evac{l}"), 1)

            def q_evac(l, g, m):
                act.wait_ge(sem(f"q_done{l}"), 2 * g + m + 1)
                c = (0 if l == 0 else 12) + m
                nc.scalar.activation(QT[:, m, g * N4:(g + 1) * N4], PS[:, 4 + (2 * g + m) % 4, 0:N4], ACT.Identity,
                                     bias=COLS[:, c:c + 1]).then_inc(sem(f"q_evac{l}"), 1)

            def v_evac1(b, par, c, bank):
                kn = KCH[c][1]
                act.wait_ge(sem("v_done1"), 3 * b + c + 1)
                ps = PS[0:kn, bank, 0:D].rearrange("p (a j d) -> p a j d", j=2, d=HD)
                for j in range(2):
                    v = VP[par][0:kn, c, j, :].rearrange("p (a j d) -> p a j d", j=2, d=HD)
                    ins = nc.scalar.activation(v[:, :, j, :], ps[:, :, j, :], ACT.Identity)
                ins.then_inc(sem("v_evac1"), 1)

            def attn_start(l, n):
                for m in range(KD):
                    k_evac(l, 0, 0, m, 4 + m)
                if l:
                    act.wait_ge(sem("vp_zeroed"), 4)
                    for c, bank in enumerate((6, 7, 4)):
                        v_evac1(0, 0, c, bank)
                for g in range(NQ):
                    for c in range(KD):
                        t_evac(n, g, c, (KD * g + c) % 4)
                    for m in range(KD):
                        q_evac(l, g, m)

            attn_start(0, 0)

            def pt_evac(b, g, wait):
                n = 8 * b + g
                act.wait_ge(sem("t_done"), n + 1)
                if wait:
                    act.wait_ge(sem("pv_done0"), n - 1)
                nc.scalar.activation(PT[g % 2][0:KMAX], PS[0:KMAX, 4:6, 0:3 * TQ],
                                     ACT.Identity).then_inc(sem("pt_evac"), 1)

            def attn0(b, par, first, last):
                for g in range(8):
                    if g == 3 and not first:
                        o_evac(0, b - 1, 1 - par)
                    if g >= 2:
                        pt_evac(b, g - 2, not first or g >= 4)
                    elif not first:
                        pt_evac(b - 1, 6 + g, True)
                    if g in (4, 5) and not last:
                        k_evac(0, b + 1, 1 - par, g - 4)
                    n = 8 * b + g
                    act.wait_ge(sem("mx_done"), n + 1)
                    if not (first and g < 4):
                        act.wait_ge(sem("t_done"), n - 3)
                    for j in range(2):
                        ins = nc.scalar.activation(PB[g % 4][0:TQ, j, 0:NK], PS[0:TQ, 2 * (g % 2) + j, 0:NK], ACT.Exp,
                                                   bias=NMX[0:TQ, 2 * g + j:2 * g + j + 1],
                                                   accum_out=SUM[0:TQ, g % 4, j:j + 1])
                    ins.then_inc(sem("exp_done"), 1)

            act.wait_ge(sem("pb_zeroed"), 1)
            attn0(0, 0, True, False)
            with act.Fori(0, (NT - 2) // 2) as r:
                for h in range(2):
                    attn0(2 * r + h + 1, 1 - h, False, False)
            attn0(NT - 1, 1, False, True)
            pt_evac(NT - 1, 6, True)
            pt_evac(NT - 1, 7, True)
            o_evac(0, NT - 1, 1)

            for q in range(NQ):
                for c in range(KD):
                    t_evac(1, q, c, 6 + c)
                for f in range(FD):
                    act.wait_ge(sem("h_done"), FD * q + f + 1)
                    if q and f == 0:
                        act.wait_ge(sem("f_done"), QUAD * q)
                    nc.scalar.activation(HT[:, f, :], PS[:, f % 4, 0:N4], ACT.Relu,
                                         bias=COLS[:, 4 + f:5 + f]).then_inc(sem("h_evac"), 1)
            transposes(2)

            def gate_exp(l, top):
                act.wait_ge(sem(f"top_ready{l}"), 1)
                nc.scalar.activation(GATE[0:TQ, 0:top], GATE[0:TQ, 0:top], ACT.Exp).then_inc(sem(f"gate_exp{l}"), 1)

            gate_exp(0, TOP0)

            def partition_code(l, top, nb):
                act.wait_ge(sem(f"block_code{l}"), 1)
                _, pb, eq = pair_codes(l, top, nb)
                nc.scalar.activation(pb[0:TQ, :, 0, :], eq[0:TQ], ACT.Identity,
                                     scale=CST[0:TQ, C_PART:C_PART + 1]).then_inc(sem(f"part_code{l}"), 1)

            partition_code(0, TOP0, NB0)

            za, zt, s = wk(1024, 512), wk(2048, 512), wk(2560, 512)

            def xt_evac(l, i, par):
                act.wait_ge(sem(f"xt_done{l}"), i + 1)
                nc.scalar.activation(wk(512 + par * D, D), PS[:, 4, 0:D], ACT.Identity).then_inc(sem(f"xt_evac{l}"), 1)

            def y_evac(l, i, par, wait):
                act.wait_ge(sem(f"y_done{l}"), i + 1)
                if wait is not None:
                    act.wait_ge(sem(f"y_out{l}_{par}"), wait)
                nc.scalar.activation(wk(3584 + par * D, D), PS[:, 3, 0:D], ACT.Identity).then_inc(sem(f"y_ready{l}"), 1)

            def blocks0(i, par, first, last, yw):
                act.wait_ge(sem("a_done"), i + 1)
                nc.scalar.activation(za, PS[:, 0, :], ACT.Identity).then_inc(sem("a_copied"), 1)
                if not first:
                    act.wait_ge(sem("st_done"), i)
                    nc.scalar.activation(wk(3072, 512), PS[:, 6, :], ACT.Identity).then_inc(sem("st_evac"), 1)
                if not last:
                    xt_evac(0, i + 1, 1 - par)
                act.wait_ge(sem("zt_done"), i + 1)
                nc.scalar.activation(zt, PS[:, 5, :], ACT.Identity).then_inc(sem("zt_evac"), 1)
                if not first:
                    y_evac(0, i - 1, 1 - par, yw)
                act.wait_ge(sem("g_done"), i + 1)
                nc.scalar.activation(s, PS[:, 2, :], ACT.Silu).then_inc(sem("s_ready"), 1)

            xt_evac(0, 0, 0)
            blocks0(0, 0, True, False, None)
            blocks0(1, 1, False, False, None)
            blocks0(2, 0, False, False, None)
            R0 = (NB0 - 4) // 2
            with act.Fori(0, R0) as r:
                for h in range(2):
                    blocks0(2 * r + 3 + h, 1 - h, False, False, 16 * (r + 1))
            for i in range(2 * R0 + 3, NB0):
                blocks0(i, i % 2, False, i == NB0 - 1, 16 * ((i - 1) // 2))
            act.wait_ge(sem("st_done"), NB0)
            nc.scalar.activation(wk(3072, 512), PS[:, 6, :], ACT.Identity).then_inc(sem("st_evac"), 1)
            y_evac(0, NB0 - 1, (NB0 - 1) % 2, 16 * ((NB0 - 1) // 2))

            attn_start(1, 3)

            def attn1(b, par, first, last):
                for ch, (k0, kn) in enumerate(KCH):
                    if ch == 2 and not first:
                        o_evac(1, b - 1, 1 - par)
                    if not first:
                        act.wait_ge(sem("pv_done1"), 3 * (b - 1) + ch + 1)
                    act.wait_ge(sem("neg_done1"), 3 * b + ch + 1)
                    nc.scalar.activation(EH[ch][0:kn, 3, :], PS[0:kn, 3, 0:N4], ACT.Exp).then_inc(sem("bank3_exp1"), 1)
                    act.wait_ge(sem("sub_done1"), 9 * b + 3 * ch + 3)
                    nc.scalar.activation(EH[ch][0:kn, 0:3, :], EH[ch][0:kn, 0:3, :], ACT.Exp).then_inc(sem("exp_done1"), 1)
                    if ch == 0 and not last:
                        k_evac(1, b + 1, 1 - par, 0)
                        k_evac(1, b + 1, 1 - par, 1)
                    if ch == 1 and not last:
                        v_evac1(b + 1, 1 - par, 0, 6)
                        v_evac1(b + 1, 1 - par, 1, 7)
                    if ch == 2 and not last:
                        v_evac1(b + 1, 1 - par, 2, 6)

            attn1(0, 0, True, False)
            with act.Fori(0, (NT - 2) // 2) as r:
                for h in range(2):
                    attn1(2 * r + h + 1, 1 - h, False, False)
            attn1(NT - 1, 1, False, True)
            o_evac(1, NT - 1, 1)

            transposes(4)
            gate_exp(1, TOP1)
            partition_code(1, TOP1, NB1)

            def blocks1(i, par, xt, st, yw):
                if xt:
                    xt_evac(1, i + 1, 1 - par)
                act.wait_ge(sem("a_min"), i + 1)
                nc.scalar.activation(wk(1280, D), wk(1024, D), ACT.Sigmoid, scale=1.702).then_inc(sem("sig_ready"), 1)
                if yw is not None:
                    y_evac(1, i - 2, par, yw)
                if st:
                    act.wait_ge(sem("st_done1"), i)
                    nc.scalar.activation(wk(3072, D), PS[:, 6, 0:D], ACT.Identity).then_inc(sem("st_evac1"), 1)

            xt_evac(1, 0, 0)
            blocks1(0, 0, True, False, None)
            blocks1(1, 1, True, True, None)
            for i in (2, 3):
                blocks1(i, i % 2, True, True, 0)
            R1 = (NB1 - 5) // 2
            with act.Fori(0, R1) as r:
                for h in range(2):
                    blocks1(2 * r + 4 + h, h, True, True, 16 * (r + 1))
            for i in range(2 * R1 + 4, NB1):
                blocks1(i, i % 2, i + 1 < NB1, True, 16 * ((i - 2) // 2))
            y_evac(1, NB1 - 2, NB1 % 2, 16 * ((NB1 - 2) // 2))
            act.wait_ge(sem("st_done1"), NB1)
            nc.scalar.activation(wk(3072, D), PS[:, 6, 0:D], ACT.Identity).then_inc(sem("st_evac1"), 1)
            y_evac(1, NB1 - 1, (NB1 - 1) % 2, 16 * ((NB1 - 1) // 2))

        @block.vector
        def _(dve):
            link = Chain(dve, sem("v_chain"))

            dve.wait_ge(sem("in_const"), 16)

            def stats(t, src):
                nc.vector.bn_stats(ST6[0:TQ, t, :], src[0:TQ, t, :]).then_inc(sem("bn_done"), 1)

            def variance(t0, nt):
                st = ST6[0:TQ, t0:t0 + nt]
                me, mo, m2e, m2o = (st[:, :, c] for c in (1, 4, 2, 5))
                mean, dif, rs = MV[0:TQ, t0:t0 + nt, 0], MV[0:TQ, t0:t0 + nt, 1], RS[0:TQ, t0:t0 + nt]
                link(nc.vector.tensor_tensor(mean, me, mo, ALU.add))
                link(nc.vector.tensor_scalar(mean, mean, 0.5, None, ALU.mult))
                link(nc.vector.tensor_tensor(dif, me, mo, ALU.subtract))
                link(nc.vector.scalar_tensor_tensor(out=dif, in0=dif, scalar=0.25, in1=dif, op0=ALU.mult, op1=ALU.mult))
                link(nc.vector.tensor_tensor(rs, m2e, m2o, ALU.add))
                link(nc.vector.scalar_tensor_tensor(out=dif, in0=rs, scalar=1.0 / D, in1=dif, op0=ALU.mult, op1=ALU.add))
                nc.vector.tensor_scalar(rs, dif, EPS, None, ALU.add).then_inc(sem("ln_var"), 1)

            def apply(q, src, gamma=None, beta=None):
                for t in range(q * QUAD, (q + 1) * QUAD):
                    ins = nc.vector.tensor_scalar(U[0:TQ, t, :], src[0:TQ, t, :], MV[0:TQ, t, 0:1],
                                                  RS[0:TQ, t:t + 1], ALU.subtract, ALU.mult)
                if gamma is not None:
                    link(ins)
                    v = U[0:TQ, q * QUAD:(q + 1) * QUAD, :]
                    link(nc.vector.tensor_tensor(v, v, gamma[0:TQ].unsqueeze(1).to_broadcast([TQ, QUAD, D]), ALU.mult))
                    ins = nc.vector.tensor_tensor(v, v, beta[0:TQ].unsqueeze(1).to_broadcast([TQ, QUAD, D]), ALU.add)
                ins.then_inc(sem("ln_out"), 1)

            def norm(bn, rstd, src, gamma=None, beta=None):
                dve.wait_ge(sem("bn_done"), bn)
                variance(0, NT)
                dve.wait_ge(sem("ln_rstd"), rstd)
                for q in range(NQ):
                    apply(q, src, gamma, beta)

            def v_evac0(b, par, c, bank):
                kn = KCH[c][1]
                dve.wait_ge(sem("v_done0"), 3 * b + c + 1)
                ps = PS[0:kn, bank, 0:D].rearrange("p (a j d) -> p a j d", j=2, d=HD)
                bv = BC[0][0:kn].rearrange("p (a j d) -> p a j d", j=2, d=HD)
                for j in range(2):
                    v = VP[par][0:kn, c, j, :].rearrange("p (a j d) -> p a j d", j=2, d=HD)
                    ins = nc.vector.tensor_tensor(v[:, :, j, :], ps[:, :, j, :], bv[:, :, j, :], ALU.add)
                ins.then_inc(sem("v_evac0"), 1)

            for t in range(NT):
                if t % QUAD == 0:
                    dve.wait_ge(sem(f"in_x{t // QUAD}"), 16)
                stats(t, X)
            dve.wait_ge(sem("bn_done"), NT)
            variance(0, NT)
            dve.wait_ge(sem("ln_rstd"), 1)
            apply(0, X)
            dve.wait_ge(sem("in_bc"), 16 * 7)
            dve.wait_ge(sem("vp_zeroed"), 2)
            for c, bank in enumerate((6, 7, 4)):
                v_evac0(0, 0, c, bank)
            for q in range(1, NQ):
                apply(q, X)

            ch0 = Chain(dve, sem("attn_chain0"))

            def p_norm(b, g, ch):
                dve.wait_ge(sem("exp_done"), 8 * b + g + 1)
                ch(nc.vector.reciprocal(RCP[0:TQ, g % 4, :], SUM[0:TQ, g % 4, :]))
                for j in range(2):
                    v = PB[g % 4][0:TQ, j, 0:NK]
                    ins = nc.vector.tensor_scalar(v, v, RCP[0:TQ, g % 4, j:j + 1], None, ALU.mult)
                ins.then_inc(sem("p_done"), 1)

            def wo_add0(b, par):
                dve.wait_ge(sem("wo_done0"), b + 1)
                nc.vector.tensor_tensor(TMP[0:TQ, par, :], PS[0:TQ, 7, 0:D], BC[1][0:TQ], ALU.add).then_inc(
                    sem("wo_evac0"), 1)
                dve.wait_ge(sem("wo_evac0"), b + 1)
                u = U[0:TQ, b, :]
                nc.vector.tensor_tensor(u, u, TMP[0:TQ, par, :], ALU.add).then_inc(sem("wo_added0"), 1)
                dve.wait_ge(sem("wo_added0"), b + 1)
                stats(b, U)

            def attn0(b, par, first, last, ch):
                for g in range(8):
                    n = 8 * b + g
                    dve.wait_ge(sem("s_done0"), n + 1)
                    nc.vector.tensor_reduce(NMX[0:TQ, 2 * g:2 * g + 2], PS[0:TQ, 2 * (g % 2):2 * (g % 2) + 2, 0:NK],
                                            axis=AX.X, op=ALU.max, negate=True).then_inc(sem("mx_done"), 1)
                    if g > 0 or not first:
                        p_norm(*((b, g - 1) if g else (b - 1, 7)), ch)
                    if g == 0 and not first:
                        v_evac0(b, par, 2, 7)
                    if g == 3 and not first:
                        wo_add0(b - 1, 1 - par)
                    if g in (6, 7) and not last:
                        v_evac0(b + 1, 1 - par, g - 6, 7)

            attn0(0, 0, True, False, ch0)
            with dve.Fori(0, (NT - 2) // 2) as r:
                ch0.begin(r * 16 + 7)
                for h in range(2):
                    attn0(2 * r + h + 1, 1 - h, False, False, ch0)
                assert ch0.n == 16
            ch0.begin(7 + 16 * ((NT - 2) // 2))
            attn0(NT - 1, 1, False, True, ch0)
            p_norm(NT - 1, 7, ch0)
            wo_add0(NT - 1, 1)

            norm(2 * NT, 2, U, BC[2], BC[3])

            def three_parts(br, w):
                link(nc.vector.tensor_copy(br, w))
                link(nc.vector.tensor_tensor(w, w, br, ALU.subtract))
                link(nc.vector.tensor_copy(br[32:64], w[32:64]))
                link(nc.vector.tensor_copy(br[64:96], w[64:96]))
                link(nc.vector.tensor_tensor(w[64:96], w[64:96], br[64:96], ALU.subtract))
                link(nc.vector.tensor_copy(br[64:96], w[64:96]))

            dve.wait_ge(sem("in_br"), 16 * 18)
            for br, o, n in ((BR0, 0, 3 * F0 + D), (BR1, 2048, 2 * F1 + D)):
                three_parts(br[0:96], wk(o, n)[0:96])

            dve.wait_ge(sem("tg_ready"), 1)
            for q in range(NQ):
                for t in range(q * QUAD, (q + 1) * QUAD):
                    dve.wait_ge(sem("f_done"), t + 1)
                    nc.vector.tensor_tensor(TMP[0:TQ, t % 2, :], PS[0:TQ, 4 + t % 2, 0:D], BC[4][0:TQ],
                                            ALU.add).then_inc(sem("f_evac"), 1)
                    dve.wait_ge(sem("f_evac"), t + 1)
                    u = U[0:TQ, t, :]
                    nc.vector.tensor_tensor(u, u, TMP[0:TQ, t % 2, :], ALU.add).then_inc(sem("ff_added"), 1)
                    dve.wait_ge(sem("ff_added"), t + 1)
                    stats(t, U)
                dve.wait_ge(sem("bn_done"), 2 * NT + 2 * QUAD * q + QUAD)
                variance(q * QUAD, QUAD)
                dve.wait_ge(sem("ln_rstd"), 3 + 2 * q)
                apply(q, U, BC[5], BC[6])
                dve.wait_ge(sem("ln_out"), 2 * NQ + 2 * q + 1)
                x, u = (v[0:TQ, q * QUAD:(q + 1) * QUAD, :] for v in (X, U))
                link(nc.vector.scalar_tensor_tensor(out=x, in0=u, scalar=TG[0:TQ, 0:1], in1=x, op0=ALU.mult, op1=ALU.add))
                for t in range(q * QUAD, (q + 1) * QUAD):
                    stats(t, X)
                dve.wait_ge(sem("bn_done"), 2 * NT + 2 * QUAD * (q + 1))
                variance(q * QUAD, QUAD)
                dve.wait_ge(sem("ln_rstd"), 4 + 2 * q)
                apply(q, X)
            dve.wait_ge(sem("ln_out"), 4 * NQ)

            def route(l, top, E, nb, stride, logit_ps):
                NE = NT * E
                c0 = 0 if l == 0 else E0
                L, SC, M, A, B, C, POS = (wk(o * 256, NE) for o in range(7))
                OH = [wk((7 + k) * 256, NE) for k in range(top)]
                v3 = lambda t, n=TQ: t[0:n].rearrange("p (t e) -> p t e", e=E)
                dve.wait_ge(sem("in_gw"), 16 * 4)
                dve.wait_ge(sem(f"logit_done{l}"), 1)
                link(nc.vector.tensor_tensor(v3(L), v3(logit_ps), GB[0:TQ, c0:c0 + E].unsqueeze(1).to_broadcast([TQ, NT, E]), ALU.add))
                rev = CST[0:TQ, (C_REV0 if l == 0 else C_REV1):(C_REV0 if l == 0 else C_REV1) + E].unsqueeze(1).to_broadcast([TQ, NT, E])
                for k in range(top):
                    link(nc.vector.tensor_reduce(GATE[0:TQ, k, :], v3(L), axis=AX.X, op=ALU.max))
                    link(nc.vector.tensor_tensor(v3(SC), v3(L), GATE[0:TQ, k, :].unsqueeze(2).to_broadcast([TQ, NT, E]), ALU.is_equal))
                    link(nc.vector.tensor_tensor(v3(SC), v3(SC), rev, ALU.mult))
                    link(nc.vector.tensor_reduce(RS[0:TQ], v3(SC), axis=AX.X, op=ALU.max))
                    link(nc.vector.tensor_tensor(v3(OH[k]), v3(SC), RS[0:TQ].unsqueeze(2).to_broadcast([TQ, NT, E]), ALU.is_equal))
                    if k + 1 < top:
                        link(nc.vector.scalar_tensor_tensor(out=L[0:TQ], in0=OH[k][0:TQ], scalar=-3.0e38, in1=L[0:TQ],
                                                            op0=ALU.mult, op1=ALU.add))
                    if k:
                        src = OH[0] if k == 1 else M
                        ins = nc.vector.tensor_tensor(M[0:TQ], src[0:TQ], OH[k][0:TQ], ALU.add)
                        if k == top - 1:
                            ins.then_inc(sem(f"mask_ready{l}"), 1)
                            dve.wait_ge(sem(f"mask_ready{l}"), 1)
                        else:
                            link(ins)
                link(nc.vector.tensor_copy(RS[0:TQ], GATE[0:TQ, 0, :]))
                nc.vector.tensor_tensor(GATE[0:TQ, 0:top], GATE[0:TQ, 0:top], RS[0:TQ].unsqueeze(1).to_broadcast([TQ, top, NT]),
                                        ALU.subtract).then_inc(sem(f"top_ready{l}"), 1)
                dve.wait_ge(sem(f"gate_exp{l}"), 1)
                link(nc.vector.tensor_reduce(RS[0:TQ], GATE[0:TQ, 0:top].rearrange("p k t -> p t k"), axis=AX.X, op=ALU.add))
                link(nc.vector.reciprocal(RS[0:TQ], RS[0:TQ]))
                link(nc.vector.tensor_scalar(RS[0:TQ], RS[0:TQ], TG[0:TQ, 2 + l:3 + l], None, ALU.mult))
                link(nc.vector.tensor_tensor(GATE[0:TQ, 0:top], GATE[0:TQ, 0:top], RS[0:TQ].unsqueeze(1).to_broadcast([TQ, top, NT]), ALU.mult))
                dve.wait_ge(sem(f"rank_done{l}"), 1)
                link(nc.vector.tensor_copy(C, PS[:, 1, 0:NE]))
                src, dst = C, A
                s = 1
                while s < NT:
                    link(nc.vector.tensor_tensor(dst[:, s * E:NE], src[:, s * E:NE], src[:, 0:NE - s * E], ALU.add))
                    link(nc.vector.tensor_copy(dst[:, 0:s * E], src[:, 0:s * E]))
                    src, dst = dst, (B if dst is A else A)
                    s *= 2
                cnt = src[:, NE - E:NE]
                link(nc.vector.tensor_tensor(POS, src, C, ALU.subtract))
                link(nc.vector.tensor_tensor(POS[0:TQ], POS[0:TQ], PS[0:TQ, 0, 0:NE], ALU.add))
                big = wk(11 * 256, 1040)
                cmp = big[:, 0:E * CNT].rearrange("p (e c) -> p e c", c=CNT)
                link(nc.vector.tensor_tensor(cmp, cnt.unsqueeze(2).to_broadcast([P, E, CNT]),
                                             CST[:, C_THR:C_THR + CNT].unsqueeze(1).to_broadcast([P, E, CNT]), ALU.is_gt))
                NBK, S1, S2 = (SC[:, o * E:(o + 1) * E] for o in range(3))
                link(nc.vector.tensor_reduce(NBK, cmp, axis=AX.X, op=ALU.add))
                src, dst, s = NBK, S1, 1
                while s < E:
                    link(nc.vector.tensor_tensor(dst[:, s:E], src[:, s:E], src[:, 0:E - s], ALU.add))
                    link(nc.vector.tensor_copy(dst[:, 0:s], src[:, 0:s]))
                    src, dst = dst, (S2 if dst is S1 else S1)
                    s *= 2
                link(nc.vector.tensor_tensor(dst, src, NBK, ALU.subtract))
                link(nc.vector.tensor_scalar(dst, dst, float(P), None, ALU.mult))
                link(nc.vector.tensor_tensor(v3(POS), v3(POS), dst[0:TQ].unsqueeze(1).to_broadcast([TQ, NT, E]), ALU.add))
                NP = top * NT
                slot, blk, pos = (wk(3872 + o * 64, NP)[0:TQ] for o in range(3))
                for k in range(top):
                    link(nc.vector.tensor_tensor(OH[k][0:TQ], OH[k][0:TQ], POS[0:TQ], ALU.mult))
                    link(nc.vector.tensor_reduce(slot[:, k * NT:(k + 1) * NT], v3(OH[k]), axis=AX.X, op=ALU.add))
                def block_experts():
                    be = big[:, 0:nb * E].rearrange("p (i e) -> p i e", e=E)
                    link(nc.vector.tensor_tensor(be, src.unsqueeze(1).to_broadcast([P, nb, E]),
                                                 CST[:, C_IOTA:C_IOTA + nb].unsqueeze(2).to_broadcast([P, nb, E]), ALU.is_le))
                    ebf = M[:, 0:nb]
                    link(nc.vector.tensor_reduce(ebf, be, axis=AX.X, op=ALU.add))
                    link(nc.vector.tensor_scalar(ebf, ebf, float(E - 1), None, ALU.min))
                    link(nc.vector.tensor_scalar(OHB[:, 0:nb], ebf, CST[:, C_PE:C_PE + 1], None, ALU.is_equal))
                    link(nc.vector.tensor_scalar(EBI[:, 0:nb], ebf, float(stride), None, ALU.mult))
                    nc.vector.tensor_copy(L[0:TQ, 0:1], RS[0:TQ, 0:1]).then_inc(sem(f"slots_ready{l}"), 1)

                if l == 0:
                    block_experts()

                link(nc.vector.tensor_scalar(blk, slot, 1.0 / P, 0.5 / P - 0.5, ALU.mult, ALU.add))
                link(nc.vector.tensor_scalar(blk, blk, ROUND, None, ALU.add))
                link(nc.vector.tensor_scalar(blk, blk, -ROUND, None, ALU.add))
                link(nc.vector.scalar_tensor_tensor(out=pos, in0=blk, scalar=-float(P), in1=slot, op0=ALU.mult, op1=ALU.add))
                if l:
                    dve.wait_ge(sem("tokens_out1"), 16 * NQ)
                pr, pb, eq = pair_codes(l, top, nb)
                nc.vector.tensor_tensor(eq[0:TQ], blk.unsqueeze(2).to_broadcast([TQ, NP, nb]),
                                        CST[0:TQ, C_IOTA:C_IOTA + nb].unsqueeze(1).to_broadcast([TQ, NP, nb]),
                                        ALU.is_equal).then_inc(sem(f"block_code{l}"), 1)
                dve.wait_ge(sem(f"block_code{l}"), 1)
                for k in range(top):
                    g = slice(k * NT, (k + 1) * NT)
                    nc.vector.tensor_tensor(pr[0:TQ, g, :], pos[:, g].unsqueeze(2).to_broadcast([TQ, NT, P]),
                                            CST[0:TQ, C_IOTA:C_IOTA + P].unsqueeze(1).to_broadcast([TQ, NT, P]),
                                            ALU.is_equal).then_inc(sem(f"row_code{l}"), 1)
                if l:
                    block_experts()
                dve.wait_ge(sem(f"tokens_found{l}"), 1)
                u, p1, t, spare = (wk(3072 + o * P, nb) for o in range(4))
                link(nc.vector.tensor_copy(p1, PS[:, 5, 0:nb]))
                link(nc.vector.tensor_copy(u, PS[:, 5, nb:2 * nb]))
                link(nc.vector.tensor_scalar(t, u, 1.0 / top, 0.5 / top - 0.5, ALU.mult, ALU.add))
                link(nc.vector.tensor_scalar(t, t, ROUND, None, ALU.add))
                link(nc.vector.tensor_scalar(t, t, -ROUND, None, ALU.add))
                link(nc.vector.scalar_tensor_tensor(out=t, in0=t, scalar=float(TQ), in1=p1, op0=ALU.mult, op1=ALU.add))
                link(nc.vector.tensor_scalar(t, t, -1.0, 0.0, ALU.add, ALU.max))
                nc.vector.tensor_copy(TOK[:, 0:nb], t).then_inc(sem(f"rows_known{l}"), 1)
                link(nc.vector.tensor_scalar(spare, CST[:, C_IOTA:C_IOTA + nb], float(P), CST[:, C_PART:C_PART + 1],
                                             ALU.mult, ALU.add))
                link(nc.vector.tensor_scalar(spare, spare, float(NTOK * top), None, ALU.add))
                link(nc.vector.scalar_tensor_tensor(out=u, in0=u, scalar=float(TQ), in1=p1, op0=ALU.mult, op1=ALU.add))
                link(nc.vector.tensor_scalar(p1, p1, 0.0, None, ALU.is_equal))
                link(nc.vector.tensor_tensor(spare, spare, p1, ALU.mult))
                link(nc.vector.tensor_tensor(u, u, spare, ALU.add))
                link(nc.vector.tensor_scalar(u, u, -1.0, None, ALU.add))
                nc.vector.tensor_copy(PAIR[:, 0:nb], u).then_inc(sem(f"rows_known{l}"), 1)

            route(0, TOP0, E0, NB0, W0, PS[:, 6, 0:NT * E0])

            def onehot(l, i, slot, done):
                if done is not None:
                    dve.wait_ge(sem(f"y_done{l}"), done)
                nc.vector.tensor_copy(OHX[0:96, slot, :], OHB[0:96, bass.ds(i, 1)].to_broadcast([96, P])).then_inc(
                    sem(f"oh_ready{l}"), 1)

            def blocks0(i, par, more):
                dve.wait_ge(sem("ab_done0"), i + 1)
                dve.wait_ge(sem("a_copied"), i + 1)
                nc.vector.tensor_tensor(wk(1536, 512), wk(1024, 512), PS[:, 1, :], ALU.mult).then_inc(sem("z_ready"), 1)
                if more:
                    onehot(0, i + 1, 1 - par, i)

            onehot(0, 0, 0, None)
            onehot(0, 1, 1, None)
            blocks0(0, 0, False)
            R = (NB0 - 2) // 2
            with dve.Fori(0, R) as r:
                for h in range(2):
                    blocks0(2 * r + h + 1, 1 - h, True)
            for i in range(2 * R + 1, NB0):
                blocks0(i, i % 2, i + 1 < NB0)

            def combine(l, top):
                n = 0
                for t0 in range(0, NT, 2):
                    for k in range(top):
                        for t in (t0, t0 + 1):
                            if k == 0:
                                j, w = (t // 2, 3) if l else (t % 8, t // 8 + 1)
                                dve.wait_ge(sem(f"y_back_{j}"), 16 * w)
                            else:
                                dve.wait_ge(sem(f"y_used{l}"), n - 1)
                            nc.vector.scalar_tensor_tensor(out=X[0:TQ, t, :], in0=results(l, t)[0:TQ, k, :],
                                                           scalar=GATE[0:TQ, k, t:t + 1], in1=X[0:TQ, t, :],
                                                           op0=ALU.mult, op1=ALU.add).then_inc(sem(f"y_used{l}"), 1)
                            n += 1
                    if l == 0:
                        dve.wait_ge(sem("y_used0"), n)
                        stats(t0, X)
                        stats(t0 + 1, X)
                        if t0 % QUAD == QUAD - 2:
                            norm_between(t0 // QUAD)

            def norm_between(q):
                dve.wait_ge(sem("bn_done"), 4 * NT + QUAD * (q + 1))
                variance(q * QUAD, QUAD)
                if q == 0:
                    dve.wait_ge(sem("in_w4b"), 16 * 6)
                    link(nc.vector.tensor_scalar(ONE3[0:96], CST[0:96, C_PE:C_PE + 1].to_broadcast([96, P]), 0.0, None,
                                                 ALU.is_equal))
                    three_parts(BVO[0:96], ar(A_BC, 2 * D)[0:96])
                    link(nc.vector.tensor_scalar(NEG, IDN, -1.0, None, ALU.mult))
                    nc.vector.memset(TMP[:, 0, 0:1], 0.0).then_inc(sem("wo_added1"), 1)
                if q:
                    dve.wait_ge(sem("ln_rstd"), 10 + q)
                    apply(q - 1, X)

            combine(0, TOP0)
            dve.wait_ge(sem("ln_rstd"), 10 + NQ)
            apply(NQ - 1, X)

            ch1 = Chain(dve, sem("attn_chain1"))

            def head_sum(b, c):
                kn = KCH[c][1]
                dve.wait_ge(sem("exp_done1"), 3 * b + c + 1)
                e = EH[c][0:kn].rearrange("p a (h t) -> p t (a h)", h=QUAD)
                nc.vector.tensor_reduce(SMH[0:kn, c, :], e, axis=AX.X, op=ALU.add).then_inc(sem("hsum_done1"), 1)
                dve.wait_ge(sem("hsum_done1"), 3 * b + c + 1)
                nc.vector.reciprocal(SMH[0:kn, c, :], SMH[0:kn, c, :]).then_inc(sem("rcp_done1"), 1)

            def wo_add1(b, par):
                dve.wait_ge(sem("wo_done1"), b + 1)
                x = X[0:TQ, b, :]
                nc.vector.scalar_tensor_tensor(out=x, in0=PS[0:TQ, 7, 0:D], scalar=TG[0:TQ, 1:2], in1=x,
                                               op0=ALU.mult, op1=ALU.add).then_inc(sem("wo_added1"), 1)
                dve.wait_ge(sem("wo_added1"), b + 2)
                stats(b, X)

            def attn1(b, par, first, last):
                for c, (k0, kn) in enumerate(KCH):
                    n = 3 * b + c
                    dve.wait_ge(sem("s_done1"), n + 1)
                    s4 = PS[0:kn, 0:4, 0:N4].rearrange("p a (h t) -> p a h t", h=QUAD)
                    nc.vector.tensor_reduce(MXH[0:kn], s4.rearrange("p a h t -> p t a h"), axis=AX.XY,
                                            op=ALU.max).then_inc(sem("hmax_done1"), 1)
                    dve.wait_ge(sem("hmax_done1"), n + 1)
                    if not first:
                        dve.wait_ge(sem("pv_done1"), 3 * (b - 1) + c + 1)
                    for bk in range(3):
                        ins = nc.vector.tensor_tensor(EH[c][0:kn, bk, :].rearrange("p (h t) -> p h t", h=QUAD), s4[:, bk],
                                                      MXH[0:kn].unsqueeze(1).to_broadcast([kn, QUAD, TQ]), ALU.subtract)
                        ins.then_inc(sem("sub_done1"), 1)
                    if c or not first:
                        head_sum(*((b, c - 1) if c else (b - 1, 2)))
                    if c == 2 and not first:
                        wo_add1(b - 1, 1 - par)

            attn1(0, 0, True, False)
            with dve.Fori(0, (NT - 2) // 2) as r:
                for h in range(2):
                    attn1(2 * r + h + 1, 1 - h, False, False)
            attn1(NT - 1, 1, False, True)
            head_sum(NT - 1, 2)
            wo_add1(NT - 1, 1)

            dve.wait_ge(sem("bn_done"), 6 * NT)
            variance(0, NT)
            dve.wait_ge(sem("ln_rstd"), 11 + NQ)
            var = MV[0:TQ, :, 1]
            link(nc.vector.tensor_tensor(var, var, RS[0:TQ], ALU.mult))
            link(nc.vector.tensor_tensor(var, var, RS[0:TQ], ALU.mult))
            nc.vector.tensor_scalar(var, var, EPS, None, ALU.add).then_inc(sem("ln_var"), 1)
            for q in range(NQ):
                for t in range(q * QUAD, (q + 1) * QUAD):
                    ins = nc.vector.tensor_scalar(U[0:TQ, t, :], X[0:TQ, t, :], MV[0:TQ, t, 0:1], RS[0:TQ, t:t + 1],
                                                  ALU.subtract, ALU.mult)
                ins.then_inc(sem("ln_out"), 1)
            dve.wait_ge(sem("ln_out"), 6 * NQ)
            dve.wait_ge(sem("ln_rstd"), 12 + NQ)
            dve.wait_ge(sem("in_nsc"), 16)
            for t in range(NT):
                nc.vector.scalar_tensor_tensor(out=XN[0:TQ, t, :], in0=U[0:TQ, t, :], scalar=MV[0:TQ, t, 1:2],
                                               in1=NSC[0:TQ], op0=ALU.mult, op1=ALU.mult).then_inc(sem("xn_out"), 1)
            link(nc.vector.scalar_tensor_tensor(out=X[0:TQ], in0=U[0:TQ], scalar=TG[0:TQ, 3:4], in1=X[0:TQ],
                                                op0=ALU.mult, op1=ALU.add))
            dve.wait_ge(sem("xn_out"), NT)
            route(1, TOP1, E1, NB1, W1, PS[:, 6, 0:NT * E1])
            for i in range(4):
                onehot(1, i, i, None)
            ch = Chain(dve, sem("blk_chain1"))

            def blocks1(i, par, slot, done, ch):
                dve.wait_ge(sem("ab_done1"), i + 1)
                nc.vector.tensor_scalar(wk(1024, D), PS[:, par, 0:D], 7.0, None, ALU.min).then_inc(sem("a_min"), 1)
                dve.wait_ge(sem("a_min"), i + 1)
                nc.vector.tensor_scalar(wk(1536, D), PS[:, par, D:2 * D], 7.0, -7.0, ALU.min, ALU.max).then_inc(
                    sem("b_clip"), 1)
                dve.wait_ge(sem("b_clip"), i + 1)
                ch(nc.vector.scalar_tensor_tensor(out=wk(1792, D), in0=wk(1536, D), scalar=1.0, in1=wk(1024, D),
                                                  op0=ALU.add, op1=ALU.mult))
                dve.wait_ge(sem("sig_ready"), i + 1)
                nc.vector.tensor_tensor(wk(2560 + par * D, D), wk(1792, D), wk(1280, D), ALU.mult).then_inc(sem("s_ready1"), 1)
                if slot is not None:
                    onehot(1, i + 2, slot, done)

            blocks1(0, 0, None, None, ch)
            blocks1(1, 1, None, None, ch)
            R = (NB1 - 4) // 4
            with dve.Fori(0, R) as r:
                ch.begin(4 * r + 2)
                for h in range(4):
                    i = 4 * r + h + 2
                    blocks1(i, h % 2, h, i - 1, ch)
            ch.begin(4 * R + 2)
            for i in range(4 * R + 2, NB1):
                blocks1(i, i % 2, (i + 2) % 4 if i + 2 < NB1 else None, i - 1, ch)
            combine(1, TOP1)

        @block.tensor
        def _(pe):
            mm = nc.tensor.matmul
            pe.wait_ge(sem("in_const"), 16)

            def transposes(n, src, ready, per_quad, quads=range(NQ), b0=0, banks=4):
                for g in quads:
                    pe.wait_ge(sem(ready), per_quad(g))
                    for c in range(KD):
                        i = KD * g + c
                        if i >= banks:
                            pe.wait_ge(sem("tr_evac"), 2 * NQ * n + i - banks + 1)
                        for j in range(QUAD):
                            ins = nc.tensor.transpose(PS[:, b0 + i % banks, j * TQ:(j + 1) * TQ],
                                                      src[0:TQ, g * QUAD + j, c * P:(c + 1) * P], IDN[0:TQ, 0:TQ])
                        ins.then_inc(sem("tr_done"), 1)

            def q_proj(l, n, g):
                pe.wait_ge(sem("tr_evac"), 2 * NQ * n + 2 * (g + 1))
                for m in range(KD):
                    i = KD * g + m
                    if i >= 4:
                        pe.wait_ge(sem(f"q_evac{l}"), i - 3)
                    for k in range(KD):
                        ins = mm(PS[:, 4 + i % 4, 0:N4], WQ[:, k, m * P:(m + 1) * P], UT[:, k, g * N4:(g + 1) * N4],
                                 start=(k == 0), stop=(k == KD - 1))
                    ins.then_inc(sem(f"q_done{l}"), 1)

            def k_proj(l, par, m, bank=None):
                for k in range(KD):
                    ins = mm(PS[:, bank or (7 if l == 0 else 6 + m), 0:NK], WK[:, k, m * P:(m + 1) * P], CT[par][:, k, :],
                             start=(k == 0), stop=(k == KD - 1))
                ins.then_inc(sem(f"k_done{l}"), 1)

            def v_proj(l, par, c, bank=None):
                k0, kn = KCH[c]
                ps = PS[0:kn, bank or (7 if l == 0 else 6 + c % 2), 0:D]
                if l:
                    mm(ps, ONE3[0:96, 0:kn], BVO[0:96, 0:D], start=True, stop=False)
                for k in range(KD):
                    ins = mm(ps, CT[par][:, k, k0:k0 + kn], WV[:, k, :], start=(k == 0 and l == 0), stop=(k == KD - 1))
                ins.then_inc(sem(f"v_done{l}"), 1)

            def wo_proj(l, b, par):
                pe.wait_ge(sem(f"o_evac{l}"), b + 1)
                if l:
                    mm(PS[0:TQ, 7, 0:D], ONE3[0:96, 0:TQ], BVO[0:96, D:2 * D], start=True, stop=False)
                for k in range(KD):
                    ins = mm(PS[0:TQ, 7, 0:D], ATV[par][:, k, :], WO[:, k, :], start=(k == 0 and l == 0),
                             stop=(k == KD - 1))
                ins.then_inc(sem(f"wo_done{l}"), 1)

            def attn_start(l, n, ready):
                for m in range(KD):
                    k_proj(l, 0, m, 4 + m)
                if l:
                    pe.wait_ge(sem("wo_added1"), 1)
                for c in range(2):
                    v_proj(l, 0, c, 6 + c)
                pe.wait_ge(sem(f"k_evac{l}"), 1)
                v_proj(l, 0, 2, 4)
                for g in range(NQ):
                    transposes(n, U, "ln_out", ready, [g])
                    if g == 0:
                        pe.wait_ge(sem(f"k_evac{l}"), 2)
                        pe.wait_ge(sem(f"v_evac{l}"), 3)
                    q_proj(l, n, g)
                pe.wait_ge(sem(f"q_evac{l}"), 2 * NQ)

            pe.wait_ge(sem("in_w4"), 16 * 4)
            pe.wait_ge(sem("in_ct0"), 16)
            attn_start(0, 0, lambda g: g + 1)

            def scores0(b, par, g, first):
                n = 8 * b + g
                if g == 0:
                    pe.wait_ge(sem("qb_done0"), 2 * (b + 1))
                    pe.wait_ge(sem("k_evac0"), 2 * (b + 1))
                if not (first and g < 2):
                    pe.wait_ge(sem("exp_done"), n - 1)
                for j in range(2):
                    h = 2 * g + j
                    ins = mm(PS[0:TQ, 2 * (g % 2) + j, 0:NK], QB[par][:, h // 8, h % 8, :], KT[par][:, h // 8, :],
                             start=True, stop=True)
                ins.then_inc(sem("s_done0"), 1)

            def p_transpose(b, g, first):
                n = 8 * b + g
                pe.wait_ge(sem("p_done"), n + 1)
                pe.wait_ge(sem("pt_evac"), n)
                for j in range(2):
                    for c in range(3):
                        ins = nc.tensor.transpose(PS[0:KMAX, 4 + j, c * TQ:(c + 1) * TQ],
                                                  PB[g % 4][0:TQ, j, c * KMAX:(c + 1) * KMAX], IDN[0:TQ, 0:TQ])
                ins.then_inc(sem("t_done"), 1)

            def values0(b, par, g):
                n = 8 * b + g
                pe.wait_ge(sem("pt_evac"), n + 1)
                if g == 0:
                    pe.wait_ge(sem("v_evac0"), 3 * (b + 1))
                    pe.wait_ge(sem("o_evac0"), b)
                q, c8 = g % 4, g // 4
                for j in range(2):
                    for c, (k0, kn) in enumerate(KCH):
                        ins = mm(PS[32 * q:32 * q + 32, 6, c8 * TQ:(c8 + 1) * TQ], VP[par][0:kn, c, j, 32 * g:32 * g + 32],
                                 PT[g % 2][0:kn, j, c * TQ:(c + 1) * TQ], start=(j == 0 and c == 0), stop=(j == 1 and c == 2))
                ins.then_inc(sem("pv_done0"), 1)

            def proj_piece0(b, par, i, first):
                if i == 0:
                    if first:
                        pe.wait_ge(sem("v_evac0"), 3)
                    else:
                        pe.wait_ge(sem("wo_evac0"), b - 1)
                    k_proj(0, par, 0)
                elif i == 1:
                    pe.wait_ge(sem("k_evac0"), 2 * b + 1)
                    k_proj(0, par, 1)
                else:
                    pe.wait_ge(sem("k_evac0"), 2 * b + 2)
                    pe.wait_ge(sem("v_evac0"), 3 * b + i - 2)
                    v_proj(0, par, i - 2)

            def attn0(b, par, first, last, ctw):
                for g in range(8):
                    scores0(b, par, g, first)
                    if g >= 2:
                        p_transpose(b, g - 2, first)
                    elif not first:
                        p_transpose(b - 1, 6 + g, first)
                    if g == 0 and not first:
                        proj_piece0(b, par, 4, None)
                    if g == 3 and not first:
                        pe.wait_ge(sem("v_evac0"), 3 * (b + 1))
                        wo_proj(0, b - 1, 1 - par)
                    if g >= 4 and not last:
                        if g == 4:
                            pe.wait_ge(sem(f"in_ct{1 - par}"), ctw)
                        proj_piece0(b + 1, 1 - par, g - 4, first)
                    if g >= 3:
                        values0(b, par, g - 3)
                    elif not first:
                        values0(b - 1, 1 - par, 5 + g)

            attn0(0, 0, True, False, 16)
            with pe.Fori(0, (NT - 2) // 2) as r:
                for h in range(2):
                    attn0(2 * r + h + 1, 1 - h, False, False, 16 * (r + 2))
            attn0(NT - 1, 1, False, True, None)
            p_transpose(NT - 1, 6, False)
            values0(NT - 1, 1, 5)
            p_transpose(NT - 1, 7, False)
            values0(NT - 1, 1, 6)
            values0(NT - 1, 1, 7)
            pe.wait_ge(sem("wo_evac0"), NT - 1)
            wo_proj(0, NT - 1, 1)

            pe.wait_ge(sem("in_ffw"), 32)
            for q in range(NQ):
                transposes(1, U, "ln_out", lambda g: NQ + g + 1, [q], 6, 2)
                pe.wait_ge(sem("tr_evac"), 2 * NQ + 2 * (q + 1))
                for f in range(FD):
                    if FD * q + f > 3:
                        pe.wait_ge(sem("h_evac"), FD * q + f - 3)
                    for k in range(KD):
                        ins = mm(PS[:, f % 4, 0:N4], W1S[:, k, f * P:(f + 1) * P], UT[:, k, q * N4:(q + 1) * N4],
                                 start=(k == 0), stop=(k == KD - 1))
                    ins.then_inc(sem("h_done"), 1)
                pe.wait_ge(sem("h_evac"), FD * q + FD)
                for j in range(QUAD):
                    t = QUAD * q + j
                    if t > 1:
                        pe.wait_ge(sem("f_evac"), t - 1)
                    for f in range(FD):
                        ins = mm(PS[0:TQ, 4 + t % 2, 0:D], HT[:, f, j * TQ:(j + 1) * TQ], W2S[:, f, :],
                                 start=(f == 0), stop=(f == FD - 1))
                    ins.then_inc(sem("f_done"), 1)

            def router(l, n, E, src, ready, per_quad, lag):
                c0 = 0 if l == 0 else E0
                pe.wait_ge(sem("in_gw"), 16 * 4)
                for g in range(NQ + lag):
                    if g < NQ:
                        transposes(n, src, ready, per_quad, [g])
                    if g < lag:
                        continue
                    pe.wait_ge(sem("tr_evac"), 2 * NQ * n + 2 * (g - lag + 1))
                    for t in range((g - lag) * QUAD, (g - lag + 1) * QUAD):
                        for k in range(KD):
                            ins = mm(PS[0:TQ, 6, t * E:(t + 1) * E], UT[:, k, t * TQ:(t + 1) * TQ],
                                     GW[:, k, c0:c0 + E], start=(k == 0), stop=(k == KD - 1))
                ins.then_inc(sem(f"logit_done{l}"), 1)
                pe.wait_ge(sem(f"mask_ready{l}"), 1)
                M = wk(2 * 256, NT * E)
                mm(PS[0:TQ, 0, 0:NT * E], CST[0:TQ, C_TRI:C_TRI + TQ], M[0:TQ], start=True, stop=True)
                mm(PS[:, 1, 0:NT * E], CST[0:TQ, C_ONE:C_ONE + P], M[0:TQ], start=True, stop=True).then_inc(
                    sem(f"rank_done{l}"), 1)

            def find_tokens(l, top, nb):
                pr, pb, _ = pair_codes(l, top, nb)
                pe.wait_ge(sem(f"part_code{l}"), 1)
                for n in range(top * NT):
                    if n % NT == 0:
                        pe.wait_ge(sem(f"row_code{l}"), n // NT + 1)
                        pe.wait_ge(sem(f"tile_code{l}"), n // NT + 1)
                    ins = mm(PS[:, 5, 0:2 * nb], pr[0:TQ, n, :], pb[0:TQ, n].rearrange("p c b -> p (c b)"),
                             start=(n == 0), stop=(n == top * NT - 1))
                ins.then_inc(sem(f"tokens_found{l}"), 1)

            router(0, 2, E0, U, "ln_out", lambda g: 2 * NQ + 2 * (g + 1), 0)
            find_tokens(0, TOP0, NB0)

            def x_transpose(l, i, par, w):
                pe.wait_ge(sem(f"in_blk{l}_{par}"), w)
                for c in range(KD):
                    ins = nc.tensor.transpose(PS[:, 4, c * P:(c + 1) * P], wk(par * D + c * P, P), IDN)
                ins.then_inc(sem(f"xt_done{l}"), 1)

            def row(o, n):
                return AR[:, bass.ds(o, n)]

            def expert_of(i, E, stride):
                return pe.value_load(EBI[0:1, bass.ds(i, 1)], min_val=0, max_val=(E - 1) * stride)

            def y_proj(l, off, nk, o3, br, brc, par):
                mm(PS[:, 3, 0:D], OHX[0:96, par, :], br[0:96, brc:brc + D], start=True, stop=False)
                for k in range(nk):
                    ins = mm(PS[:, 3, 0:D], wk(3072 + k * P, P), row(off + o3 + k * D, D), start=False, stop=(k == nk - 1))
                ins.then_inc(sem(f"y_done{l}"), 1)

            def ab0(i, par, first):
                off = expert_of(i, E0, W0)
                pe.wait_ge(sem("xt_evac0"), i + 1)
                pe.wait_ge(sem("oh_ready0"), i + 1)
                if not first:
                    pe.wait_ge(sem("z_ready"), i)
                for m in range(2):
                    mm(PS[:, m, :], OHX[0:96, par, :], BR0[0:96, m * F0:(m + 1) * F0], start=True, stop=False)
                    for k in range(KD):
                        ins = mm(PS[:, m, :], wk(512 + par * D + k * P, P), row(off + m * 1024 + k * F0, F0),
                                 start=False, stop=(k == KD - 1))
                    ins.then_inc(sem("a_done" if m == 0 else "ab_done0"), 1)

            def t4(src, bank, name, waits):
                for s_, v in waits:
                    pe.wait_ge(sem(s_), v)
                for k in range(4):
                    ins = nc.tensor.transpose(PS[:, bank, k * P:(k + 1) * P], wk(src + k * P, P), IDN)
                ins.then_inc(sem(name), 1)

            def blocks0(i, par, first, last, w):
                ab0(i, par, first)
                if not first:
                    t4(2560, 6, "st_done", [("s_ready", i)])
                if not last:
                    x_transpose(0, i + 1, 1 - par, w)
                t4(1536, 5, "zt_done", [("z_ready", i + 1)])
                if not first:
                    off = expert_of(i - 1, E0, W0)
                    pe.wait_ge(sem("st_evac"), i)
                    y_proj(0, off, 4, 4096, BR0, 3 * F0, 1 - par)
                off = expert_of(i, E0, W0)
                pe.wait_ge(sem("zt_evac"), i + 1)
                if not first:
                    pe.wait_ge(sem("s_ready"), i)
                mm(PS[:, 2, :], OHX[0:96, par, :], BR0[0:96, 2 * F0:3 * F0], start=True, stop=False)
                for k in range(4):
                    ins = mm(PS[:, 2, :], wk(2048 + k * P, P), row(off + 2048 + k * F0, F0), start=False, stop=(k == 3))
                ins.then_inc(sem("g_done"), 1)

            pe.wait_ge(sem("slots_ready0"), 1)
            pe.wait_ge(sem("in_e0"), 16 * 4 * E0)
            x_transpose(0, 0, 0, 16)
            blocks0(0, 0, True, False, 16)
            R = (NB0 - 2) // 2
            with pe.Fori(0, R) as r:
                for h in range(2):
                    blocks0(2 * r + h + 1, 1 - h, False, False, 16 * (r + 2))
            for i in range(2 * R + 1, NB0):
                blocks0(i, i % 2, False, i == NB0 - 1, 16 * ((i + 1) // 2 + 1))
            t4(2560, 6, "st_done", [("s_ready", NB0)])
            off = expert_of(NB0 - 1, E0, W0)
            pe.wait_ge(sem("st_evac"), NB0)
            pe.wait_ge(sem("y_ready0"), NB0 - 1)
            y_proj(0, off, 4, 4096, BR0, 3 * F0, (NB0 - 1) % 2)

            pe.wait_ge(sem("in_w4b"), 16 * 6)
            pe.wait_ge(sem("in_ct0b"), 16)
            attn_start(1, 3, lambda g: 4 * NQ + g + 1)

            def scores1(b, par, c, first):
                k0, kn = KCH[c]
                n = 3 * b + c
                if c == 0:
                    pe.wait_ge(sem("qb_done1"), 2 * (b + 1))
                    pe.wait_ge(sem("k_evac1"), 2 * (b + 1))
                for bk in range(4):
                    if c or not first:
                        if bk < 3:
                            pe.wait_ge(sem("sub_done1"), 3 * n - 2 + bk)
                        else:
                            pe.wait_ge(sem("bank3_exp1"), n)
                    q = QB[par][:, bk // 2, (bk % 2) * 4:(bk % 2) * 4 + 4, :].rearrange("p h t -> p (h t)")
                    ins = mm(PS[0:kn, bk, 0:N4], KT[par][:, bk // 2, k0:k0 + kn], q, start=True, stop=True)
                ins.then_inc(sem("s_done1"), 1)

            def minus_max1(b, c):
                kn = KCH[c][1]
                pe.wait_ge(sem("hmax_done1"), 3 * b + c + 1)
                mm(PS[0:kn, 3, 0:N4].rearrange("p (h t) -> p h t", h=QUAD), NEG[0:kn, 0:kn],
                   MXH[0:kn].unsqueeze(1).to_broadcast([kn, QUAD, TQ]), start=False, stop=True,
                   skip_group_check=True).then_inc(sem("neg_done1"), 1)

            def values1(b, par, c):
                k0, kn = KCH[c]
                pe.wait_ge(sem("p_done1"), 3 * b + c + 1)
                if c == 0:
                    pe.wait_ge(sem("v_evac1"), 3 * (b + 1))
                for g in range(8):
                    q, c8 = g % 4, g // 4
                    for j in range(2):
                        h = 2 * g + j
                        ins = mm(PS[32 * q:32 * q + 32, 4 + c8, 0:TQ], VP[par][0:kn, c, j, 32 * g:32 * g + 32],
                                 EH[c][0:kn, h // 4, (h % 4) * TQ:(h % 4 + 1) * TQ],
                                 start=(c == 0 and j == 0), stop=(c == 2 and j == 1), skip_group_check=True)
                ins.then_inc(sem("pv_done1"), 1)

            def attn1(b, par, first, last, ctw):
                for c in range(3):
                    scores1(b, par, c, first)
                    if not first:
                        values1(b - 1, 1 - par, c)
                    if c == 0 and not last:
                        pe.wait_ge(sem(f"in_ct{1 - par}b"), ctw)
                        pe.wait_ge(sem("v_evac1"), 3 * (b + 1))
                        k_proj(1, 1 - par, 0)
                        if not first:
                            pe.wait_ge(sem("wo_added1"), b)
                        k_proj(1, 1 - par, 1)
                    if c == 1 and not last:
                        pe.wait_ge(sem("k_evac1"), 2 * (b + 2))
                        v_proj(1, 1 - par, 0)
                        v_proj(1, 1 - par, 1)
                    if c == 2 and not last:
                        pe.wait_ge(sem("v_evac1"), 3 * (b + 1) + 1)
                        v_proj(1, 1 - par, 2)
                    if c == 2 and not first:
                        pe.wait_ge(sem("v_evac1"), 3 * (b + 1) + (0 if last else 2))
                        wo_proj(1, b - 1, 1 - par)
                    minus_max1(b, c)

            attn1(0, 0, True, False, 16)
            with pe.Fori(0, (NT - 2) // 2) as r:
                for h in range(2):
                    attn1(2 * r + h + 1, 1 - h, False, False, 16 * (r + 2))
            attn1(NT - 1, 1, False, True, None)
            values1(NT - 1, 1, 0)
            values1(NT - 1, 1, 1)
            values1(NT - 1, 1, 2)
            pe.wait_ge(sem("wo_added1"), NT)
            wo_proj(1, NT - 1, 1)

            router(1, 4, E1, XN, "xn_out", lambda g: QUAD * (g + 1), 1)
            find_tokens(1, TOP1, NB1)

            def ab1(i, par, slot, first):
                off = expert_of(i, E1, W1)
                pe.wait_ge(sem("xt_evac1"), i + 1)
                pe.wait_ge(sem("oh_ready1"), i + 1)
                if not first:
                    pe.wait_ge(sem("b_clip"), i - 1)
                mm(PS[:, par, :], OHX[0:96, slot, :], BR1[0:96, 0:2 * F1], start=True, stop=False)
                for k in range(KD):
                    ins = mm(PS[:, par, :], wk(512 + par * D + k * P, P), row(off + k * 512, 512), start=False,
                             stop=(k == KD - 1))
                ins.then_inc(sem("ab_done1"), 1)

            def st1(i, par):
                pe.wait_ge(sem("s_ready1"), i + 1)
                for k in range(2):
                    ins = nc.tensor.transpose(PS[:, 6, k * P:(k + 1) * P], wk(2560 + par * D + k * P, P), IDN)
                ins.then_inc(sem("st_done1"), 1)

            def y1(i, slot):
                off = expert_of(i, E1, W1)
                pe.wait_ge(sem("st_evac1"), i + 1)
                y_proj(1, off, 2, 1024, BR1, 2 * F1, slot)

            pe.wait_ge(sem("slots_ready1"), 1)
            pe.wait_ge(sem("in_e1"), 16 * 2 * E1)
            x_transpose(1, 0, 0, 16)
            ab1(0, 0, 0, True)
            x_transpose(1, 1, 1, 16)
            ab1(1, 1, 1, True)
            x_transpose(1, 2, 0, 32)
            st1(0, 0)
            R = (NB1 - 4) // 4
            with pe.Fori(0, R) as r:
                for h in range(4):
                    i = 4 * r + h + 2
                    ab1(i, h % 2, (h + 2) % 4, False)
                    x_transpose(1, i + 1, (h + 1) % 2, 16 * (2 * r + (h + 3) // 2 + 1))
                    y1(i - 2, h)
                    st1(i - 1, (h + 1) % 2)
            for i in range(4 * R + 2, NB1):
                ab1(i, i % 2, i % 4, False)
                if i + 1 < NB1:
                    x_transpose(1, i + 1, (i + 1) % 2, 16 * ((i + 1) // 2 + 1))
                y1(i - 2, (i - 2) % 4)
                st1(i - 1, (i - 1) % 2)
            y1(NB1 - 2, (NB1 - 2) % 4)
            st1(NB1 - 1, (NB1 - 1) % 2)
            y1(NB1 - 1, (NB1 - 1) % 4)


def constants():
    import numpy as np
    c = np.zeros((P, C_N), np.float32)
    p = np.arange(P)
    c[:, C_ID:C_ID + P] = np.eye(P)
    c[:, C_TRI:C_TRI + P] = p[:, None] < p[None, :]
    c[:, C_ONE:C_ONE + P] = 1.0
    c[:, C_MASK:C_MASK + 8] = np.where(p[:, None] // HD == np.arange(8)[None, :], HD ** -0.5, 0.0)
    c[:, C_PE] = p % 32
    c[:, C_HALF] = -0.5
    c[:, C_THR:C_THR + CNT] = P * np.arange(CNT)
    c[:, C_PART] = p + 1
    c[:, C_IOTA:C_IOTA + P] = p
    c[:, C_REV0:C_REV0 + E0] = E0 - np.arange(E0)
    c[:, C_REV1:C_REV1 + E1] = E1 - np.arange(E1)
    return c


def kernel(**inputs):
    import numpy as np
    import concourse.bacc as bacc
    from concourse.bass_utils import run_bass_kernel_spmd as run

    g = {k: np.asarray(v) for k, v in inputs.items()}
    arrays = {"x": g["x"], "ctx_t": g["ctx_1024"].transpose(0, 2, 1), "consts": constants()}
    arrays["gates"] = np.concatenate([g["g_xattn"], g["g_ffn"]])

    def cols(v):
        return v.reshape(-1, P).T

    arrays["cols"] = np.concatenate([cols(g["L0_xattn_bq"]), cols(g["L0_xattn_bk"]), cols(g["L0_xattn_b1"]),
                                     cols(g["L1_xattn_Wq_b"]), cols(g["L1_xattn_Wk_b"])], axis=1)
    for n in ["wq", "wk", "wv", "wo", "w1", "w2", "bv", "bo", "g1", "be1", "b2", "g2", "be2"]:
        arrays["L0_xattn_" + n] = g["L0_xattn_" + n]
    for n in ["Wq_w", "Wk_w", "Wv_w", "Wo_w"]:
        arrays["L1_xattn_" + n] = g["L1_xattn_" + n].T
    for n in ["Wv_b", "Wo_b"]:
        arrays["L1_xattn_" + n] = g["L1_xattn_" + n]
    for n in ["gate_w", "gate_b", "w1", "w2", "wg", "w3", "b1", "b2", "bg", "b3"]:
        arrays["L0_ffn_" + n] = g["L0_ffn_" + n]
    for n in ["norm_scale", "wg", "bg", "w2", "b2"]:
        arrays["L1_ffn_" + n] = g["L1_ffn_" + n]
    arrays["L1_ffn_w1"] = g["L1_ffn_w1"].reshape(E1, D, F1, 2).transpose(0, 1, 3, 2).reshape(E1, D, 2 * F1)
    arrays["L1_ffn_b1"] = g["L1_ffn_b1"].reshape(E1, F1, 2).transpose(0, 2, 1).reshape(E1, 2 * F1)

    nc = bacc.Bacc("TRN2", target_bir_lowering=False, num_devices=1)
    feed, aps = {}, {}
    for n, v in arrays.items():
        v = np.ascontiguousarray(v)
        feed["in_" + n] = v
        aps[n] = nc.dram_tensor("in_" + n, v.shape, mybir.dt.from_np(v.dtype), kind="ExternalInput").ap()
    out = nc.dram_tensor("out_0", (NT, TQ, D), F32, kind="ExternalOutput").ap()
    build(nc, aps, out)
    r = run(nc, [feed], core_ids=[0])
    return r.results[0]["out_0"]
```
